# Optimizing a Trainium2 kernel written in Bass

```python
import numpy as np
import jax
import jax.numpy as jnp

def _softmax(x, axis=-1):
    return jax.nn.softmax(x, axis=axis)

def _gelu(x):
    return jax.nn.gelu(x, approximate=True)

def _silu(x):
    return jax.nn.silu(x)

def _sigmoid(x):
    return jax.nn.sigmoid(x)

def _layernorm(x, axis=-1, eps=1e-05):
    m = jnp.mean(x, axis=axis, keepdims=True)
    v = jnp.var(x, axis=axis, keepdims=True)
    return (x - m) / jnp.sqrt(v + eps)

def _scatter_add(tgt, idx, src, axis=0):
    return tgt.at[idx].add(src)

def _segment_sum(src, seg, n):
    return jax.ops.segment_sum(src, seg, n)
kernel_name = 'mk_early_fusion_d2_tok_img512_r4_bf597b'

def setup_inputs(seed: int=0):
    np.random.seed(seed)
    _w = jnp.asarray

    def _rec_inputs():
        import jax
        import jax.numpy as jnp
        _rk = jax.random.key(seed)
        x = -0.000121822 + 0.999869 * jax.random.normal(jax.random.fold_in(_rk, 1), (16, 3, 196, 196), jnp.float32)
        txt = 0.322801 + 1.18033 * jax.random.normal(jax.random.fold_in(_rk, 2), (16, 128, 128), jnp.float32)
        return (x, txt)
    x, txt = _rec_inputs()

    def _L0_tok_setup():
        import jax, jax.numpy as jnp
        import numpy as np
        B, C, H, N_P, HID = (64, 3, 196, 14, 128)
        P = H // N_P
        IN_DIM = C * P * P
        SEQ = N_P * N_P + 1

        def sinusoidal_position(length, d):
            pos = jnp.arange(length, dtype=jnp.float32)[:, None]
            i = jnp.arange(d)[None, :]
            angle = pos / jnp.power(10000.0, (2 * (i // 2)).astype(jnp.float32) / d)
            return jnp.where(i % 2 == 0, jnp.sin(angle), jnp.cos(angle)).astype(jnp.float32)
        key = jax.random.key(seed)
        k_img, k_w, k_b, k_tok = jax.random.split(key, 4)
        img = jax.random.normal(k_img, (B, C, H, H), dtype=jnp.float32)
        W = jax.random.normal(k_w, (HID, IN_DIM), dtype=jnp.float32) / np.sqrt(IN_DIM)
        b = jax.random.normal(k_b, (HID,), dtype=jnp.float32) * 0.01
        token = jax.random.uniform(k_tok, (1, HID), dtype=jnp.float32)
        pos = sinusoidal_position(SEQ, HID)
        return {'img': img, 'W': W, 'b': b, 'token': token, 'pos': pos}
    _L0_tok_all = _L0_tok_setup()
    _L0_tok_in = {k: v for k, v in _L0_tok_all.items() if k in ('W', 'b', 'token', 'pos')}
    del _L0_tok_all

    def _L0_attn_setup():
        import jax, jax.numpy as jnp
        import numpy as np
        B, S, E, H = (4, 256, 128, 16)
        key = jax.random.key(seed)
        ks = jax.random.split(key, 6)
        return {'x': jax.random.normal(ks[0], (B, S, E), dtype=jnp.float32), 'Wq': jax.random.normal(ks[1], (E, E), dtype=jnp.float32) * E ** (-0.5), 'Wk': jax.random.normal(ks[2], (E, E), dtype=jnp.float32) * E ** (-0.5), 'Wv': jax.random.normal(ks[3], (E, E), dtype=jnp.float32) * E ** (-0.5), 'W1': jax.random.normal(ks[4], (H, 2 * E), dtype=jnp.float32) * (2 * E) ** (-0.5), 'b1': jnp.zeros((H,), dtype=jnp.float32), 'W2': jax.random.normal(ks[5], (1, H), dtype=jnp.float32) * H ** (-0.5), 'b2': jnp.zeros((1,), dtype=jnp.float32)}
    _L0_attn_all = _L0_attn_setup()
    _L0_attn_in = {k: v for k, v in _L0_attn_all.items() if k in ('Wq', 'Wk', 'Wv', 'W1', 'b1', 'W2', 'b2')}
    del _L0_attn_all

    def _L0_ffn_setup():
        import jax, jax.numpy as jnp
        import numpy as np
        D_MODEL = 128
        D_FF = 512
        N_EXPERTS = 8
        TOP_K = 2
        key = jax.random.key(seed)
        ks = jax.random.split(key, 8)
        x = jax.random.normal(ks[0], (2, 512, D_MODEL), dtype=jnp.float32)
        router_w = jax.random.normal(ks[1], (D_MODEL, N_EXPERTS), dtype=jnp.float32) * 0.02
        router_b = jnp.zeros((N_EXPERTS,), dtype=jnp.float32)
        s1 = 1.0 / np.sqrt(D_MODEL)
        s2 = 1.0 / np.sqrt(D_FF)
        W1 = jax.random.uniform(ks[2], (N_EXPERTS, D_MODEL, D_FF), jnp.float32, -s1, s1)
        b1 = jax.random.uniform(ks[3], (N_EXPERTS, D_FF), jnp.float32, -s1, s1)
        W2 = jax.random.uniform(ks[4], (N_EXPERTS, D_FF, D_MODEL), jnp.float32, -s2, s2)
        b2 = jax.random.uniform(ks[5], (N_EXPERTS, D_MODEL), jnp.float32, -s2, s2)
        return {'x': x, 'router_w': router_w, 'router_b': router_b, 'W1': W1, 'b1': b1, 'W2': W2, 'b2': b2}
    _L0_ffn_all = _L0_ffn_setup()
    _L0_ffn_in = {k: v for k, v in _L0_ffn_all.items() if k in ('router_w', 'router_b', 'W1', 'b1', 'W2', 'b2')}
    del _L0_ffn_all

    def _L1_attn_setup():
        import jax, jax.numpy as jnp
        import numpy as np
        B, S, D, H = (4, 512, 128, 8)
        KD = D // H
        FFN = 4 * D

        def _ln(x, g, b, eps):
            mu = x.mean(-1, keepdims=True)
            var = ((x - mu) ** 2).mean(-1, keepdims=True)
            return (x - mu) / jnp.sqrt(var + eps) * g + b
        key = jax.random.key(seed)
        ks = jax.random.split(key, 8)

        def lin(k, o, i, scale=0.02):
            k1, k2 = jax.random.split(k)
            return (jax.random.normal(k1, (o, i), jnp.float32) * scale, jax.random.normal(k2, (o,), jnp.float32) * scale)
        wq, bq = lin(ks[0], D, D)
        wk, bk = lin(ks[1], D, D)
        wv, bv = lin(ks[2], D, D)
        wg, bg = lin(ks[3], D, D)
        wo, bo = lin(ks[4], D, D)
        fc1_w, fc1_b = lin(ks[5], FFN, D)
        fc2_w, fc2_b = lin(ks[6], D, FFN)
        return {'src': jax.random.normal(ks[7], (B, S, D), jnp.float32), 'mask': jnp.zeros((S, S), jnp.bool_), 'padding_mask': jnp.zeros((B, S), jnp.bool_), 'wq': wq, 'bq': bq, 'wk': wk, 'bk': bk, 'wv': wv, 'bv': bv, 'wg': wg, 'bg': bg, 'wo': wo, 'bo': bo, 'fc1_w': fc1_w, 'fc1_b': fc1_b, 'fc2_w': fc2_w, 'fc2_b': fc2_b, 'ln_ffn_g': jnp.ones((FFN,), jnp.float32), 'ln_ffn_b': jnp.zeros((FFN,), jnp.float32), 'n0_g': jnp.ones((D,), jnp.float32), 'n0_b': jnp.zeros((D,), jnp.float32), 'n1_g': jnp.ones((D,), jnp.float32), 'n1_b': jnp.zeros((D,), jnp.float32)}
    _L1_attn_all = _L1_attn_setup()
    _L1_attn_in = {k: v for k, v in _L1_attn_all.items() if k in ('mask', 'padding_mask', 'wq', 'bq', 'wk', 'bk', 'wv', 'bv', 'wg', 'bg', 'wo', 'bo', 'fc1_w', 'fc1_b', 'fc2_w', 'fc2_b', 'ln_ffn_g', 'ln_ffn_b', 'n0_g', 'n0_b', 'n1_g', 'n1_b')}
    del _L1_attn_all

    def _L1_ffn_setup():
        import jax, jax.numpy as jnp
        import numpy as np
        D_MODEL = 128
        D_FF = 128
        N_EXPERTS = 16
        TOP_K = 3
        BATCH, SEQ = (1, 512)

        def _swiglu(combined):
            gate, up = jnp.split(combined, 2, axis=-1)
            return jax.nn.silu(gate) * up
        key = jax.random.key(seed)
        ks = jax.random.split(key, 6)
        x = jax.random.normal(ks[0], (BATCH, SEQ, D_MODEL), dtype=jnp.float32)
        gate_w = 0.01 * jax.random.normal(ks[1], (N_EXPERTS, D_MODEL), dtype=jnp.float32)
        expert_bias = jnp.zeros((N_EXPERTS,), dtype=jnp.float32)
        shared_gate_up = 0.02 * jax.random.normal(ks[2], (2 * D_FF, D_MODEL), dtype=jnp.float32)
        shared_down = 0.02 * jax.random.normal(ks[3], (D_MODEL, D_FF), dtype=jnp.float32)
        expert_gate_up = 0.02 * jax.random.normal(ks[4], (N_EXPERTS, 2 * D_FF, D_MODEL), dtype=jnp.float32)
        expert_down = 0.02 * jax.random.normal(ks[5], (N_EXPERTS, D_MODEL, D_FF), dtype=jnp.float32)
        return {'x': x, 'gate_w': gate_w, 'expert_bias': expert_bias, 'shared_gate_up': shared_gate_up, 'shared_down': shared_down, 'expert_gate_up': expert_gate_up, 'expert_down': expert_down}
    _L1_ffn_all = _L1_ffn_setup()
    _L1_ffn_in = {k: v for k, v in _L1_ffn_all.items() if k in ('gate_w', 'expert_bias', 'shared_gate_up', 'shared_down', 'expert_gate_up', 'expert_down')}
    del _L1_ffn_all
    return {'x': x, 'txt': txt, 'L0_tok_W': _L0_tok_in['W'], 'L0_tok_b': _L0_tok_in['b'], 'L0_tok_token': _L0_tok_in['token'], 'L0_tok_pos': _L0_tok_in['pos'], 'L0_attn_Wq': _L0_attn_in['Wq'], 'L0_attn_Wk': _L0_attn_in['Wk'], 'L0_attn_Wv': _L0_attn_in['Wv'], 'L0_attn_W1': _L0_attn_in['W1'], 'L0_attn_b1': _L0_attn_in['b1'], 'L0_attn_W2': _L0_attn_in['W2'], 'L0_attn_b2': _L0_attn_in['b2'], 'L0_ffn_router_w': _L0_ffn_in['router_w'], 'L0_ffn_router_b': _L0_ffn_in['router_b'], 'L0_ffn_W1': _L0_ffn_in['W1'], 'L0_ffn_b1': _L0_ffn_in['b1'], 'L0_ffn_W2': _L0_ffn_in['W2'], 'L0_ffn_b2': _L0_ffn_in['b2'], 'L1_attn_mask': _L1_attn_in['mask'], 'L1_attn_padding_mask': _L1_attn_in['padding_mask'], 'L1_attn_wq': _L1_attn_in['wq'], 'L1_attn_bq': _L1_attn_in['bq'], 'L1_attn_wk': _L1_attn_in['wk'], 'L1_attn_bk': _L1_attn_in['bk'], 'L1_attn_wv': _L1_attn_in['wv'], 'L1_attn_bv': _L1_attn_in['bv'], 'L1_attn_wg': _L1_attn_in['wg'], 'L1_attn_bg': _L1_attn_in['bg'], 'L1_attn_wo': _L1_attn_in['wo'], 'L1_attn_bo': _L1_attn_in['bo'], 'L1_attn_fc1_w': _L1_attn_in['fc1_w'], 'L1_attn_fc1_b': _L1_attn_in['fc1_b'], 'L1_attn_fc2_w': _L1_attn_in['fc2_w'], 'L1_attn_fc2_b': _L1_attn_in['fc2_b'], 'L1_attn_ln_ffn_g': _L1_attn_in['ln_ffn_g'], 'L1_attn_ln_ffn_b': _L1_attn_in['ln_ffn_b'], 'L1_attn_n0_g': _L1_attn_in['n0_g'], 'L1_attn_n0_b': _L1_attn_in['n0_b'], 'L1_attn_n1_g': _L1_attn_in['n1_g'], 'L1_attn_n1_b': _L1_attn_in['n1_b'], 'L1_ffn_gate_w': _L1_ffn_in['gate_w'], 'L1_ffn_expert_bias': _L1_ffn_in['expert_bias'], 'L1_ffn_shared_gate_up': _L1_ffn_in['shared_gate_up'], 'L1_ffn_shared_down': _L1_ffn_in['shared_down'], 'L1_ffn_expert_gate_up': _L1_ffn_in['expert_gate_up'], 'L1_ffn_expert_down': _L1_ffn_in['expert_down']}

def reference(x, txt, L0_tok_W, L0_tok_b, L0_tok_token, L0_tok_pos, L0_attn_Wq, L0_attn_Wk, L0_attn_Wv, L0_attn_W1, L0_attn_b1, L0_attn_W2, L0_attn_b2, L0_ffn_router_w, L0_ffn_router_b, L0_ffn_W1, L0_ffn_b1, L0_ffn_W2, L0_ffn_b2, L1_attn_mask, L1_attn_padding_mask, L1_attn_wq, L1_attn_bq, L1_attn_wk, L1_attn_bk, L1_attn_wv, L1_attn_bv, L1_attn_wg, L1_attn_bg, L1_attn_wo, L1_attn_bo, L1_attn_fc1_w, L1_attn_fc1_b, L1_attn_fc2_w, L1_attn_fc2_b, L1_attn_ln_ffn_g, L1_attn_ln_ffn_b, L1_attn_n0_g, L1_attn_n0_b, L1_attn_n1_g, L1_attn_n1_b, L1_ffn_gate_w, L1_ffn_expert_bias, L1_ffn_shared_gate_up, L1_ffn_shared_down, L1_ffn_expert_gate_up, L1_ffn_expert_down):
    import jax
    import jax.numpy as jnp

    def _L0_tok_ref(img, W, b, token, pos):
        import jax, jax.numpy as jnp
        import numpy as np
        B, C, H, N_P, HID = (64, 3, 196, 14, 128)
        P = H // N_P
        IN_DIM = C * P * P
        SEQ = N_P * N_P + 1

        def sinusoidal_position(length, d):
            pos = jnp.arange(length, dtype=jnp.float32)[:, None]
            i = jnp.arange(d)[None, :]
            angle = pos / jnp.power(10000.0, (2 * (i // 2)).astype(jnp.float32) / d)
            return jnp.where(i % 2 == 0, jnp.sin(angle), jnp.cos(angle)).astype(jnp.float32)
        Bn = img.shape[0]
        patches = img.reshape(Bn, C, N_P, P, N_P, P)
        patches = patches.transpose(0, 2, 4, 1, 3, 5).reshape(Bn, N_P * N_P, IN_DIM)
        tokens = jnp.einsum('bsd,hd->bsh', patches, W) + b
        cls = jnp.broadcast_to(token[None, :, :], (Bn, 1, HID))
        out = jnp.concatenate([cls, tokens], axis=1) + pos
        return out

    def _L0_attn_ref(x, Wq, Wk, Wv, W1, b1, W2, b2):
        import jax, jax.numpy as jnp
        import numpy as np
        B, S, E, H = (4, 256, 128, 16)
        embed_dim = x.shape[-1]
        Q = jnp.einsum('bse,oe->bso', x, Wq)
        K = jnp.einsum('bse,oe->bso', x, Wk)
        V = jnp.einsum('bse,oe->bso', x, Wv)
        scores = jnp.einsum('bqe,bke->bqk', Q, K) / jnp.sqrt(jnp.float32(embed_dim))
        W1q, W1k = (W1[:, :embed_dim], W1[:, embed_dim:])
        hq = jnp.einsum('bqe,he->bqh', Q, W1q)
        hk = jnp.einsum('bke,he->bkh', K, W1k)
        hid = jnp.tanh(hq[:, :, None, :] + hk[:, None, :, :] + b1)
        est = jnp.einsum('bqkh,h->bqk', hid, W2[0]) + b2[0]
        attn = jax.nn.softmax(scores + est, axis=-1)
        return jnp.einsum('bqk,bke->bqe', attn, V)

    def _L0_ffn_ref(x, router_w, router_b, W1, b1, W2, b2):
        import jax, jax.numpy as jnp
        import numpy as np
        D_MODEL = 128
        D_FF = 512
        N_EXPERTS = 8
        TOP_K = 2
        leading = x.shape[:-1]
        d = x.shape[-1]
        xf = x.reshape(-1, d)
        n = xf.shape[0]
        logits = xf @ router_w + router_b
        probs = jax.nn.softmax(logits, axis=-1)
        sel_w, sel_idx = jax.lax.top_k(probs, TOP_K)
        sel_w = sel_w / (jnp.sum(sel_w, axis=-1, keepdims=True) + 1e-09)
        comb = jnp.zeros((n, N_EXPERTS), dtype=xf.dtype)
        comb = comb.at[jnp.arange(n)[:, None], sel_idx].add(sel_w)
        h = jnp.einsum('nd,edf->nef', xf, W1) + b1[None]
        h = jax.nn.gelu(h, approximate=False)
        y = jnp.einsum('nef,efd->ned', h, W2) + b2[None]
        out = jnp.einsum('ne,ned->nd', comb, y)
        return out.reshape(*leading, d)

    def _L1_attn_ref(src, mask, padding_mask, wq, bq, wk, bk, wv, bv, wg, bg, wo, bo, fc1_w, fc1_b, fc2_w, fc2_b, ln_ffn_g, ln_ffn_b, n0_g, n0_b, n1_g, n1_b):
        import jax, jax.numpy as jnp
        import numpy as np
        B, S, D, H = (4, 512, 128, 8)
        KD = D // H
        FFN = 4 * D

        def _ln(x, g, b, eps):
            mu = x.mean(-1, keepdims=True)
            var = ((x - mu) ** 2).mean(-1, keepdims=True)
            return (x - mu) / jnp.sqrt(var + eps) * g + b
        b, s, d = src.shape
        idx = jnp.arange(s)
        diff = (idx[:, None] - idx[None, :]).astype(src.dtype)
        decay = jnp.log(1.0 - 2.0 ** (-5.0 - jnp.arange(H, dtype=src.dtype)))
        dm = jnp.where(diff[None] >= 0, jnp.exp(diff[None] * decay[:, None, None]), 0.0)
        dm = dm / jnp.sqrt(dm.sum(-1, keepdims=True))
        q = (src @ wq.T + bq).reshape(b, s, H, KD).transpose(0, 2, 1, 3)
        k = ((src @ wk.T + bk) * KD ** (-0.5)).reshape(b, s, H, KD).transpose(0, 2, 1, 3)
        v = src @ wv.T + bv
        g = src @ wg.T + bg
        qk = jnp.einsum('bhid,bhjd->bhij', q, k) + dm[None]
        den = jnp.maximum(jnp.abs(jax.lax.stop_gradient(qk).sum(-1, keepdims=True)), 1.0)
        qk = qk / den
        vr = v.reshape(b, s, H, KD).transpose(0, 2, 1, 3)
        o = jnp.einsum('bhij,bhjd->bhid', qk, vr).transpose(0, 2, 1, 3)
        mu = o.mean(-1, keepdims=True)
        o = (o - mu) / jnp.sqrt(((o - mu) ** 2).mean(-1, keepdims=True) + 1e-06)
        o = jax.nn.silu(g) * o.reshape(b, s, d)
        o = o @ wo.T + bo
        x = _ln(src + o, n0_g, n0_b, 1e-05)
        h = jax.nn.gelu(x @ fc1_w.T + fc1_b, approximate=False)
        h = _ln(h, ln_ffn_g, ln_ffn_b, 1e-06)
        h = h @ fc2_w.T + fc2_b
        return _ln(x + h, n1_g, n1_b, 1e-05)

    def _L1_ffn_ref(x, gate_w, expert_bias, shared_gate_up, shared_down, expert_gate_up, expert_down):
        import jax, jax.numpy as jnp
        import numpy as np
        D_MODEL = 128
        D_FF = 128
        N_EXPERTS = 16
        TOP_K = 3
        BATCH, SEQ = (1, 512)

        def _swiglu(combined):
            gate, up = jnp.split(combined, 2, axis=-1)
            return jax.nn.silu(gate) * up
        B, S, D = x.shape
        xf = x.reshape(-1, D)
        shared_out = _swiglu(xf @ shared_gate_up.T) @ shared_down.T
        logits = xf @ gate_w.T
        affinity = jax.nn.sigmoid(logits)
        routing_scores = affinity + expert_bias
        _, sel = jax.lax.top_k(routing_scores, TOP_K)
        sel_aff = jnp.take_along_axis(affinity, sel, axis=1)
        gating = sel_aff / (sel_aff.sum(axis=-1, keepdims=True) + 1e-09)
        combined = jnp.einsum('td,efd->tef', xf, expert_gate_up)
        hidden = _swiglu(combined)
        expert_out = jnp.einsum('tef,edf->ted', hidden, expert_down)
        sel_out = jnp.take_along_axis(expert_out, sel[:, :, None], axis=1)
        routed_out = jnp.einsum('tk,tkd->td', gating, sel_out)
        out = shared_out + routed_out
        return out.reshape(B, S, D)
    h = _L0_tok_ref(x, L0_tok_W, L0_tok_b, L0_tok_token, L0_tok_pos)
    h = jnp.concatenate([h, txt], axis=1)
    h = h + _L0_attn_ref(_layernorm(h, axis=-1), L0_attn_Wq, L0_attn_Wk, L0_attn_Wv, L0_attn_W1, L0_attn_b1, L0_attn_W2, L0_attn_b2)
    h = h + _L0_ffn_ref(_layernorm(h, axis=-1), L0_ffn_router_w, L0_ffn_router_b, L0_ffn_W1, L0_ffn_b1, L0_ffn_W2, L0_ffn_b2)
    h = h + _L1_attn_ref(_layernorm(h, axis=-1), L1_attn_mask, L1_attn_padding_mask, L1_attn_wq, L1_attn_bq, L1_attn_wk, L1_attn_bk, L1_attn_wv, L1_attn_bv, L1_attn_wg, L1_attn_bg, L1_attn_wo, L1_attn_bo, L1_attn_fc1_w, L1_attn_fc1_b, L1_attn_fc2_w, L1_attn_fc2_b, L1_attn_ln_ffn_g, L1_attn_ln_ffn_b, L1_attn_n0_g, L1_attn_n0_b, L1_attn_n1_g, L1_attn_n1_b)
    h = h + _L1_ffn_ref(_layernorm(h, axis=-1), L1_ffn_gate_w, L1_ffn_expert_bias, L1_ffn_shared_gate_up, L1_ffn_shared_down, L1_ffn_expert_gate_up, L1_ffn_expert_down)
    return h

_drawn_inputs = setup_inputs


def setup_inputs(seed=0):
    import zlib

    import numpy as np

    out = dict(_drawn_inputs(seed))
    spreads = {'L0_attn_b1': (0.0, 0.8),
     'L0_ffn_router_b': (0.0, 0.1),
     'L1_attn_ln_ffn_g': (1.0, 0.2),
     'L1_attn_ln_ffn_b': (0.0, 0.436),
     'L1_attn_n0_g': (1.0, 0.2),
     'L1_attn_n0_b': (0.0, 0.1),
     'L1_attn_n1_g': (1.0, 0.2),
     'L1_attn_n1_b': (0.0, 0.1),
     'L1_ffn_expert_bias': (0.0, 0.8)}
    factors = {'L0_tok_b': 4.72,
     'L0_tok_token': 2.756,
     'L0_ffn_b1': 5.221,
     'L0_ffn_b2': 3.778,
     'L1_attn_wq': 8.0,
     'L1_attn_bq': 8.0,
     'L1_attn_wk': 8.0,
     'L1_attn_bk': 8.0,
     'L1_attn_wv': 4.799,
     'L1_attn_bv': 8.0,
     'L1_attn_wg': 4.628,
     'L1_attn_bg': 8.0,
     'L1_attn_wo': 4.655,
     'L1_attn_bo': 6.274,
     'L1_attn_fc1_b': 3.548,
     'L1_attn_fc2_b': 7.339,
     'L1_ffn_gate_w': 8.0,
     'L1_ffn_shared_gate_up': 8.0,
     'L1_ffn_shared_down': 8.0,
     'L1_ffn_expert_gate_up': 8.0,
     'L1_ffn_expert_down': 8.0}
    for name, (base, spread) in spreads.items():
        noise = np.random.default_rng([zlib.crc32(name.encode()), seed]).standard_normal(out[name].shape)
        drawn = base * np.exp(spread * noise) if base else spread * noise
        out[name] = jnp.asarray(drawn.astype(out[name].dtype))
    for name, factor in factors.items():
        out[name] = (out[name] * factor).astype(out[name].dtype)
    return out
```

```python
import math
from contextlib import ExitStack

import numpy as np
import concourse.bass as bass
from concourse import mybir

FP32 = mybir.dt.float32
U32 = mybir.dt.uint32
ALU = mybir.AluOpType
ACT = mybir.ActivationFunctionType
AX = mybir.AxisListType

B = 16
D = 128
N_PATCH, S_IMG, S_TXT = 14, 197, 128
S = S_IMG + S_TXT
P = 128
NC = (S + P - 1) // P
SP = NC * P
LAST = S - (NC - 1) * P
ROWS = [P] * (NC - 1) + [LAST]
KT, KR = 5, 118
E0, F0 = 8, 512
FC = F0 // P
E1, F1 = 16, 128
NH, HD = 8, 16
AH = 16
QG = P // AH
NG = (S + QG - 1) // QG
FF = 512
EPS = 1e-5
SCALE = 1.0 / math.sqrt(D)
NTH = 8
SLOTS = {(n // 2, n % 2): (5 * (n - 1), min(5 * n, NG)) for n in range(1, 10)}


class Signal:

    def __init__(self, sem, per, start=0):
        self.sem, self.per, self.start = sem, per, start

    def at(self, b, k):
        return b * self.per + k + self.start


def need(eng, sig, b, k, alone=None):
    v = sig.at(b, k)
    if not (isinstance(v, int) and v <= 0):
        eng.wait_ge(sig.sem, v)
        if alone is not None:
            eng.sem_inc(alone.sem, 1)


class Chain:

    def __init__(self, eng, sig, b):
        self.eng, self.sig, self.b, self.n = eng, sig, b, 0

    def __call__(self, ins):
        self.n += 1
        ins.then_inc(self.sig.sem, 1)
        self.eng.wait_ge(self.sig.sem, self.sig.at(self.b, self.n))

    def end(self, per):
        assert self.n == per, (self.n, per)
        return per


def program(nc, t, out, stop=None):
    ctx = ExitStack()
    with ctx:
        def sb(name, shape, dt=FP32):
            return ctx.enter_context(nc.sbuf_tensor(name, shape, dt))

        def signal(name, per=1, start=0):
            return Signal(ctx.enter_context(nc.semaphore(name)), per, start)

        h_all = sb("h_all", [P, B * SP])
        OW = D + NH
        v_all = sb("v_all", [P, B * SP])
        src_d = nc.dram_tensor("src_d", (B, P, SP), FP32, kind="Internal").ap()
        g_d = nc.dram_tensor("g_d", (B, P, SP), FP32, kind="Internal").ap()
        o_d = nc.dram_tensor("o_d", (B, P, NC * OW), FP32, kind="Internal").ap()
        src_saved, g_saved, o_saved = signal("src_saved", 16), signal("g_saved", 16), signal("o_saved", 16)
        ident = sb("ident", [P, P])
        ones = sb("ones", [P, P])
        neghalf = sb("neghalf", [P, 24])
        iota = sb("iota", [P, 16])
        w_moe0 = sb("w_moe0", [P, E0 * F0 + E0 * FC * D])
        w1 = w_moe0[:, 0:E0 * F0].rearrange("p (e f) -> p e f", e=E0)
        w2 = w_moe0[:, E0 * F0:].rearrange("p (e c d) -> p e c d", e=E0, c=FC)
        decay = w_moe0[:, 0:NH * NC * S].rearrange("p (h c i) -> p h c i", h=NH, c=NC)
        b1 = sb("b1", [P, E0 * FC])
        b2 = sb("b2", [E0, D])
        rw = sb("rw", [P, E0])
        rb = sb("rb", [P, E0])
        tokw = sb("tokw", [KR, KT, D])
        base = sb("base", [P, 2, D])
        base_add = sb("base_add", [P, 2, D])
        wqkv = sb("wqkv", [P, 3, D])
        w1q = sb("w1q", [P, QG, P])
        w1k = sb("w1k", [P, P])
        hb1 = sb("hb1", [P, 1])
        w2s = sb("w2s", [P, 24 + QG + 24])
        b2a = sb("b2a", [P, 1])
        wkvg = sb("wkvg", [P, 3 * D])
        bkvg = sb("bkvg", [P, 3 * D])
        wq1 = sb("wq1", [P, D])
        bq1 = sb("bq1", [P, 1])
        bd = sb("bd", [P, D])
        bd8 = sb("bd8", [P, NH])
        dsum = sb("dsum", [P, NC, NH])
        wo = sb("wo", [P, D])
        bo = sb("bo", [1, D])
        fc1 = sb("fc1", [P, FF])
        fc1b = sb("fc1b", [P, FC])
        fc2 = sb("fc2", [P, FC, D])
        fc2g = sb("fc2g", [P, FC, D + 1])
        fc2b = sb("fc2b", [1, D])
        lng = sb("lng", [P, FC])
        lnb = sb("lnb", [P, FC])
        c1 = sb("c1", [P, D])
        c2 = sb("c2", [P, D])
        n0g = sb("n0g", [P, D]); n0b = sb("n0b", [P, D])
        n1g = sb("n1g", [P, D]); n1b = sb("n1b", [P, D])
        gw = sb("gw", [P, E1])
        eb = sb("eb", [P, E1])

        xn = sb("xn", [P, SP])
        xT = sb("xT", [P, SP])
        st = sb("st", [P, NC, 6]); mv = sb("mv", [P, NC, 2]); ve = sb("ve", [P, NC]); rs = sb("rs", [P, NC])
        xTm = sb("xTm", [P, SP])
        combm = sb("combm", [P, NC, E1])
        combT = sb("combT", [E0, SP])
        cst = sb("cst", [P, NC, 6]); cmv = sb("cmv", [P, NC, 2]); cve = sb("cve", [P, NC]); crs = sb("crs", [P, NC])

        banks = [ctx.enter_context(nc.psum_tensor(f"bank{i}", [P, 512], FP32)) for i in range(8)]
        misc = banks[0:2]

        w_tok, w_att, w_moe, w_l1, txt_in, dec_in = (signal(n) for n in ("w_tok", "w_att", "w_moe", "w_l1", "txt_in", "dec_in"))
        base_in, tok_row_in, consts, ident_step = (signal(n) for n in ("base_in", "tok_row_in", "consts", "ident_step"))
        consts_v, setup_v, setup_pe = signal("consts_v"), signal("setup_v"), signal("setup_pe")
        waited = signal("waited")
        patch_in, patch_used = signal("patch_in", 16), signal("patch_used")

        def h3(b):
            return h_all[:, bass.ds(b * SP, SP)].rearrange("p (c d) -> p c d", c=NC)

        def h1(b, c):
            return h_all[:, bass.ds(b * SP + c * P, P)]

        def row(x, b):
            return x[bass.ds(b, 1)].rearrange("a p n -> (a p) n")

        def token_stats(x, st, mv, link):
            nc.vector.sem_inc(waited.sem, 1)
            for c in range(NC):
                last = nc.vector.bn_stats(st[:, c, :], x[c])
            link(last)
            nc.vector.sem_inc(waited.sem, 1)
            for c in range(NC):
                last = nc.vector.bn_aggr(mv[:, c, :], st[:, c, :])
            link(last)

        with ExitStack() as l0:
            def sb0(name, shape, dt=FP32):
                return l0.enter_context(nc.sbuf_tensor(name, shape, dt))

            hid = sb0("hid", [P, 2, FC, SP])
            src_st = sb0("src_st", [P, SP]); srcT = sb0("srcT", [P, SP])
            k_st = sb0("k_st", [P, NC, D]); v_st = sb0("v_st", [P, NC, D + 1])
            g_st = sb0("g_st", [P, NC, D]); qrT = sb0("qrT", [P, SP])
            kv_st = sb0("kv_st", [P, OW]); ksum = sb0("ksum", [P, 1])
            patch = sb0("patch", [KR, KT, S_IMG])
            xf = sb0("xf", [P, SP]); xfT = sb0("xfT", [P, SP])
            st_f = sb0("st_f", [P, NC, 6]); mv_f = sb0("mv_f", [P, NC, 2]); ve_f = sb0("ve_f", [P, NC]); rs_f = sb0("rs_f", [P, NC])
            qT = sb0("qT", [P, SP]); qTs = sb0("qTs", [P, SP]); kT = sb0("kT", [P, S])
            v_sb = sb0("v_sb", [P, NC, D])
            hk = sb0("hk", [P, S]); hq = sb0("hq", [P, NG])
            th = sb0("th", [P, NTH, S])
            sc = sb0("sc", [P, NC, S]); smax = sb0("smax", [P, NC]); nmax = sb0("nmax", [P, NC])
            pr = sb0("pr", [P, NC, S]); rsum = sb0("rsum", [P, NC]); rinv = sb0("rinv", [P, NC])
            pT = sb0("pT", [P, NC, SP])
            lg = sb0("lg", [P, NC, E0]); lmax = sb0("lmax", [P, NC]); ex = sb0("ex", [P, NC, E0])
            esum = sb0("esum", [P, NC]); einv = sb0("einv", [P, NC]); prob = sb0("prob", [P, NC, E0])
            top = sb0("top", [P, NC, 8]); tidx = sb0("tidx", [P, NC, 8], U32); tidf = sb0("tidf", [P, NC, 2])
            wsum = sb0("wsum", [P, NC]); winv = sb0("winv", [P, NC]); wt = sb0("wt", [P, NC, 2])
            eq = sb0("eq", [P, 2, NC, E0]); cp = sb0("cp", [P, 2, NC, E0])
            sc_ps, h_ps, y_ps, r_ps = banks[2:4], banks[4:6], banks[6], banks[7]

            misc_full, misc_free = signal("misc_full", 5), signal("misc_free", 5)
            m_full, m_free = signal("m_full", 3), signal("m_free", 3)
            f_full, f_free = signal("f_full", 6), signal("f_free", 6)
            fvar_ok0, frstd_ok, xf_ok = signal("fvar_ok0"), signal("frstd_ok"), signal("xf_ok")
            var_ok, rstd_ok, xn_ok = signal("var_ok"), signal("rstd_ok"), signal("xn_ok")
            hbias_ok, tanh_ok, est_ok = signal("hbias_ok"), signal("tanh_ok", NG), signal("est_ok", NG)
            sc_full, sc_free = signal("sc_full", NC), signal("sc_free", NC)
            nmax_ok, exp_ok = signal("nmax_ok"), signal("exp_ok")
            lg_ok, ex_ok, comb_ok, in_ok = signal("lg_ok"), signal("ex_ok"), signal("comb_ok"), signal("in_ok")
            hid_full, hid_ok = signal("hid_full", E0 * FC), signal("hid_ok", E0 * FC, 2)
            y_full, y_free = signal("y_full", E0, 2), signal("y_free", E0, 1)
            a_chain, f_chain, m_chain = signal("a_chain", 3), signal("f_chain", 2), signal("m_chain", 12)
            l0_done = signal("l0_done")
            r_chain, rvar_ok, rrstd_ok = signal("r_chain", 3), signal("rvar_ok"), signal("rrstd_ok")
            src_ok, v_saved, o_ok = signal("src_ok"), signal("v_saved"), signal("o_ok")
            parts_free = signal("parts_free", 1, 1)
            o_st = sb0("o_st", [P, NC * OW])
            r_full, r_free = signal("r_full", 6), signal("r_free", 6, 1)
            kvg_ok = signal("kvg_ok")
            st_r = sb0("st_r", [P, NC, 6]); mv_r = sb0("mv_r", [P, NC, 2]); ve_r = sb0("ve_r", [P, NC]); rs_r = sb0("rs_r", [P, NC])

            block = l0.enter_context(nc.Block())

            @block.sync
            def _(sp):
                sp.dma_start(tokw[:], t["tokw"]).then_inc(w_tok.sem, 16)
                sp.dma_start(patch[:], t["patches"][0]).then_inc(patch_in.sem, 16)
                sp.dma_start(base[:, 0, :], t["L0_tok_pos"][0:P, :]).then_inc(w_tok.sem, 16)
                sp.dma_start(base[0:S_IMG - P, 1, :], t["L0_tok_pos"][P:S_IMG, :]).then_inc(w_tok.sem, 16)
                sp.dma_start(base_add[:, 0, :], t["L0_tok_b"].partition_broadcast(P)).then_inc(base_in.sem, 16)
                sp.dma_start(base_add[:, 1, :], t["L0_tok_b"].partition_broadcast(P)).then_inc(w_tok.sem, 16)
                sp.wait_ge(base_in.sem, 16)
                sp.dma_start(base_add[0:1, 0, :], t["L0_tok_token"]).then_inc(w_tok.sem, 16)
                sp.wait_ge(consts_v.sem, 1)
                txt, hv = t["txt"], h_all[:, :].rearrange("p (b c d) -> p b c d", b=B, c=NC)
                sp.dma_start(hv[S_IMG - P:P, :, 1, :], txt[:, 0:2 * P - S_IMG, :].rearrange("b s d -> s b d")).then_inc(txt_in.sem, 16)
                sp.dma_start(hv[0:LAST, :, 2, :], txt[:, 2 * P - S_IMG:, :].rearrange("b s d -> s b d")).then_inc(txt_in.sem, 16)
                sp.dma_start(wqkv[:], t["wqkv0"]).then_inc(w_att.sem, 16)
                sp.wait_ge(consts.sem, 1)
                for r in range(QG):
                    sp.dma_start(w1q[:, r, r * AH:(r + 1) * AH], t["w1q"]).then_inc(w_att.sem, 16)
                    sp.dma_start(w1k[:, r * AH:(r + 1) * AH], t["w1k"]).then_inc(w_att.sem, 16)
                    sp.dma_start(hb1[r * AH:(r + 1) * AH, :], t["b1a"]).then_inc(w_att.sem, 16)
                    sp.dma_start(w2s[r * AH:(r + 1) * AH, 24 + r:25 + r], t["w2a"]).then_inc(w_att.sem, 16)
                sp.dma_start(b2a[:], t["L0_attn_b2"].partition_broadcast(P)).then_inc(w_att.sem, 16)
                sp.dma_start(rw[:], t["L0_ffn_router_w"]).then_inc(w_att.sem, 16)
                sp.dma_start(rb[:], t["L0_ffn_router_b"].partition_broadcast(P)).then_inc(w_att.sem, 16)
                sp.dma_start(w1, t["w1e"]).then_inc(w_moe.sem, 16)
                sp.dma_start(b1[:], t["b1e"]).then_inc(w_moe.sem, 16)
                sp.dma_start(w2, t["w2e"]).then_inc(w_moe.sem, 16)
                sp.dma_start(b2[:], t["L0_ffn_b2"]).then_inc(w_moe.sem, 16)
                for dst, src in ((wkvg[:], t["wkvg"]), (wq1[:], t["wq1"]), (bq1[:], t["bq1"]), (bd[:], t["bd"]), (bd8[:], t["bd8"]),
                                 (dsum[:], t["dsum"]), (wo[:], t["wo"]), (bo[:], t["bo"]), (fc1[:], t["fc1"]), (fc1b[:], t["fc1b"]),
                                 (fc2[:], t["fc2"]), (fc2b[:], t["fc2b"]), (lng[:], t["lng"]), (lnb[:], t["lnb"]),
                                 (bkvg[:, 0:D], t["L1_attn_bk"].partition_broadcast(P)),
                                 (bkvg[:, D:2 * D], t["L1_attn_bv"].partition_broadcast(P)),
                                 (bkvg[:, 2 * D:], t["L1_attn_bg"].partition_broadcast(P)),
                                 (n0g[:], t["L1_attn_n0_g"].partition_broadcast(P)), (n0b[:], t["L1_attn_n0_b"].partition_broadcast(P)),
                                 (n1g[:], t["L1_attn_n1_g"].partition_broadcast(P)), (n1b[:], t["L1_attn_n1_b"].partition_broadcast(P)),
                                 (gw[:], t["gw"]), (eb[:], t["L1_ffn_expert_bias"].partition_broadcast(P)),
                                 ):
                    sp.dma_start(dst, src).then_inc(w_l1.sem, 16)
                with sp.Fori(1, B) as b:
                    sp.wait_ge(patch_used.sem, b)
                    sp.dma_start(patch[:], t["patches"][bass.ds(b, 1)].rearrange("b k c s -> k (b c) s")).then_inc(patch_in.sem, 16)
                sp.wait_ge(w_l1.sem, 16 * 23)
                sp.wait_ge(l0_done.sem, 1)
                sp.dma_start(decay, t["decay"]).then_inc(dec_in.sem, 16)

            @block.gpsimd
            def _(pool):
                nc.gpsimd.memset(w1q[:], 0.0)
                nc.gpsimd.memset(w2s[:], 0.0).then_inc(consts.sem, 1)
                nc.gpsimd.memset(neghalf[:], -0.5)
                nc.gpsimd.memset(ident[:], 0.0).then_inc(ident_step.sem, 1)
                nc.gpsimd.iota(iota[:], pattern=[[1, 16]], base=0, channel_multiplier=0, allow_small_or_imprecise_dtypes=True)
                pool.wait_ge(ident_step.sem, 1)
                nc.gpsimd.affine_select(out=ident[:], in_=ident[:], compare_op=ALU.not_equal, fill=1.0, base=0,
                                        pattern=[[-1, P]], channel_multiplier=1).then_inc(consts.sem, 1)

                def step(att, front, ret):
                    if ret is not None:
                        need(pool, rvar_ok, ret, 1)
                        nc.gpsimd.tensor_tensor(rs_r[:], ve_r[:], neghalf[:, 0:NC], ALU.pow).then_inc(rrstd_ok.sem, 1)
                        need(pool, src_ok, ret, 1, waited)
                        pool.dma_start(row(src_d, ret), src_st[:]).then_inc(src_saved.sem, 16)
                    if front is not None:
                        need(pool, fvar_ok0, front, 1)
                        nc.gpsimd.tensor_tensor(rs_f[:], ve_f[:], neghalf[:, 0:NC], ALU.pow).then_inc(frstd_ok.sem, 1)
                    if ret is not None:
                        need(pool, kvg_ok, ret, 1, waited)
                        pool.dma_start(row(g_d, ret), g_st[:].rearrange("p c d -> p (c d)")).then_inc(g_saved.sem, 16)
                    if att is not None:
                        need(pool, var_ok, att, 1)
                        nc.gpsimd.tensor_tensor(rs[:], ve[:], neghalf[:, 0:NC], ALU.pow).then_inc(rstd_ok.sem, 1)
                    if ret is not None:
                        nc.gpsimd.tensor_copy(v_all[:, bass.ds(ret * SP, SP)].rearrange("p (c d) -> p c d", c=NC), v_st[:, :, 0:D])\
                            .then_inc(v_saved.sem, 1)
                        need(pool, o_ok, ret, 1, waited)
                        pool.dma_start(row(o_d, ret), o_st[:]).then_inc(o_saved.sem, 16)
                        for sig in (src_saved, g_saved, o_saved):
                            need(pool, sig, ret, 16)
                        need(pool, v_saved, ret, 1, parts_free)

                pool.sem_inc(parts_free.sem, parts_free.start)
                step(None, 0, None)
                step(0, 1, None)
                step(1, 2, None)
                with pool.Fori(0, B - 3) as b:
                    step(b + 2, b + 3, b)
                step(B - 1, None, B - 3)
                step(None, None, B - 2)
                step(None, None, B - 1)
                for sig in (src_saved, g_saved, o_saved):
                    pool.wait_ge(sig.sem, sig.at(B, 0))

            @block.tensor
            def _(pe):
                def claim(b, n):
                    if n == 0:
                        need(pe, misc_free, b, 0)
                        need(pe, m_free, b, 0)
                    else:
                        need(pe, misc_free, b, n - 1)
                    return misc[n % 2]

                def claim_f(b, n):
                    need(pe, f_free, b, n - 1 if n else 0)
                    if n < 2:
                        need(pe, sc_free, b, 0)
                    return sc_ps[1 - n % 2]

                def tokens(b):
                    need(pe, patch_in, b, 16)
                    m = claim_f(b, 0)
                    for c, rows in ((0, P), (1, S_IMG - P)):
                        for k in range(KT):
                            last = nc.tensor.matmul(m[0:rows, c * D:(c + 1) * D], patch[:, k, c * P:c * P + rows], tokw[:, k, :],
                                                    start=(k == 0), stop=(k == KT - 1))
                            if c == 1 and k == KT - 1:
                                last.then_inc(f_full.sem, 1)
                    pe.drain().then_inc(patch_used.sem, 1)

                def front(b, slot):
                    if slot == (5, 0):
                        tokens(b)
                    if slot == (6, 0):
                        need(pe, xf_ok, b, 1)
                        m = claim_f(b, 1)
                        for c in range(NC):
                            last = nc.tensor.transpose(m[:, c * P:(c + 1) * P], xf[:, c * D:(c + 1) * D], ident[:])
                        last.then_inc(f_full.sem, 1)
                    if slot == (6, 1):
                        need(pe, f_free, b, 2)
                        for n in (2, 3):
                            m = claim_f(b, n)
                            nc.tensor.matmul(m[:, 0:S], wqkv[:, n - 2, :], xfT[:, 0:S], start=True, stop=True).then_inc(f_full.sem, 1)
                    if slot == (7, 0):
                        m = claim_f(b, 4)
                        for c in range(NC):
                            last = nc.tensor.matmul(m[:, c * D:(c + 1) * D], xfT[:, c * P:(c + 1) * P], wqkv[:, 2, :], start=True, stop=True)
                        last.then_inc(f_full.sem, 1)
                    if slot == (7, 1):
                        need(pe, f_free, b, 4)
                        m = claim_f(b, 5)
                        nc.tensor.matmul(m[:, 0:S], w1k[:], kT[:], start=True, stop=True)
                        for r in range(QG):
                            last = nc.tensor.matmul(m[:, S:S + NG], w1q[:, r, :], qT[:, r:r + QG * (NG - 1) + 1:QG],
                                                    start=(r == 0), stop=(r == QG - 1))
                        last.then_inc(f_full.sem, 1)

                def score_groups(b, g0, g1):
                    for g in range(g0, g1):
                        c, gl = g // 16, g % 16
                        if gl == 0:
                            if c < 2:
                                need(pe, f_free, b, 6)
                            else:
                                need(pe, sc_free, b, c - 1)
                            nc.tensor.matmul(sc_ps[c % 2][:, 0:S], qTs[:, c * P:(c + 1) * P], kT[:], start=True, stop=True)
                        need(pe, tanh_ok, b, g + 1)
                        j, off = gl // 4, 24 - QG * (gl % 4)
                        last = nc.tensor.matmul(sc_ps[c % 2][32 * j:32 * j + 32, 0:S], w2s[:, off:off + 32], th[:, g % NTH, :],
                                                start=False, stop=True, skip_group_check=True)
                        last.then_inc(est_ok.sem, 1)

                def attend(b, slot):
                    if slot in SLOTS:
                        score_groups(b, *SLOTS[slot])
                    if slot == (6, 0):
                        need(pe, exp_ok, b, 1)
                        for kc in range(NC):
                            m = claim(b, kc)
                            for qc in range(NC):
                                last = nc.tensor.transpose(m[0:ROWS[kc], qc * P:(qc + 1) * P], pr[:, qc, kc * P:kc * P + ROWS[kc]], ident[:])
                            last.then_inc(misc_full.sem, 1)
                    if slot == (6, 1):
                        need(pe, misc_free, b, 3)
                        m = claim(b, 3)
                        for qc in range(NC):
                            for kc in range(NC):
                                last = nc.tensor.matmul(m[:, qc * D:(qc + 1) * D], pT[0:ROWS[kc], kc, qc * P:(qc + 1) * P],
                                                        v_sb[0:ROWS[kc], kc, :], start=(kc == 0), stop=(kc == NC - 1))
                        last.then_inc(misc_full.sem, 1)
                    if slot == (7, 1):
                        need(pe, xn_ok, b, 1)
                        m = claim(b, 4)
                        for c in range(NC):
                            last = nc.tensor.transpose(m[:, c * P:(c + 1) * P], xn[:, c * D:(c + 1) * D], ident[:])
                        last.then_inc(misc_full.sem, 1)

                def router(b):
                    need(pe, in_ok, b, 1)
                    for c in range(NC):
                        last = nc.tensor.matmul(misc[1][:, c * E0:(c + 1) * E0], xTm[:, c * P:(c + 1) * P], rw[:], start=True, stop=True)
                    last.then_inc(m_full.sem, 1)

                def up(b, e, half):
                    if e == 0:
                        need(pe, in_ok, b, 1)
                    for f in (2 * half, 2 * half + 1):
                        need(pe, hid_ok, b, FC * e + f - 1)
                        nc.tensor.matmul(h_ps[f % 2][:, 0:S], w1[:, e, f * P:(f + 1) * P], xTm[:, 0:S], start=True, stop=True)\
                            .then_inc(hid_full.sem, 1)

                def down(b, e):
                    need(pe, hid_ok, b, FC * (e + 1))
                    need(pe, y_free, b, e)
                    for c in range(NC):
                        for f in range(FC):
                            last = nc.tensor.matmul(y_ps[:, c * D:(c + 1) * D], hid[:, e % 2, f, c * P:(c + 1) * P], w2[:, e, f, :],
                                                    start=(f == 0), stop=(f == FC - 1))
                    last.then_inc(y_full.sem, 1)

                def biases(b, k):
                    if k == 0:
                        need(pe, comb_ok, b, 1)
                        for c in range(NC):
                            last = nc.tensor.transpose(misc[0][0:E0, c * P:(c + 1) * P], combm[:, c, 0:E0], ident[:])
                        last.then_inc(m_full.sem, 1)
                    if k == 1:
                        need(pe, m_free, b, 2)
                        for c in range(NC):
                            last = nc.tensor.matmul(misc[1][:, c * D:(c + 1) * D], combT[:, c * P:(c + 1) * P], b2[:], start=True, stop=True)
                        last.then_inc(m_full.sem, 1)

                def retain(b, slot):
                    if slot == (1, 1):
                        need(pe, src_ok, b, 1)
                        need(pe, r_free, b, 0)
                        for c in range(NC):
                            last = nc.tensor.transpose(r_ps[:, c * P:(c + 1) * P], src_st[:, c * D:(c + 1) * D], ident[:])
                        last.then_inc(r_full.sem, 1)
                    for c in range(NC):
                        if slot == (c + 2, 1):
                            need(pe, r_free, b, c + 1)
                            nc.tensor.matmul(r_ps[:, 0:3 * D], srcT[:, c * P:(c + 1) * P], wkvg[:], start=True, stop=True).then_inc(r_full.sem, 1)
                    if slot == (5, 1):
                        need(pe, r_free, b, 4)
                        nc.tensor.matmul(r_ps[:, 0:S], wq1[:], srcT[:, 0:S], start=True, stop=True)
                        for c in range(NC):
                            last = nc.tensor.matmul(r_ps[:, S:S + D + 1], k_st[0:ROWS[c], c, :], v_st[0:ROWS[c], c, :],
                                                    start=(c == 0), stop=(c == NC - 1))
                        last.then_inc(r_full.sem, 1)
                    if slot == (6, 1):
                        need(pe, r_free, b, 5)
                        for c in range(NC):
                            last = nc.tensor.matmul(r_ps[:, c * OW:(c + 1) * OW], qrT[:, c * P:(c + 1) * P], kv_st[:], start=True, stop=True)
                        last.then_inc(r_full.sem, 1)

                def step(moe, att, fro, ret):
                    for e in range(E0):
                        for k in range(2):
                            if moe is not None:
                                up(moe, e, k)
                                if k == 1 and e:
                                    down(moe, e - 1)
                                if (e, k) == (0, 0):
                                    router(moe)
                                if (e, k) in ((2, 0), (2, 1)):
                                    biases(moe, k)
                            if att is not None:
                                attend(att, (e, k))
                            if fro is not None:
                                front(fro, (e, k))
                            if ret is not None:
                                retain(ret, (e, k))
                    if moe is not None:
                        down(moe, E0 - 1)

                pe.sem_inc(y_full.sem, y_full.start)
                pe.wait_ge(w_tok.sem, 16 * 5)
                pe.wait_ge(consts.sem, 2)
                pe.wait_ge(w_att.sem, 16 * (4 * QG + 4))
                pe.wait_ge(consts_v.sem, 2)
                step(None, None, 0, None)
                step(None, 0, 1, None)
                pe.wait_ge(w_moe.sem, 16 * 4)
                pe.wait_ge(w_l1.sem, 16 * 23)
                step(0, 1, 2, None)
                with pe.Fori(0, B - 3) as b:
                    step(b + 1, b + 2, b + 3, b)
                step(B - 2, B - 1, None, B - 3)
                step(B - 1, None, None, B - 2)
                step(None, None, None, B - 1)
                pe.drain().then_inc(l0_done.sem, 1)

            @block.scalar
            def _(act):
                def attend(b, slot):
                    n = 2 * slot[0] + slot[1] + 1
                    for g in range(*SLOTS.get((n // 2, n % 2), (0, 0))):
                        if g == 0:
                            need(act, hbias_ok, b, 1)
                        if g >= NTH:
                            need(act, est_ok, b, g - NTH + 1)
                        else:
                            need(act, est_ok, b, 0)
                        nc.scalar.activation(th[:, g % NTH, :], hk[:], ACT.Tanh, bias=hq[:, g:g + 1]).then_inc(tanh_ok.sem, 1)
                    if slot == (5, 0):
                        need(act, nmax_ok, b, 1)
                        need(act, misc_free, b, 0)
                        for c in range(NC):
                            last = nc.scalar.activation(pr[:, c, :], sc[:, c, :], ACT.Exp, bias=nmax[:, c:c + 1], accum_out=rsum[:, c:c + 1])
                        last.then_inc(exp_ok.sem, 1)

                def route(b):
                    need(act, lg_ok, b, 1)
                    nc.scalar.activation(ex[:], lg[:], ACT.Exp).then_inc(ex_ok.sem, 1)

                def gelu(b, e):
                    need(act, y_full, b, e - 1)
                    for f in range(FC):
                        need(act, hid_full, b, FC * e + f + 1)
                        nc.scalar.activation(hid[:, e % 2, f, 0:S], h_ps[f % 2][:, 0:S], ACT.Gelu, bias=b1[:, e * FC + f:e * FC + f + 1])\
                            .then_inc(hid_ok.sem, 1)

                def step(moe, att):
                    for e in range(E0):
                        if moe is not None and e == 1:
                            route(moe)
                        if moe is not None:
                            gelu(moe, e)
                        if att is not None:
                            attend(att, (e, 0))
                            attend(att, (e, 1))

                act.sem_inc(hid_ok.sem, hid_ok.start)
                act.wait_ge(consts_v.sem, 2)
                step(None, 0)
                act.wait_ge(w_moe.sem, 16 * 4)
                step(0, 1)
                with act.Fori(1, B - 1) as b:
                    step(b, b + 1)
                step(B - 1, None)

            @block.vector
            def _(dve):
                dve.sem_inc(y_free.sem, y_free.start)
                nc.vector.memset(h_all[64:P, :], 0.0).then_inc(consts_v.sem, 1)
                nc.vector.memset(ones[:], 1.0)
                nc.vector.memset(qT[:, S:SP], 0.0)
                nc.vector.memset(qTs[:, S:SP], 0.0)
                nc.vector.memset(qrT[:, S:SP], 0.0)
                nc.vector.memset(v_st[:], 1.0)
                dve.sem_inc(r_free.sem, r_free.start)
                nc.vector.memset(hid[:], 0.0).then_inc(consts_v.sem, 1)
                dve.wait_ge(w_tok.sem, 16 * 5)
                nc.vector.tensor_tensor(base[:, 0, :], base[:, 0, :], base_add[:, 0, :], ALU.add)
                nc.vector.tensor_tensor(base[0:S_IMG - P, 1, :], base[0:S_IMG - P, 1, :], base_add[0:S_IMG - P, 1, :], ALU.add)\
                    .then_inc(consts_v.sem, 1)
                dve.wait_ge(consts_v.sem, 3)
                dve.wait_ge(txt_in.sem, 32)
                dve.wait_ge(consts.sem, 2)
                dve.wait_ge(w_att.sem, 16 * (4 * QG + 4))

                def attend(b, slot, link):
                    for c, at in ((0, (2, 1)), (1, (4, 0)), (2, (5, 0))):
                        if slot == at:
                            need(dve, est_ok, b, min(16 * (c + 1), NG))
                            need(dve, exp_ok, b, 0)
                            nc.vector.tensor_scalar(sc[:, c, :], sc_ps[c % 2][:, 0:S], b2a[:], None, ALU.add, ALU.max,
                                                    accum_out=smax[:, c:c + 1]).then_inc(sc_free.sem, 1)
                    if slot == (5, 0):
                        need(dve, sc_free, b, NC)
                        nc.vector.tensor_scalar(nmax[:], smax[:], -1.0, None, ALU.mult).then_inc(nmax_ok.sem, 1)
                    if slot == (6, 0):
                        for kc in range(NC):
                            need(dve, misc_full, b, kc + 1)
                            nc.vector.tensor_copy(pT[0:ROWS[kc], kc, :], misc[kc % 2][0:ROWS[kc], 0:SP]).then_inc(misc_free.sem, 1)
                    if slot == (6, 1):
                        need(dve, exp_ok, b, 1)
                        link(nc.vector.reciprocal(rinv[:], rsum[:]))
                        need(dve, misc_full, b, 4)
                        for c in range(NC):
                            last = nc.vector.scalar_tensor_tensor(h1(b, c), misc[1][:, c * D:(c + 1) * D], rinv[:, c:c + 1], h1(b, c), ALU.mult, ALU.add)
                        last.then_inc(misc_free.sem, 1)
                        need(dve, misc_free, b, 4)
                        token_stats([h1(b, c) for c in range(NC)], st, mv, link)
                        nc.vector.tensor_scalar(ve[:], mv[:, :, 1], EPS, None, ALU.add).then_inc(var_ok.sem, 1)
                    if slot == (7, 0):
                        need(dve, rstd_ok, b, 1)
                        for c in range(NC):
                            last = nc.vector.tensor_scalar(xn[:, c * D:(c + 1) * D], h1(b, c), mv[:, c, 0:1], rs[:, c:c + 1],
                                                           ALU.subtract, ALU.mult)
                        last.then_inc(xn_ok.sem, 1)
                    if slot == (7, 1):
                        need(dve, hid_full, b, 0)
                        need(dve, misc_full, b, 5)
                        nc.vector.tensor_copy(xTm[:], misc[0][:, 0:SP]).then_inc(misc_free.sem, 1)
                        need(dve, misc_free, b, 5)
                        dve.sem_inc(in_ok.sem, 1)

                def front(b, slot, link):
                    if slot == (5, 0):
                        need(dve, f_full, b, 1)
                        m = sc_ps[1]
                        nc.vector.tensor_tensor(h1(b, 0), m[:, 0:D], base[:, 0, :], ALU.add)
                        rows = S_IMG - P
                        nc.vector.tensor_tensor(h_all[0:rows, bass.ds(b * SP + P, P)], m[0:rows, D:2 * D], base[0:rows, 1, :], ALU.add)\
                            .then_inc(f_free.sem, 1)
                        need(dve, f_free, b, 1)
                        token_stats([h1(b, c) for c in range(NC)], st_f, mv_f, link)
                        nc.vector.tensor_scalar(ve_f[:], mv_f[:, :, 1], EPS, None, ALU.add).then_inc(fvar_ok0.sem, 1)
                    if slot == (5, 1):
                        need(dve, frstd_ok, b, 1)
                        for c in range(NC):
                            last = nc.vector.tensor_scalar(xf[:, c * D:(c + 1) * D], h1(b, c), mv_f[:, c, 0:1], rs_f[:, c:c + 1],
                                                           ALU.subtract, ALU.mult)
                        last.then_inc(xf_ok.sem, 1)
                    if slot == (6, 0):
                        need(dve, f_full, b, 2)
                        nc.vector.tensor_copy(xfT[:], sc_ps[0][:, 0:SP]).then_inc(f_free.sem, 1)
                    if slot == (6, 1):
                        need(dve, f_full, b, 3)
                        nc.vector.tensor_copy(qT[:, 0:S], sc_ps[1][:, 0:S])
                        nc.vector.tensor_scalar(qTs[:, 0:S], sc_ps[1][:, 0:S], SCALE, None, ALU.mult).then_inc(f_free.sem, 1)
                        need(dve, f_full, b, 4)
                        nc.vector.tensor_copy(kT[:], sc_ps[0][:, 0:S]).then_inc(f_free.sem, 1)
                    if slot == (7, 0):
                        need(dve, f_full, b, 5)
                        nc.vector.tensor_copy(v_sb[:].rearrange("p c d -> p (c d)"), sc_ps[1][:, 0:SP]).then_inc(f_free.sem, 1)
                    if slot == (7, 1):
                        need(dve, f_full, b, 6)
                        need(dve, tanh_ok, b, 0)
                        nc.vector.tensor_copy(hk[:], sc_ps[0][:, 0:S])
                        nc.vector.tensor_scalar(hq[:], sc_ps[0][:, S:S + NG], hb1[:], None, ALU.add).then_inc(f_free.sem, 1)
                        need(dve, f_free, b, 6)
                        dve.sem_inc(hbias_ok.sem, 1)

                def bc(x, n):
                    return x.unsqueeze(2).broadcast_to([P, NC, n])

                def route(b, link):
                    need(dve, m_full, b, 1)
                    m3 = misc[1][:, 0:NC * E0].rearrange("p (c e) -> p c e", c=NC)
                    rb3 = rb[:].unsqueeze(1).broadcast_to([P, NC, E0])
                    nc.vector.tensor_tensor(lg[:], m3, rb3, ALU.add).then_inc(m_free.sem, 1)
                    need(dve, m_free, b, 1)
                    link(nc.vector.tensor_reduce(lmax[:], lg[:], AX.X, ALU.max))
                    nc.vector.tensor_tensor(lg[:], lg[:], bc(lmax[:], E0), ALU.subtract).then_inc(lg_ok.sem, 1)
                    need(dve, ex_ok, b, 1)
                    link(nc.vector.tensor_reduce(esum[:], ex[:], AX.X, ALU.add))
                    link(nc.vector.reciprocal(einv[:], esum[:]))
                    link(nc.vector.tensor_tensor(prob[:], ex[:], bc(einv[:], E0), ALU.mult))
                    dve.sem_inc(waited.sem, 1)
                    for c in range(NC):
                        last = nc.vector.max(top[:, c, :], prob[:, c, :])
                    link(last)
                    dve.sem_inc(waited.sem, 1)
                    for c in range(NC):
                        last = nc.vector.max_index(tidx[:, c, :], top[:, c, :], prob[:, c, :])
                    link(last)
                    nc.vector.tensor_copy(tidf[:], tidx[:, :, 0:2])
                    link(nc.vector.scalar_tensor_tensor(wsum[:], top[:, :, 0], 1.0, top[:, :, 1], ALU.mult, ALU.add))
                    link(nc.vector.tensor_scalar(wsum[:], wsum[:], 1e-9, None, ALU.add))
                    link(nc.vector.reciprocal(winv[:], wsum[:]))
                    link(nc.vector.tensor_tensor(wt[:], top[:, :, 0:2], bc(winv[:], 2), ALU.mult))
                    io = iota[:, 0:E0].unsqueeze(1).broadcast_to([P, NC, E0])
                    for k in range(2):
                        last = nc.vector.tensor_tensor(eq[:, k], io, bc(tidf[:, :, k], E0), ALU.is_equal)
                    link(last)
                    for k in range(2):
                        last = nc.vector.tensor_tensor(cp[:, k], eq[:, k], bc(wt[:, :, k], E0), ALU.mult)
                    link(last)
                    need(dve, y_free, b, 0)
                    nc.vector.tensor_tensor(combm[:, :, 0:E0], cp[:, 0], cp[:, 1], ALU.add).then_inc(comb_ok.sem, 1)

                def biases(b, k):
                    need(dve, m_full, b, 2 + k)
                    if k == 0:
                        nc.vector.tensor_copy(combT[:], misc[0][0:E0, 0:SP]).then_inc(m_free.sem, 1)
                    if k == 1:
                        need(dve, y_free, b, 2)
                        nc.vector.tensor_tensor(h_all[:, bass.ds(b * SP, SP)], h_all[:, bass.ds(b * SP, SP)], misc[1][:, 0:SP], ALU.add)\
                            .then_inc(m_free.sem, 1)
                        need(dve, m_free, b, 3)

                def add_expert(b, e):
                    if e == 0:
                        need(dve, comb_ok, b, 1)
                    need(dve, y_full, b, e + 1)
                    need(dve, y_free, b, e)
                    for c in range(NC):
                        last = nc.vector.scalar_tensor_tensor(h1(b, c), y_ps[:, c * D:(c + 1) * D], combm[:, c, e:e + 1], h1(b, c),
                                                              ALU.mult, ALU.add)
                    last.then_inc(y_free.sem, 1)

                def retain(b, slot, rlink):
                    if slot == (0, 0):
                        need(dve, y_free, b, E0, waited)
                        token_stats([h1(b, c) for c in range(NC)], st_r, mv_r, rlink)
                        nc.vector.tensor_scalar(ve_r[:], mv_r[:, :, 1], EPS, None, ALU.add).then_inc(rvar_ok.sem, 1)
                    if slot == (1, 0):
                        need(dve, rrstd_ok, b, 1)
                        need(dve, parts_free, b, 0)
                        for c in range(NC):
                            last = nc.vector.tensor_scalar(src_st[:, c * D:(c + 1) * D], h1(b, c), mv_r[:, c, 0:1], rs_r[:, c:c + 1],
                                                           ALU.subtract, ALU.mult)
                        last.then_inc(src_ok.sem, 1)
                    if slot == (2, 0):
                        need(dve, r_full, b, 1)
                        nc.vector.tensor_copy(srcT[:], r_ps[:, 0:SP]).then_inc(r_free.sem, 1)
                    for c in range(NC):
                        if slot == (c + 3, 0):
                            need(dve, r_full, b, c + 2)
                            if c == 0:
                                need(dve, parts_free, b, 0)
                            nc.vector.tensor_tensor(k_st[:, c, :], r_ps[:, 0:D], bkvg[:, 0:D], ALU.add)
                            nc.vector.tensor_tensor(v_st[:, c, 0:D], r_ps[:, D:2 * D], bkvg[:, D:2 * D], ALU.add)
                            nc.vector.tensor_tensor(g_st[:, c, :], r_ps[:, 2 * D:3 * D], bkvg[:, 2 * D:], ALU.add).then_inc(r_free.sem, 1)
                            if c == NC - 1:
                                need(dve, r_free, b, 4)
                                dve.sem_inc(kvg_ok.sem, 1)
                    if slot == (6, 0):
                        need(dve, r_full, b, 5)
                        nc.vector.tensor_scalar(qrT[:, 0:S], r_ps[:, 0:S], bq1[:], None, ALU.add)
                        rlink(nc.vector.tensor_copy(ksum[:], r_ps[:, S + D:S + D + 1]))
                        nc.vector.tensor_tensor(kv_st[:, 0:D], r_ps[:, S:S + D], bd[:], ALU.mult)
                        nc.vector.tensor_scalar(kv_st[:, D:], bd8[:], ksum[:], None, ALU.mult).then_inc(r_free.sem, 1)
                    if slot == (7, 0):
                        need(dve, r_full, b, 6)
                        need(dve, parts_free, b, 0)
                        nc.vector.tensor_copy(o_st[:], r_ps[:, 0:NC * OW]).then_inc(r_free.sem, 1)
                        need(dve, r_free, b, 6)
                        dve.sem_inc(o_ok.sem, 1)

                def step(moe, att, fro, ret):
                    link, flink, mlink, rlink = Chain(dve, a_chain, att), Chain(dve, f_chain, fro), Chain(dve, m_chain, moe), Chain(dve, r_chain, ret)
                    for e in range(E0):
                        for k in range(2):
                            if k == 1 and moe is not None and e:
                                add_expert(moe, e - 1)
                            if ret is not None:
                                retain(ret, (e, k), rlink)
                            if moe is not None:
                                if (e, k) == (0, 1):
                                    route(moe, mlink)
                                if (e, k) in ((2, 0), (2, 1)):
                                    biases(moe, k)
                            if att is not None:
                                attend(att, (e, k), link)
                            if fro is not None:
                                front(fro, (e, k), flink)
                    if moe is not None:
                        add_expert(moe, E0 - 1)
                        mlink.end(m_chain.per)
                    if att is not None:
                        link.end(a_chain.per)
                    if fro is not None:
                        flink.end(f_chain.per)
                    if ret is not None:
                        rlink.end(r_chain.per)

                step(None, None, 0, None)
                step(None, 0, 1, None)
                step(0, 1, 2, None)
                with dve.Fori(0, B - 3) as b:
                    step(b + 1, b + 2, b + 3, b)
                step(B - 2, B - 1, None, B - 3)
                step(B - 1, None, None, B - 2)
                step(None, None, None, B - 1)
                dve.wait_ge(y_free.sem, y_free.at(B, 0))
                dve.wait_ge(w_moe.sem, 16 * 4)

        if stop == "l0":
            fin = signal("fin")
            with nc.Block() as block:
                @block.sync
                def _(sp):
                    for b in range(B):
                        for c in range(NC):
                            sp.dma_start(out[b, c * P:c * P + ROWS[c], :], h_all[0:ROWS[c], b * SP + c * P:b * SP + (c + 1) * P]).then_inc(fin.sem, 16)
                    sp.wait_ge(fin.sem, 16 * B * NC)
            return

        with ExitStack() as l1:
            def sb1(name, shape, dt=FP32):
                return l1.enter_context(nc.sbuf_tensor(name, shape, dt))

            wgu = sb1("wgu", [P, E1 + 1, 2 * F1])
            wdn = sb1("wdn", [P, E1 + 1, D])
            lnb_w = sb1("lnb_w", [P, FC, P])
            o_in = sb1("o_in", [P, NC * OW]); g_in = sb1("g_in", [P, SP]); src_in = sb1("src_in", [P, SP])
            qk_sum = sb1("qk_sum", [P, NC, NH]); qk_abs = sb1("qk_abs", [P, NC, NH]); den = sb1("den", [P, NC, NH]); rden = sb1("rden", [P, NC, NH])
            og = sb1("og", [P, NC, NH, HD]); sq = sb1("sq", [P, NC, NH, HD])
            gsum = sb1("gsum", [P, NC, NH]); gmean = sb1("gmean", [P, NC, NH]); gss = sb1("gss", [P, NC, NH])
            gve = sb1("gve", [P, NC, NH]); grs = sb1("grs", [P, NC, NH])
            sg = sb1("sg", [P, SP]); oT = sb1("oT", [P, SP])
            x_pre = sb1("x_pre", [P, NC, D]); x1 = sb1("x1", [P, NC, D]); x1T = sb1("x1T", [P, S])
            ff = sb1("ff", [P, FC, SP]); ffsq = sb1("ffsq", [P, FC, SP])
            fmean = sb1("fmean", [P, NC]); fms = sb1("fms", [P, NC]); fm2 = sb1("fm2", [P, NC]); fvar = sb1("fvar", [P, NC])
            fve = sb1("fve", [P, NC]); frs = sb1("frs", [P, NC]); fnm = sb1("fnm", [P, NC])
            z = sb1("z", [P, NC, D]); x2 = sb1("x2", [P, NC, D]); x3 = sb1("x3", [P, NC, D])
            aff = sb1("aff", [P, NC, E1]); rscore = sb1("rscore", [P, NC, E1])
            top3 = sb1("top3", [P, NC, 8]); idx3 = sb1("idx3", [P, NC, 8], U32); idf3 = sb1("idf3", [P, NC, 3])
            eq3 = sb1("eq3", [P, 3, NC, E1]); sel = sb1("sel", [P, NC, E1])
            asum = sb1("asum", [P, NC]); ainv = sb1("ainv", [P, NC])
            ast = sb1("ast", [P, NC, 6]); amv = sb1("amv", [P, NC, 2]); ave = sb1("ave", [P, NC]); ars = sb1("ars", [P, NC])
            gate = sb1("gate", [P, 2, S]); hid1 = sb1("hid1", [P, 2, SP])

            head_full, head_free = signal("head_full", NC), signal("head_free", NC)
            w_moe1, o_here, g_here, src_here = signal("w_moe1"), signal("o_here", 16), signal("g_here", 16), signal("src_here", 16)
            o_used, g_used, src_used = signal("o_used"), signal("g_used"), signal("src_used")
            og_ctr, sq_ok, gve_ok, grs_ok, silu_ok, og_ok = (signal(n) for n in ("og_ctr", "sq_ok", "gve_ok", "grs_ok", "silu_ok", "og_ok"))
            oT_full, oT_ok, wo_full, wo_read = (signal(n) for n in ("oT_full", "oT_ok", "wo_full", "wo_read"))
            avar_ok, arstd_ok, xpre_ok, x1g, x1_ok = (signal(n) for n in ("avar_ok", "arstd_ok", "xpre_ok", "x1g", "x1_ok"))
            x1T_full, x1T_ok, fc1_full = signal("x1T_full"), signal("x1T_ok"), signal("fc1_full", FC)
            ff_ok, ffsq_ok = signal("ff_ok", FC), signal("ffsq_ok")
            fc2_full, fc2_read = signal("fc2_full"), signal("fc2_read")
            cvar_ok, crstd_ok = signal("cvar_ok", 3), signal("crstd_ok", 3)
            x2_ok, x3g, x3_ok, xn4_ok = signal("x2_ok"), signal("x3g"), signal("x3_ok"), signal("xn4_ok")
            xT_full, xT_ok, rt_full, rt_read = (signal(n) for n in ("xT_full", "xT_ok", "rt_full", "rt_read"))
            lin_ok, aff_ok = signal("lin_ok"), signal("aff_ok")
            a_link, b_link, h_link = signal("a_link", 10), signal("b_link", 22), signal("h_link", 1)
            gu_full, gate_ok = signal("gu_full", E1 + 1, 0), signal("gate_ok", E1 + 1, 2)
            hid1_ok = signal("hid1_ok", E1 + 1, 2)
            z_full, z_free = signal("z_full", E1 + 1, 2), signal("z_free", E1 + 1, 2)
            out_ok = signal("out_ok", 16)
            gu_ps, z_ps = banks[2:6], banks[6:8]
            NE = E1 + 1

            def back(e):
                return max(e - 1, 0)

            block = l1.enter_context(nc.Block())

            @block.sync
            def _(sp):
                sp.dma_start(wgu[:], t["wgu"]).then_inc(w_moe1.sem, 16)
                sp.dma_start(wdn[:], t["wdn"]).then_inc(w_moe1.sem, 16)

                def load(b):
                    need(sp, o_used, b, 0)
                    sp.dma_start(o_in[:], row(o_d, b)).then_inc(o_here.sem, 16)
                    need(sp, g_used, b, 0)
                    sp.dma_start(g_in[:], row(g_d, b)).then_inc(g_here.sem, 16)
                    need(sp, src_used, b, 0)
                    sp.dma_start(src_in[:], row(src_d, b)).then_inc(src_here.sem, 16)

                def store(b):
                    need(sp, z_free, b, NE)
                    for c in range(NC):
                        dst = out[bass.ds(b, 1), c * P:c * P + ROWS[c], :].rearrange("a s d -> (a s) d")
                        sp.dma_start(dst, h_all[0:ROWS[c], bass.ds(b * SP + c * P, P)]).then_inc(out_ok.sem, 16)

                load(0)
                load(1)
                with sp.Fori(0, B - 2) as b:
                    load(b + 2)
                    store(b)
                store(B - 2)
                store(B - 1)
                sp.wait_ge(out_ok.sem, 16 * NC * B)

            @block.gpsimd
            def _(pool):
                def root(x, y, sig_in, sig_out, b, k):
                    need(pool, sig_in, b, k)
                    nc.gpsimd.tensor_tensor(y[:], x[:], neghalf[:, 0:NC], ALU.pow).then_inc(sig_out.sem, 1)

                def gain(b, x, y, g_, b_, sig_in, sig_mid, sig_out):
                    need(pool, sig_in, b, 1)
                    nc.gpsimd.tensor_tensor(y[:], x[:], g_[:].unsqueeze(1).broadcast_to([P, NC, D]), ALU.mult).then_inc(sig_mid.sem, 1)
                    need(pool, sig_mid, b, 1)
                    nc.gpsimd.tensor_tensor(y[:], y[:], b_[:].unsqueeze(1).broadcast_to([P, NC, D]), ALU.add).then_inc(sig_out.sem, 1)

                def step(two, one):
                    if two is not None:
                        root(cve, crs, cvar_ok, crstd_ok, two, 1)
                        root(cve, crs, cvar_ok, crstd_ok, two, 2)
                    if one is not None:
                        need(pool, gve_ok, one, 1)
                        nc.gpsimd.tensor_tensor(grs[:].rearrange("p c h -> p (c h)"), gve[:].rearrange("p c h -> p (c h)"), neghalf[:], ALU.pow)\
                            .then_inc(grs_ok.sem, 1)
                    if two is not None:
                        gain(two, x2, x3, n1g, n1b, x2_ok, x3g, x3_ok)
                        root(cve, crs, cvar_ok, crstd_ok, two, 3)
                    if one is not None:
                        root(ave, ars, avar_ok, arstd_ok, one, 1)
                        gain(one, x_pre, x1, n0g, n0b, xpre_ok, x1g, x1_ok)

                step(None, 0)
                with pool.Fori(0, B - 1) as b:
                    step(b, b + 1)
                step(B - 1, None)

            @block.tensor
            def _(pe):
                pe.sem_inc(z_full.sem, z_full.start)
                pe.wait_ge(setup_v.sem, 1)
                for f in range(FC):
                    nc.tensor.matmul(banks[6][:, 0:D], ones[:], fc2g[:, f, 0:D], start=(f == 0), stop=(f == FC - 1))
                for f in range(FC):
                    nc.tensor.matmul(banks[7][:, 0:D], lnb_w[:, f, :], fc2[:, f, :], start=(f == 0), stop=False)
                nc.tensor.matmul(banks[7][:, 0:D], ones[0:1, :], fc2b[:], start=False, stop=True).then_inc(setup_pe.sem, 1)
                pe.wait_ge(dec_in.sem, 16)
                for h in range(NH):
                    for ic in range(NC):
                        if h >= 2:
                            need(pe, head_free, h, ic + 1 - 2 * NC)
                        bank = banks[3 * (h % 2) + ic]
                        for jc in range(ic + 1):
                            last = nc.tensor.matmul(bank[0:ROWS[ic], 0:B * HD], decay[0:ROWS[jc], h, jc, ic * P:ic * P + ROWS[ic]],
                                                    v_all[0:ROWS[jc], :].rearrange("p (b c d) -> p b c d", b=B, c=NC)[:, :, jc, h * HD:(h + 1) * HD],
                                                    start=(jc == 0), stop=(jc == ic))
                        last.then_inc(head_full.sem, 1)
                pe.wait_ge(head_free.sem, NH * NC)

                def first_part(b, slot):
                    if slot == 5:
                        need(pe, og_ok, b, 1)
                        need(pe, ff_ok, b, 0)
                        for c in range(NC):
                            last = nc.tensor.transpose(banks[0][:, c * P:(c + 1) * P], og[:, c].rearrange("p h d -> p (h d)"), ident[:])
                        last.then_inc(oT_full.sem, 1)
                    if slot == 7:
                        need(pe, oT_ok, b, 1)
                        for c in range(NC):
                            nc.tensor.matmul(banks[0][:, c * D:(c + 1) * D], oT[:, c * P:(c + 1) * P], wo[:], start=True, stop=False)
                            last = nc.tensor.matmul(banks[0][:, c * D:(c + 1) * D], ones[0:1, :], bo[:], start=False, stop=True)
                        last.then_inc(wo_full.sem, 1)
                    if slot == 12:
                        need(pe, x1_ok, b, 1)
                        need(pe, wo_read, b, 1)
                        for c in range(NC):
                            last = nc.tensor.transpose(banks[0][:, c * P:(c + 1) * P], x1[:, c, :], ident[:])
                        last.then_inc(x1T_full.sem, 1)

                def feed_forward(b, k):
                    if k == 0:
                        need(pe, x1T_ok, b, 1)
                        need(pe, rt_read, b, 0)
                    for f in (2 * k, 2 * k + 1):
                        if k:
                            need(pe, ff_ok, b, f - 1)
                        nc.tensor.matmul(banks[f % 2][:, 0:S], fc1[:, f * P:(f + 1) * P], x1T[:], start=True, stop=True).then_inc(fc1_full.sem, 1)

                def second_part(b, slot):
                    if slot == 0:
                        need(pe, ffsq_ok, b, 1)
                        m = banks[1]
                        for c in range(NC):
                            o0 = c * (D + 2)
                            for f in range(FC):
                                nc.tensor.matmul(m[:, o0:o0 + D + 1], ff[:, f, c * P:(c + 1) * P], fc2g[:, f, :], start=(f == 0), stop=(f == FC - 1))
                            for f in range(FC):
                                last = nc.tensor.matmul(m[:, o0 + D + 1:o0 + D + 2], ffsq[:, f, c * P:(c + 1) * P], ones[:, 0:1],
                                                        start=(f == 0), stop=(f == FC - 1))
                        last.then_inc(fc2_full.sem, 1)
                    if slot == 9:
                        need(pe, xn4_ok, b, 1)
                        need(pe, fc2_read, b, 1)
                        for c in range(NC):
                            last = nc.tensor.transpose(banks[1][:, c * P:(c + 1) * P], xn[:, c * D:(c + 1) * D], ident[:])
                        last.then_inc(xT_full.sem, 1)
                    if slot == 11:
                        need(pe, xT_ok, b, 1)
                        for c in range(NC):
                            last = nc.tensor.matmul(banks[1][:, c * E1:(c + 1) * E1], xT[:, c * P:(c + 1) * P], gw[:], start=True, stop=True)
                        last.then_inc(rt_full.sem, 1)

                def up(b, e):
                    if e == 0:
                        need(pe, lin_ok, b, 1)
                    need(pe, hid1_ok, b, back(e))
                    for k in range(2):
                        last = nc.tensor.matmul(gu_ps[2 * (e % 2) + k][:, 0:S], wgu[:, e, k * F1:(k + 1) * F1], xTm[:, 0:S], start=True, stop=True)
                    last.then_inc(gu_full.sem, 1)

                def down(b, e):
                    need(pe, hid1_ok, b, e + 1)
                    need(pe, z_free, b, back(e))
                    for c in range(NC):
                        last = nc.tensor.matmul(z_ps[e % 2][:, c * D:(c + 1) * D], hid1[:, e % 2, c * P:(c + 1) * P], wdn[:, e, :], start=True, stop=True)
                    last.then_inc(z_full.sem, 1)

                def step(moe, two, one):
                    for e in range(NE):
                        if moe is not None:
                            up(moe, e)
                        if two is not None:
                            second_part(two, e)
                        if one is not None:
                            first_part(one, e)
                            if e == 14:
                                feed_forward(one, 0)
                        if moe is not None and e:
                            down(moe, e - 1)
                        if one is not None and e == 14:
                            feed_forward(one, 1)
                    if moe is not None:
                        down(moe, NE - 1)

                step(None, None, 0)
                step(None, 0, 1)
                pe.wait_ge(w_moe1.sem, 32)
                with pe.Fori(0, B - 2) as b:
                    step(b, b + 1, b + 2)
                step(B - 2, B - 1, None)
                step(B - 1, None, None)

            @block.scalar
            def _(act):
                act.sem_inc(gate_ok.sem, gate_ok.start)

                def first_part(b, slot):
                    if slot == 0:
                        need(act, g_here, b, 16)
                        need(act, og_ok, b, 0)
                        nc.scalar.activation(sg[:], g_in[:], ACT.Silu).then_inc(silu_ok.sem, 1)
                    if slot == 1:
                        need(act, og_ctr, b, 1)
                        nc.scalar.activation(sq[:], og[:], ACT.Square).then_inc(sq_ok.sem, 1)
                    if slot == 6:
                        need(act, oT_full, b, 1)
                        nc.scalar.activation(oT[:], banks[0][:, 0:SP], ACT.Copy).then_inc(oT_ok.sem, 1)
                    if slot == 13:
                        need(act, x1T_full, b, 1)
                        nc.scalar.activation(x1T[:], banks[0][:, 0:S], ACT.Copy).then_inc(x1T_ok.sem, 1)
                    if slot == 14:
                        for f in range(FC):
                            need(act, fc1_full, b, f + 1)
                            nc.scalar.activation(ff[:, f, 0:S], banks[f % 2][:, 0:S], ACT.Gelu, bias=fc1b[:, f:f + 1]).then_inc(ff_ok.sem, 1)
                    if slot == 15:
                        need(act, ff_ok, b, FC)
                        nc.scalar.activation(ffsq[:, :, 0:S], ff[:, :, 0:S], ACT.Square).then_inc(ffsq_ok.sem, 1)

                def second_part(b, slot):
                    if slot == 10:
                        need(act, xT_full, b, 1)
                        need(act, lin_ok, b, 0)
                        nc.scalar.activation(xT[:], banks[1][:, 0:SP], ACT.Copy).then_inc(xT_ok.sem, 1)
                    if slot == 12:
                        need(act, rt_full, b, 1)
                        nc.scalar.activation(aff[:], banks[1][:, 0:NC * E1].rearrange("p (c e) -> p c e", c=NC), ACT.Sigmoid).then_inc(aff_ok.sem, 1)
                        need(act, aff_ok, b, 1)
                        act.sem_inc(rt_read.sem, 1)

                def silu(b, e):
                    need(act, gu_full, b, e + 1)
                    need(act, hid1_ok, b, back(e))
                    nc.scalar.activation(gate[:, e % 2, :], gu_ps[2 * (e % 2)][:, 0:S], ACT.Silu).then_inc(gate_ok.sem, 1)

                def step(moe, two, one):
                    for e in range(NE):
                        if moe is not None:
                            silu(moe, e)
                        if two is not None:
                            second_part(two, e)
                        if one is not None:
                            first_part(one, e)

                step(None, None, 0)
                step(None, 0, 1)
                with act.Fori(0, B - 2) as b:
                    step(b, b + 1, b + 2)
                step(B - 2, B - 1, None)
                step(B - 1, None, None)

            @block.vector
            def _(dve):
                dve.sem_inc(hid1_ok.sem, hid1_ok.start)
                dve.sem_inc(z_free.sem, z_free.start)
                dve.wait_ge(w_l1.sem, 16 * 23)
                nc.vector.memset(hid1[:], 0.0)
                nc.vector.memset(ff[:], 0.0)
                nc.vector.memset(ffsq[:], 0.0)
                for f in range(FC):
                    nc.vector.tensor_scalar(fc2g[:, f, 0:D], fc2[:, f, :], lng[:, f:f + 1], None, ALU.mult)
                    nc.vector.tensor_scalar(lnb_w[:, f, :], ones[:], lnb[:, f:f + 1], None, ALU.mult)
                nc.vector.memset(fc2g[:, :, D:], 1.0).then_inc(setup_v.sem, 1)
                dve.wait_ge(setup_pe.sem, 1)
                nc.vector.tensor_copy(c1[:], banks[6][:, 0:D])
                nc.vector.tensor_copy(c2[:], banks[7][:, 0:D]).then_inc(setup_v.sem, 1)
                for h in range(NH):
                    for ic in range(NC):
                        need(dve, head_full, h, ic + 1)
                        if ic == 0:
                            need(dve, head_full, h, NC)
                        dst = v_all[0:ROWS[ic], :].rearrange("p (b c d) -> p b c d", b=B, c=NC)[:, :, ic, h * HD:(h + 1) * HD]
                        nc.vector.tensor_copy(dst, banks[3 * (h % 2) + ic][0:ROWS[ic], 0:B * HD].rearrange("p (b d) -> p b d", b=B))\
                            .then_inc(head_free.sem, 1)
                dve.wait_ge(head_free.sem, NH * NC)
                dve.wait_ge(setup_v.sem, 2)

                def bc(x, n):
                    return x.unsqueeze(2).broadcast_to([P, NC, n])

                def per_head(x):
                    return x[:].rearrange("p c h -> p (c h)").unsqueeze(2).broadcast_to([P, NC * NH, HD])

                def flat(x):
                    return x[:].rearrange("p c h d -> p (c h) d")

                def normalise(x, y, mean, rstd):
                    for c in range(NC):
                        last = nc.vector.tensor_scalar(y[c], x[c], mean[:, c, 0:1], rstd[:, c:c + 1], ALU.subtract, ALU.mult)
                    return last

                def first_part(b, slot, link):
                    xs = [x_pre[:, c, :] for c in range(NC)]
                    og_flat = og[:].rearrange("p c h d -> p (c h d)")
                    if slot == 0:
                        need(dve, o_here, b, 16)
                        o3 = o_in[:].rearrange("p (c n) -> p c n", c=NC)
                        link(nc.vector.tensor_tensor(qk_sum[:], o3[:, :, D:], dsum[:], ALU.add))
                        link(nc.vector.scalar_tensor_tensor(qk_abs[:], qk_sum[:], -1.0, qk_sum[:], ALU.mult, ALU.max))
                        link(nc.vector.tensor_scalar(den[:], qk_abs[:], 1.0, None, ALU.max))
                        nc.vector.reciprocal(rden[:], den[:])
                        need(dve, oT_full, b, 0)
                        nc.vector.tensor_tensor(og[:].rearrange("p c h d -> p c (h d)"), o3[:, :, 0:D],
                                                v_all[:, bass.ds(b * SP, SP)].rearrange("p (c d) -> p c d", c=NC), ALU.add)\
                            .then_inc(o_used.sem, 1)
                        need(dve, o_used, b, 1)
                        link(nc.vector.tensor_tensor(flat(og), flat(og), per_head(rden), ALU.mult))
                        link(nc.vector.tensor_reduce(gsum[:].rearrange("p c h -> p (c h)"), flat(og), AX.X, ALU.add))
                        link(nc.vector.tensor_scalar(gmean[:], gsum[:], 1.0 / HD, None, ALU.mult))
                        nc.vector.tensor_tensor(flat(og), flat(og), per_head(gmean), ALU.subtract).then_inc(og_ctr.sem, 1)
                    if slot == 2:
                        need(dve, sq_ok, b, 1)
                        link(nc.vector.tensor_reduce(gss[:].rearrange("p c h -> p (c h)"), flat(sq), AX.X, ALU.add))
                        nc.vector.tensor_scalar(gve[:], gss[:], 1.0 / HD, 1e-6, ALU.mult, ALU.add).then_inc(gve_ok.sem, 1)
                    if slot == 4:
                        need(dve, grs_ok, b, 1)
                        link(nc.vector.tensor_tensor(flat(og), flat(og), per_head(grs), ALU.mult))
                        need(dve, silu_ok, b, 1)
                        nc.vector.tensor_tensor(og_flat, og_flat, sg[:], ALU.mult).then_inc(og_ok.sem, 1)
                        need(dve, og_ok, b, 1)
                        dve.sem_inc(g_used.sem, 1)
                    if slot == 8:
                        need(dve, wo_full, b, 1)
                        need(dve, src_here, b, 16)
                        nc.vector.tensor_tensor(x_pre[:].rearrange("p c d -> p (c d)"), banks[0][:, 0:SP], src_in[:], ALU.add).then_inc(wo_read.sem, 1)
                        need(dve, wo_read, b, 1, waited)
                        dve.sem_inc(src_used.sem, 1)
                        token_stats(xs, ast, amv, link)
                        nc.vector.tensor_scalar(ave[:], amv[:, :, 1], EPS, None, ALU.add).then_inc(avar_ok.sem, 1)
                    if slot == 10:
                        need(dve, arstd_ok, b, 1)
                        normalise(xs, xs, amv, ars).then_inc(xpre_ok.sem, 1)

                def second_part(b, slot, link):
                    m3 = banks[1][:, 0:NC * (D + 2)].rearrange("p (c n) -> p c n", c=NC)
                    xs = [x2[:, c, :] for c in range(NC)]
                    hs = [h1(b, c) for c in range(NC)]
                    if slot == 0:
                        need(dve, fc2_full, b, 1)
                        nc.vector.tensor_scalar(fmean[:], m3[:, :, D], 1.0 / FF, None, ALU.mult)
                        link(nc.vector.tensor_scalar(fms[:], m3[:, :, D + 1], 1.0 / FF, None, ALU.mult))
                        link(nc.vector.tensor_tensor(fm2[:], fmean[:], fmean[:], ALU.mult))
                        link(nc.vector.tensor_tensor(fvar[:], fms[:], fm2[:], ALU.subtract))
                        nc.vector.tensor_scalar(cve[:], fvar[:], 0.0, 1e-6, ALU.max, ALU.add).then_inc(cvar_ok.sem, 1)
                    if slot == 1:
                        need(dve, crstd_ok, b, 1)
                        link(nc.vector.scalar_tensor_tensor(fnm[:], fmean[:], -1.0, crs[:], ALU.mult, ALU.mult))
                        for c in range(NC):
                            last = nc.vector.scalar_tensor_tensor(z[:, c, :], c1[:], fnm[:, c:c + 1], c2[:], ALU.mult, ALU.add)
                        link(last)
                        for c in range(NC):
                            last = nc.vector.scalar_tensor_tensor(z[:, c, :], m3[:, c, 0:D], crs[:, c:c + 1], z[:, c, :], ALU.mult, ALU.add)
                        last.then_inc(fc2_read.sem, 1)
                        need(dve, fc2_read, b, 1)
                        link(nc.vector.tensor_tensor(x2[:], z[:], x1[:], ALU.add))
                        token_stats(xs, cst, cmv, link)
                        nc.vector.tensor_scalar(cve[:], cmv[:, :, 1], EPS, None, ALU.add).then_inc(cvar_ok.sem, 1)
                    if slot == 2:
                        need(dve, crstd_ok, b, 2)
                        normalise(xs, xs, cmv, crs).then_inc(x2_ok.sem, 1)
                    if slot == 6:
                        need(dve, x3_ok, b, 1)
                        hb = h_all[:, bass.ds(b * SP, SP)]
                        link(nc.vector.tensor_tensor(hb, hb, x3[:].rearrange("p c d -> p (c d)"), ALU.add))
                        token_stats(hs, cst, cmv, link)
                        nc.vector.tensor_scalar(cve[:], cmv[:, :, 1], EPS, None, ALU.add).then_inc(cvar_ok.sem, 1)
                    if slot == 8:
                        need(dve, crstd_ok, b, 3)
                        normalise(hs, [xn[:, c * D:(c + 1) * D] for c in range(NC)], cmv, crs).then_inc(xn4_ok.sem, 1)
                    if slot == 13:
                        need(dve, aff_ok, b, 1)
                        link(nc.vector.tensor_tensor(rscore[:], aff[:], eb[:].unsqueeze(1).broadcast_to([P, NC, E1]), ALU.add))
                        dve.sem_inc(waited.sem, 1)
                        for c in range(NC):
                            last = nc.vector.max(top3[:, c, :], rscore[:, c, :])
                        link(last)
                        dve.sem_inc(waited.sem, 1)
                        for c in range(NC):
                            last = nc.vector.max_index(idx3[:, c, :], top3[:, c, :], rscore[:, c, :])
                        link(last)
                        link(nc.vector.tensor_copy(idf3[:], idx3[:, :, 0:3]))
                    if slot == 14:
                        io = iota[:].unsqueeze(1).broadcast_to([P, NC, E1])
                        for k in range(3):
                            last = nc.vector.tensor_tensor(eq3[:, k], io, bc(idf3[:, :, k], E1), ALU.is_equal)
                        link(last)
                        link(nc.vector.tensor_tensor(sel[:], eq3[:, 0], eq3[:, 1], ALU.add))
                        link(nc.vector.tensor_tensor(sel[:], sel[:], eq3[:, 2], ALU.add))
                        link(nc.vector.tensor_tensor(sel[:], sel[:], aff[:], ALU.mult))
                    if slot == 15:
                        link(nc.vector.tensor_reduce(asum[:], sel[:], AX.X, ALU.add))
                        link(nc.vector.tensor_scalar(asum[:], asum[:], 1e-9, None, ALU.add))
                        link(nc.vector.reciprocal(ainv[:], asum[:]))

                def hidden(b, e):
                    need(dve, gate_ok, b, e + 1)
                    need(dve, z_full, b, back(e))
                    nc.vector.tensor_tensor(hid1[:, e % 2, 0:S], gate[:, e % 2, :], gu_ps[2 * (e % 2) + 1][:, 0:S], ALU.mult)\
                        .then_inc(hid1_ok.sem, 1)

                def add_expert(b, e):
                    need(dve, z_full, b, e + 1)
                    need(dve, z_free, b, e)
                    if e == 0:
                        hb = h_all[:, bass.ds(b * SP, SP)]
                        nc.vector.tensor_tensor(hb, hb, z_ps[0][:, 0:SP], ALU.add).then_inc(z_free.sem, 1)
                        return
                    for c in range(NC):
                        last = nc.vector.scalar_tensor_tensor(h1(b, c), z_ps[e % 2][:, c * D:(c + 1) * D], combm[:, c, e - 1:e], h1(b, c),
                                                              ALU.mult, ALU.add)
                    last.then_inc(z_free.sem, 1)

                def step(moe, two, one):
                    alink, blink, hlink = Chain(dve, a_link, one), Chain(dve, b_link, two), Chain(dve, h_link, two)
                    for e in range(NE):
                        if moe is not None:
                            hidden(moe, e)
                            if e == NE - 1 and two is not None:
                                need(dve, gu_full, moe, NE)
                        if e == NE - 1 and two is not None:
                            need(dve, xT_ok, two, 1)
                            nc.vector.tensor_copy(xTm[:], xT[:]).then_inc(lin_ok.sem, 1)
                        if moe is not None and e >= 2:
                            add_expert(moe, e - 2)
                        if two is not None:
                            second_part(two, e, blink)
                        if one is not None:
                            first_part(one, e, alink)
                    if moe is not None:
                        add_expert(moe, NE - 2)
                        add_expert(moe, NE - 1)
                    if two is not None:
                        need(dve, z_free, two, 0)
                        hlink(nc.vector.tensor_tensor(combm[:], sel[:], bc(ainv[:], E1), ALU.mult))
                        blink.end(b_link.per)
                    if one is not None:
                        alink.end(a_link.per)

                step(None, None, 0)
                step(None, 0, 1)
                with dve.Fori(0, B - 2) as b:
                    step(b, b + 1, b + 2)
                step(B - 2, B - 1, None)
                step(B - 1, None, None)


def decay_matrices():
    i = np.arange(S)
    diff = (i[:, None] - i[None, :]).astype(np.float64)
    dec = np.log(1.0 - 2.0 ** (-5.0 - np.arange(NH)))
    dm = np.where(diff[None] >= 0, np.exp(np.maximum(diff[None], 0) * dec[:, None, None]), 0.0)
    dm = (dm / np.sqrt(dm.sum(-1, keepdims=True))).astype(np.float32)
    dT = np.zeros((P, NH, NC, S), np.float32)
    sums = np.zeros((P, NC, NH), np.float32)
    for c in range(NC):
        dT[:ROWS[c], :, c, :] = dm[:, :, c * P:c * P + ROWS[c]].transpose(2, 0, 1)
        sums[:ROWS[c], c, :] = dm.sum(-1)[:, c * P:c * P + ROWS[c]].T
    return dT, sums


def kernel(**inputs):
    import concourse.bacc as _bacc
    from concourse.bass_utils import run_bass_kernel_spmd as _run

    x = {k: np.asarray(v) for k, v in inputs.items()}
    a = {}
    for k in ("txt", "L0_tok_b", "L0_tok_token", "L0_tok_pos", "L0_attn_b2", "L0_ffn_router_w", "L0_ffn_router_b", "L0_ffn_b2",
              "L1_attn_bk", "L1_attn_bv", "L1_attn_bg", "L1_attn_n0_g", "L1_attn_n0_b", "L1_attn_n1_g", "L1_attn_n1_b", "L1_ffn_expert_bias"):
        a[k] = x[k]
    px = x["x"].reshape(B, 3, N_PATCH, 14, N_PATCH, 14).transpose(0, 1, 3, 5, 2, 4).reshape(B, 588, S_IMG - 1)
    px = np.pad(px, ((0, 0), (0, KT * KR - 588), (1, 0)))
    a["patches"] = px.reshape(B, KT, KR, S_IMG).transpose(0, 2, 1, 3)
    a["tokw"] = np.pad(x["L0_tok_W"].T, ((0, KT * KR - 588), (0, 0))).reshape(KT, KR, D).transpose(1, 0, 2)
    a["wqkv0"] = np.stack([x["L0_attn_Wq"].T, x["L0_attn_Wk"].T, x["L0_attn_Wv"].T], 1)
    a["w1q"] = x["L0_attn_W1"][:, :D].T
    a["w1k"] = x["L0_attn_W1"][:, D:].T
    a["b1a"] = x["L0_attn_b1"].reshape(AH, 1)
    a["w2a"] = x["L0_attn_W2"].reshape(AH, 1)
    a["w1e"] = x["L0_ffn_W1"].transpose(1, 0, 2)
    a["b1e"] = x["L0_ffn_b1"].reshape(E0 * FC, P).T
    a["w2e"] = x["L0_ffn_W2"].reshape(E0, FC, P, D).transpose(2, 0, 1, 3)
    a["wkvg"] = np.concatenate([x["L1_attn_wk"].T, x["L1_attn_wv"].T, x["L1_attn_wg"].T], 1)
    a["wq1"] = x["L1_attn_wq"].T
    a["bq1"] = x["L1_attn_bq"].reshape(D, 1)
    same = np.arange(D)[:, None] // HD == np.arange(D)[None, :] // HD
    a["bd"] = np.where(same, np.float32(HD ** -0.5), np.float32(0))
    a["bd8"] = a["bd"][:, ::HD]
    a["decay"], a["dsum"] = decay_matrices()
    a["wo"] = x["L1_attn_wo"].T
    a["bo"] = x["L1_attn_bo"].reshape(1, D)
    a["fc1"] = x["L1_attn_fc1_w"].T
    a["fc1b"] = x["L1_attn_fc1_b"].reshape(FC, P).T
    a["fc2"] = x["L1_attn_fc2_w"].T.reshape(FC, P, D).transpose(1, 0, 2)
    a["fc2b"] = x["L1_attn_fc2_b"].reshape(1, D)
    a["lng"] = x["L1_attn_ln_ffn_g"].reshape(FC, P).T
    a["lnb"] = x["L1_attn_ln_ffn_b"].reshape(FC, P).T
    a["gw"] = x["L1_ffn_gate_w"].T
    a["wgu"] = np.concatenate([x["L1_ffn_shared_gate_up"][None], x["L1_ffn_expert_gate_up"]]).transpose(2, 0, 1)
    a["wdn"] = np.concatenate([x["L1_ffn_shared_down"][None], x["L1_ffn_expert_down"]]).transpose(2, 0, 1)

    nc = _bacc.Bacc("TRN2", target_bir_lowering=False, num_devices=1)
    arrays, t = {}, {}
    for k, v in a.items():
        v = np.ascontiguousarray(v)
        arrays[f"in_{k}"] = v
        t[k] = nc.dram_tensor(f"in_{k}", v.shape, FP32, kind="ExternalInput").ap()
    out = nc.dram_tensor("out_0", (B, S, D), FP32, kind="ExternalOutput").ap()
    program(nc, t, out, STOP)
    r = _run(nc, [arrays], core_ids=[0])
    return r.results[0]["out_0"]


STOP = None
```

```python
import math
from contextlib import ExitStack

import numpy as np
import concourse.bass as bass
from concourse import mybir

FP32 = mybir.dt.float32
FP32R = mybir.dt.float32r
U32 = mybir.dt.uint32
ALU = mybir.AluOpType
ACT = mybir.ActivationFunctionType
AX = mybir.AxisListType

B = 16
D = 128
N_PATCH, S_IMG, S_TXT = 14, 197, 128
S = S_IMG + S_TXT
P = 128
NC = (S + P - 1) // P
SP = NC * P
LAST = S - (NC - 1) * P
S2 = S + S % 2
ROWS = [P] * (NC - 1) + [LAST]
KT, KR = 5, 118
E0, F0 = 8, 512
FC = F0 // P
E1, F1 = 16, 128
NH, HD = 8, 16
AH = 16
QG = P // AH
NG = (S + QG - 1) // QG
FF = 512
EPS = 1e-5
SCALE = 1.0 / math.sqrt(D)
NTH = 10
SLOTS = {(n // 2, n % 2): (3 * (n - 1), 3 * n) if n < 3 else (6 + 5 * (n - 3), 6 + 5 * (n - 2)) for n in range(1, 10)}


class Signal:

    def __init__(self, sem, per, start=0):
        self.sem, self.per, self.start = sem, per, start

    def at(self, b, k):
        return b * self.per + k + self.start


def need(eng, sig, b, k, alone=None):
    v = sig.at(b, k)
    if not (isinstance(v, int) and v <= 0):
        eng.wait_ge(sig.sem, v)
        if alone is not None:
            eng.sem_inc(alone.sem, 1)


class Chain:

    def __init__(self, eng, sig, b):
        self.eng, self.sig, self.b, self.n = eng, sig, b, 0

    def __call__(self, ins):
        self.n += 1
        ins.then_inc(self.sig.sem, 1)
        self.eng.wait_ge(self.sig.sem, self.sig.at(self.b, self.n))

    def end(self, per):
        assert self.n == per, (self.n, per)
        return per


def program(nc, t, out, stop=None):
    ctx = ExitStack()
    with ctx:
        def sb(name, shape, dt=FP32):
            return ctx.enter_context(nc.sbuf_tensor(name, shape, dt))

        def signal(name, per=1, start=0):
            return Signal(ctx.enter_context(nc.semaphore(name)), per, start)

        h_all = sb("h_all", [P, B * SP])
        OW = D + NH
        v_all = sb("v_all", [P, B * SP])
        src_d = nc.dram_tensor("src_d", (B, P, SP), FP32, kind="Internal").ap()
        g_d = nc.dram_tensor("g_d", (B, P, SP), FP32, kind="Internal").ap()
        o_d = nc.dram_tensor("o_d", (B, P, NC * OW), FP32, kind="Internal").ap()
        src_saved, g_saved, o_saved = signal("src_saved", 16), signal("g_saved", 16), signal("o_saved", 16)
        ident = sb("ident", [P, P])
        ones = sb("ones", [P, P])
        neghalf = sb("neghalf", [P, 24])
        iota = sb("iota", [P, 16])
        w_moe0 = sb("w_moe0", [P, E0 * F0 + E0 * FC * D])
        w1 = w_moe0[:, 0:E0 * F0].rearrange("p (e f) -> p e f", e=E0)
        w2 = w_moe0[:, E0 * F0:].rearrange("p (e c d) -> p e c d", e=E0, c=FC)
        decay = w_moe0[:, 0:NH * NC * S].rearrange("p (h c i) -> p h c i", h=NH, c=NC)
        dsum = sb("dsum", [P, NC, NH])
        wo = sb("wo", [P, D])
        bo = sb("bo", [1, D])
        fc1 = sb("fc1", [P, FF])
        fc1b = sb("fc1b", [P, FC])
        fc2 = sb("fc2", [P, FC, D])
        fc2g = sb("fc2g", [P, FC, D + 1])
        fc2b = sb("fc2b", [1, D])
        lng = sb("lng", [P, FC])
        lnb = sb("lnb", [P, FC])
        c1 = sb("c1", [P, D])
        c2 = sb("c2", [P, D])
        n0g = sb("n0g", [P, D]); n0b = sb("n0b", [P, D])
        n1g = sb("n1g", [P, D]); n1b = sb("n1b", [P, D])
        gw = sb("gw", [P, E1])
        eb = sb("eb", [P, E1])

        xn = sb("xn", [P, SP])
        xT = sb("xT", [P, SP])
        st = sb("st", [P, NC, 6]); mv = sb("mv", [P, NC, 2]); ve = sb("ve", [P, NC]); rs = sb("rs", [P, NC])
        combm = sb("combm", [P, NC, E1])
        cst = sb("cst", [P, NC, 6]); cmv = sb("cmv", [P, NC, 2]); cve = sb("cve", [P, NC]); crs = sb("crs", [P, NC])

        banks = [ctx.enter_context(nc.psum_tensor(f"bank{i}", [P, 512], FP32)) for i in range(8)]
        misc = banks[0:2]

        w_tok, w_att, w_moe, w_l1, txt_in, dec_in = (signal(n) for n in ("w_tok", "w_att", "w_moe", "w_l1", "txt_in", "dec_in"))
        base_in, tok_row_in, consts, ident_step = (signal(n) for n in ("base_in", "tok_row_in", "consts", "ident_step"))
        consts_v, setup_v, setup_pe = signal("consts_v"), signal("setup_v"), signal("setup_pe")
        waited = signal("waited")
        patch_in, patch_used = signal("patch_in", 16), signal("patch_used")

        def h3(b):
            return h_all[:, bass.ds(b * SP, SP)].rearrange("p (c d) -> p c d", c=NC)

        def h1(b, c):
            return h_all[:, bass.ds(b * SP + c * P, P)]

        def row(x, b):
            return x[bass.ds(b, 1)].rearrange("a p n -> (a p) n")

        def token_stats(x, st, mv, link):
            nc.vector.sem_inc(waited.sem, 1)
            for c in range(NC):
                last = nc.vector.bn_stats(st[:, c, :], x[c])
            link(last)
            nc.vector.sem_inc(waited.sem, 1)
            for c in range(NC):
                last = nc.vector.bn_aggr(mv[:, c, :], st[:, c, :])
            link(last)

        with ExitStack() as l0:
            def sb0(name, shape, dt=FP32):
                return l0.enter_context(nc.sbuf_tensor(name, shape, dt))

            b1 = sb0("b1", [P, E0 * FC])
            b2 = sb0("b2", [E0, D])
            rw = sb0("rw", [P, E0])
            rb = sb0("rb", [P, E0])
            tokw = sb0("tokw", [KR, KT, D])
            base = sb0("base", [P, 2, D])
            base_add = sb0("base_add", [P, 2, D])
            wqkv = sb0("wqkv", [P, 3, D])
            w1q = sb0("w1q", [P, QG, P])
            w1k = sb0("w1k", [P, P])
            hb1 = sb0("hb1", [P, 1])
            w2s = sb0("w2s", [P, 24 + QG + 24])
            b2a = sb0("b2a", [P, 1])
            wkvg = sb0("wkvg", [P, 3 * D])
            bkvg = sb0("bkvg", [P, 3 * D])
            wq1 = sb0("wq1", [P, D])
            bq1 = sb0("bq1", [P, 1])
            bd = sb0("bd", [P, D])
            bd8 = sb0("bd8", [P, NH])
            xTm = sb0("xTm", [P, SP])
            combT = sb0("combT", [E0, SP])
            hid = sb0("hid", [P, 2, FC, SP])
            src_st = sb0("src_st", [P, SP]); srcT = sb0("srcT", [P, SP])
            k_st = sb0("k_st", [P, NC, D]); v_st = sb0("v_st", [P, NC, D + 1])
            g_st = sb0("g_st", [P, NC, D]); qrT = sb0("qrT", [P, SP])
            kv_st = sb0("kv_st", [P, OW]); ksum = sb0("ksum", [P, 1])
            patch = sb0("patch", [KR, KT, S_IMG])
            xf = sb0("xf", [P, SP]); xfT = sb0("xfT", [P, SP])
            st_f = sb0("st_f", [P, NC, 6]); mv_f = sb0("mv_f", [P, NC, 2]); ve_f = sb0("ve_f", [P, NC]); rs_f = sb0("rs_f", [P, NC])
            qT = sb0("qT", [P, SP]); qTs = sb0("qTs", [P, SP]); kT = sb0("kT", [P, S])
            v_sb = sb0("v_sb", [P, NC, D])
            hk = sb0("hk", [P, S]); hq = sb0("hq", [P, NG])
            th = sb0("th", [P, NTH, S])
            sc = sb0("sc", [P, NC, S]); smax = sb0("smax", [P, NC]); nmax = sb0("nmax", [P, NC])
            pr = sb0("pr", [P, NC, S]); rsum = sb0("rsum", [P, NC]); rinv = sb0("rinv", [P, NC])
            pT = sb0("pT", [P, NC, SP])
            lg = sb0("lg", [P, NC, E0]); lmax = sb0("lmax", [P, NC]); ex = sb0("ex", [P, NC, E0])
            esum = sb0("esum", [P, NC]); einv = sb0("einv", [P, NC]); prob = sb0("prob", [P, NC, E0])
            top = sb0("top", [P, NC, 8]); tidx = sb0("tidx", [P, NC, 8], U32); tidf = sb0("tidf", [P, NC, 2])
            wsum = sb0("wsum", [P, NC]); winv = sb0("winv", [P, NC]); wt = sb0("wt", [P, NC, 2])
            eq = sb0("eq", [P, 2, NC, E0]); cp = sb0("cp", [P, 2, NC, E0])
            sc_ps, h_ps, y_ps, r_ps = banks[2:4], banks[4:6], banks[6], banks[7]

            misc_full, misc_free = signal("misc_full", 5), signal("misc_free", 5)
            m_full, m_free = signal("m_full", 3), signal("m_free", 3)
            f_full, f_free = signal("f_full", 6), signal("f_free", 6)
            fvar_ok0, frstd_ok, xf_ok = signal("fvar_ok0"), signal("frstd_ok"), signal("xf_ok")
            var_ok, rstd_ok, xn_ok = signal("var_ok"), signal("rstd_ok"), signal("xn_ok")
            hbias_ok, tanh_ok, est_ok = signal("hbias_ok"), signal("tanh_ok", NG), signal("est_ok", NG)
            sc_full, sc_free = signal("sc_full", NC), signal("sc_free", NC)
            nmax_ok, exp_ok = signal("nmax_ok"), signal("exp_ok")
            lg_ok, ex_ok, comb_ok, in_ok = signal("lg_ok"), signal("ex_ok"), signal("comb_ok"), signal("in_ok")
            hid_full, hid_ok = signal("hid_full", E0 * FC), signal("hid_ok", E0 * FC, 2)
            y_full, y_free = signal("y_full", E0, 2), signal("y_free", E0, 1)
            a_chain, f_chain, m_chain = signal("a_chain", 3), signal("f_chain", 2), signal("m_chain", 12)
            l0_done = signal("l0_done")
            r_chain, rvar_ok, rrstd_ok = signal("r_chain", 3), signal("rvar_ok"), signal("rrstd_ok")
            src_ok, v_saved, o_ok = signal("src_ok"), signal("v_saved"), signal("o_ok")
            parts_free = signal("parts_free", 1, 1)
            o_st = sb0("o_st", [P, NC * OW])
            r_full, r_free = signal("r_full", 6), signal("r_free", 6, 1)
            kvg_ok = signal("kvg_ok")
            st_r = sb0("st_r", [P, NC, 6]); mv_r = sb0("mv_r", [P, NC, 2]); ve_r = sb0("ve_r", [P, NC]); rs_r = sb0("rs_r", [P, NC])

            block = l0.enter_context(nc.Block())

            @block.sync
            def _(sp):
                sp.dma_start(tokw[:], t["tokw"]).then_inc(w_tok.sem, 16)
                sp.dma_start(patch[:], t["patches"][0]).then_inc(patch_in.sem, 16)
                sp.dma_start(base[:, 0, :], t["L0_tok_pos"][0:P, :]).then_inc(w_tok.sem, 16)
                sp.dma_start(base[0:S_IMG - P, 1, :], t["L0_tok_pos"][P:S_IMG, :]).then_inc(w_tok.sem, 16)
                sp.dma_start(base_add[:, 0, :], t["L0_tok_b"].partition_broadcast(P)).then_inc(base_in.sem, 16)
                sp.dma_start(base_add[:, 1, :], t["L0_tok_b"].partition_broadcast(P)).then_inc(w_tok.sem, 16)
                sp.wait_ge(base_in.sem, 16)
                sp.dma_start(base_add[0:1, 0, :], t["L0_tok_token"]).then_inc(w_tok.sem, 16)
                sp.wait_ge(consts_v.sem, 1)
                txt, hv = t["txt"], h_all[:, :].rearrange("p (b c d) -> p b c d", b=B, c=NC)
                sp.dma_start(hv[S_IMG - P:P, :, 1, :], txt[:, 0:2 * P - S_IMG, :].rearrange("b s d -> s b d")).then_inc(txt_in.sem, 16)
                sp.dma_start(hv[0:LAST, :, 2, :], txt[:, 2 * P - S_IMG:, :].rearrange("b s d -> s b d")).then_inc(txt_in.sem, 16)
                sp.dma_start(wqkv[:], t["wqkv0"]).then_inc(w_att.sem, 16)
                for dst, src in ((w1q[:], t["w1q"]), (w1k[:], t["w1k"]), (hb1[:], t["b1a"]), (w2s[:], t["w2a"])):
                    sp.dma_start(dst, src).then_inc(w_att.sem, 16)
                sp.dma_start(b2a[:], t["L0_attn_b2"].partition_broadcast(P)).then_inc(w_att.sem, 16)
                sp.dma_start(rw[:], t["L0_ffn_router_w"]).then_inc(w_att.sem, 16)
                sp.dma_start(rb[:], t["L0_ffn_router_b"].partition_broadcast(P)).then_inc(w_att.sem, 16)
                sp.dma_start(w1, t["w1e"]).then_inc(w_moe.sem, 16)
                sp.dma_start(b1[:], t["b1e"]).then_inc(w_moe.sem, 16)
                sp.dma_start(w2, t["w2e"]).then_inc(w_moe.sem, 16)
                sp.dma_start(b2[:], t["L0_ffn_b2"]).then_inc(w_moe.sem, 16)
                for dst, src in ((wkvg[:], t["wkvg"]), (wq1[:], t["wq1"]), (bq1[:], t["bq1"]), (bd[:], t["bd"]), (bd8[:], t["bd8"]),
                                 (dsum[:], t["dsum"]), (wo[:], t["wo"]), (bo[:], t["bo"]), (fc1[:], t["fc1"]), (fc1b[:], t["fc1b"]),
                                 (fc2[:], t["fc2"]), (fc2b[:], t["fc2b"]), (lng[:], t["lng"]), (lnb[:], t["lnb"]),
                                 (bkvg[:, 0:D], t["L1_attn_bk"].partition_broadcast(P)),
                                 (bkvg[:, D:2 * D], t["L1_attn_bv"].partition_broadcast(P)),
                                 (bkvg[:, 2 * D:], t["L1_attn_bg"].partition_broadcast(P)),
                                 (n0g[:], t["L1_attn_n0_g"].partition_broadcast(P)), (n0b[:], t["L1_attn_n0_b"].partition_broadcast(P)),
                                 (n1g[:], t["L1_attn_n1_g"].partition_broadcast(P)), (n1b[:], t["L1_attn_n1_b"].partition_broadcast(P)),
                                 (gw[:], t["gw"]), (eb[:], t["L1_ffn_expert_bias"].partition_broadcast(P)),
                                 ):
                    sp.dma_start(dst, src).then_inc(w_l1.sem, 16)
                with sp.Fori(1, B) as b:
                    sp.wait_ge(patch_used.sem, b)
                    sp.dma_start(patch[:], t["patches"][bass.ds(b, 1)].rearrange("b k c s -> k (b c) s")).then_inc(patch_in.sem, 16)
                sp.wait_ge(w_l1.sem, 16 * 23)
                sp.wait_ge(l0_done.sem, 1)
                sp.dma_start(decay, t["decay"]).then_inc(dec_in.sem, 16)

            @block.gpsimd
            def _(pool):
                nc.gpsimd.memset(neghalf[:], -0.5).then_inc(consts.sem, 1)
                nc.gpsimd.memset(ident[:], 0.0).then_inc(ident_step.sem, 1)
                nc.gpsimd.iota(iota[:], pattern=[[1, 16]], base=0, channel_multiplier=0, allow_small_or_imprecise_dtypes=True)
                pool.wait_ge(ident_step.sem, 1)
                nc.gpsimd.affine_select(out=ident[:], in_=ident[:], compare_op=ALU.not_equal, fill=1.0, base=0,
                                        pattern=[[-1, P]], channel_multiplier=1).then_inc(consts.sem, 1)

                def step(att, front, ret):
                    if ret is not None:
                        need(pool, rvar_ok, ret, 1)
                        nc.gpsimd.tensor_tensor(rs_r[:], ve_r[:], neghalf[:, 0:NC], ALU.pow).then_inc(rrstd_ok.sem, 1)
                        need(pool, src_ok, ret, 1, waited)
                        pool.dma_start(row(src_d, ret), src_st[:]).then_inc(src_saved.sem, 16)
                    if front is not None:
                        need(pool, fvar_ok0, front, 1)
                        nc.gpsimd.tensor_tensor(rs_f[:], ve_f[:], neghalf[:, 0:NC], ALU.pow).then_inc(frstd_ok.sem, 1)
                    if ret is not None:
                        need(pool, kvg_ok, ret, 1, waited)
                        pool.dma_start(row(g_d, ret), g_st[:].rearrange("p c d -> p (c d)")).then_inc(g_saved.sem, 16)
                    if att is not None:
                        need(pool, var_ok, att, 1)
                        nc.gpsimd.tensor_tensor(rs[:], ve[:], neghalf[:, 0:NC], ALU.pow).then_inc(rstd_ok.sem, 1)
                    if ret is not None:
                        nc.gpsimd.tensor_copy(v_all[:, bass.ds(ret * SP, SP)].rearrange("p (c d) -> p c d", c=NC), v_st[:, :, 0:D])\
                            .then_inc(v_saved.sem, 1)
                        need(pool, o_ok, ret, 1, waited)
                        pool.dma_start(row(o_d, ret), o_st[:]).then_inc(o_saved.sem, 16)
                        for sig in (src_saved, g_saved, o_saved):
                            need(pool, sig, ret, 16)
                        need(pool, v_saved, ret, 1, parts_free)

                pool.sem_inc(parts_free.sem, parts_free.start)
                step(None, 0, None)
                step(0, 1, None)
                step(1, 2, None)
                with pool.Fori(0, B - 3) as b:
                    step(b + 2, b + 3, b)
                step(B - 1, None, B - 3)
                step(None, None, B - 2)
                step(None, None, B - 1)
                for sig in (src_saved, g_saved, o_saved):
                    pool.wait_ge(sig.sem, sig.at(B, 0))

            @block.tensor
            def _(pe):
                def claim(b, n):
                    if n == 0:
                        need(pe, misc_free, b, 0)
                        need(pe, m_free, b, 0)
                    else:
                        need(pe, misc_free, b, n - 1)
                    return misc[n % 2]

                def claim_f(b, n):
                    need(pe, f_free, b, n - 1 if n else 0)
                    if n < 2:
                        need(pe, sc_free, b, 0)
                    return sc_ps[1 - n % 2]

                def tokens(b):
                    need(pe, patch_in, b, 16)
                    m = claim_f(b, 0)
                    for c, rows in ((0, P), (1, S_IMG - P)):
                        for k in range(KT):
                            last = nc.tensor.matmul(m[0:rows, c * D:(c + 1) * D], patch[:, k, c * P:c * P + rows], tokw[:, k, :],
                                                    start=(k == 0), stop=(k == KT - 1))
                            if c == 1 and k == KT - 1:
                                last.then_inc(f_full.sem, 1)
                    pe.drain().then_inc(patch_used.sem, 1)

                def front(b, slot):
                    if slot == (5, 0) and not (isinstance(b, int) and b == 0):
                        tokens(b)
                    if slot == (6, 0):
                        need(pe, xf_ok, b, 1)
                        m = claim_f(b, 1)
                        for c in range(NC):
                            last = nc.tensor.transpose(m[:, c * P:(c + 1) * P], xf[:, c * D:(c + 1) * D], ident[:])
                        last.then_inc(f_full.sem, 1)
                    if slot == (6, 1):
                        need(pe, f_free, b, 2)
                        for n in (2, 3):
                            m = claim_f(b, n)
                            nc.tensor.matmul(m[:, 0:S], wqkv[:, n - 2, :], xfT[:, 0:S], start=True, stop=True).then_inc(f_full.sem, 1)
                    if slot == (7, 0):
                        m = claim_f(b, 4)
                        for c in range(NC):
                            last = nc.tensor.matmul(m[:, c * D:(c + 1) * D], xfT[:, c * P:(c + 1) * P], wqkv[:, 2, :], start=True, stop=True)
                        last.then_inc(f_full.sem, 1)
                    if slot == (7, 1):
                        need(pe, f_free, b, 4)
                        m = claim_f(b, 5)
                        nc.tensor.matmul(m[:, 0:S], w1k[:], kT[:], start=True, stop=True)
                        for r in range(QG):
                            last = nc.tensor.matmul(m[:, S:S + NG], w1q[:, r, :], qT[:, r:r + QG * (NG - 1) + 1:QG],
                                                    start=(r == 0), stop=(r == QG - 1))
                        last.then_inc(f_full.sem, 1)

                def score_groups(b, g0, g1):
                    for g in range(g0, g1):
                        c, gl = g // 16, g % 16
                        if gl == 0:
                            if c < 2:
                                need(pe, f_free, b, 6)
                            else:
                                need(pe, sc_free, b, c - 1)
                            nc.tensor.matmul(sc_ps[c % 2][:, 0:S], qTs[:, c * P:(c + 1) * P], kT[:], start=True, stop=True)
                        need(pe, tanh_ok, b, g + 1)
                        j, off = gl // 4, 24 - QG * (gl % 4)
                        last = nc.tensor.matmul(sc_ps[c % 2][32 * j:32 * j + 32, 0:S], w2s[:, off:off + 32], th[:, g % NTH, :],
                                                start=False, stop=True, skip_group_check=True)
                        last.then_inc(est_ok.sem, 1)

                def attend(b, slot):
                    if slot in SLOTS:
                        score_groups(b, *SLOTS[slot])
                    if slot == (6, 0):
                        need(pe, exp_ok, b, 1)
                        for kc in range(NC):
                            m = claim(b, kc)
                            for qc in range(NC):
                                last = nc.tensor.transpose(m[0:ROWS[kc], qc * P:(qc + 1) * P], pr[:, qc, kc * P:kc * P + ROWS[kc]], ident[:])
                            last.then_inc(misc_full.sem, 1)
                    if slot == (6, 1):
                        need(pe, misc_free, b, 3)
                        m = claim(b, 3)
                        for qc in range(NC):
                            for kc in range(NC):
                                last = nc.tensor.matmul(m[:, qc * D:(qc + 1) * D], pT[0:ROWS[kc], kc, qc * P:(qc + 1) * P],
                                                        v_sb[0:ROWS[kc], kc, :], start=(kc == 0), stop=(kc == NC - 1))
                        last.then_inc(misc_full.sem, 1)
                    if slot == (7, 1):
                        need(pe, xn_ok, b, 1)
                        m = claim(b, 4)
                        for c in range(NC):
                            last = nc.tensor.transpose(m[:, c * P:(c + 1) * P], xn[:, c * D:(c + 1) * D], ident[:])
                        last.then_inc(misc_full.sem, 1)

                def router(b):
                    need(pe, in_ok, b, 1)
                    for c in range(NC):
                        last = nc.tensor.matmul(misc[1][:, c * E0:(c + 1) * E0], xTm[:, c * P:(c + 1) * P], rw[:], start=True, stop=True)
                    last.then_inc(m_full.sem, 1)

                def up(b, e, half):
                    if e == 0:
                        need(pe, in_ok, b, 1)
                    for f in (2 * half, 2 * half + 1):
                        need(pe, hid_ok, b, FC * e + f - 1)
                        nc.tensor.matmul(h_ps[f % 2][:, 0:S], w1[:, e, f * P:(f + 1) * P], xTm[:, 0:S], start=True, stop=True)\
                            .then_inc(hid_full.sem, 1)

                def down(b, e):
                    need(pe, hid_ok, b, FC * (e + 1))
                    need(pe, y_free, b, e)
                    for c in range(NC):
                        for f in range(FC):
                            last = nc.tensor.matmul(y_ps[:, c * D:(c + 1) * D], hid[:, e % 2, f, c * P:(c + 1) * P], w2[:, e, f, :],
                                                    start=(f == 0), stop=(f == FC - 1))
                    last.then_inc(y_full.sem, 1)

                def biases(b, k):
                    if k == 0:
                        need(pe, comb_ok, b, 1)
                        for c in range(NC):
                            last = nc.tensor.transpose(misc[0][0:E0, c * P:(c + 1) * P], combm[:, c, 0:E0], ident[:])
                        last.then_inc(m_full.sem, 1)
                    if k == 1:
                        need(pe, m_free, b, 2)
                        for c in range(NC):
                            last = nc.tensor.matmul(misc[1][:, c * D:(c + 1) * D], combT[:, c * P:(c + 1) * P], b2[:], start=True, stop=True)
                        last.then_inc(m_full.sem, 1)

                def retain(b, slot):
                    if slot == (1, 1):
                        need(pe, src_ok, b, 1)
                        need(pe, r_free, b, 0)
                        for c in range(NC):
                            last = nc.tensor.transpose(r_ps[:, c * P:(c + 1) * P], src_st[:, c * D:(c + 1) * D], ident[:])
                        last.then_inc(r_full.sem, 1)
                    for c in range(NC):
                        if slot == (c + 2, 1):
                            need(pe, r_free, b, c + 1)
                            nc.tensor.matmul(r_ps[:, 0:3 * D], srcT[:, c * P:(c + 1) * P], wkvg[:], start=True, stop=True).then_inc(r_full.sem, 1)
                    if slot == (5, 1):
                        need(pe, r_free, b, 4)
                        nc.tensor.matmul(r_ps[:, 0:S], wq1[:], srcT[:, 0:S], start=True, stop=True)
                        for c in range(NC):
                            last = nc.tensor.matmul(r_ps[:, S:S + D + 1], k_st[0:ROWS[c], c, :], v_st[0:ROWS[c], c, :],
                                                    start=(c == 0), stop=(c == NC - 1))
                        last.then_inc(r_full.sem, 1)
                    if slot == (6, 1):
                        need(pe, r_free, b, 5)
                        for c in range(NC):
                            last = nc.tensor.matmul(r_ps[:, c * OW:(c + 1) * OW], qrT[:, c * P:(c + 1) * P], kv_st[:], start=True, stop=True)
                        last.then_inc(r_full.sem, 1)

                def step(moe, att, fro, ret):
                    for e in range(E0):
                        for k in range(2):
                            if moe is not None:
                                up(moe, e, k)
                                if k == 1 and e:
                                    down(moe, e - 1)
                                if (e, k) == (0, 0):
                                    router(moe)
                                if (e, k) in ((2, 0), (2, 1)):
                                    biases(moe, k)
                            if att is not None:
                                attend(att, (e, k))
                            if fro is not None:
                                front(fro, (e, k))
                            if ret is not None:
                                retain(ret, (e, k))
                    if moe is not None:
                        down(moe, E0 - 1)

                pe.sem_inc(y_full.sem, y_full.start)
                pe.wait_ge(w_tok.sem, 16 * 5)
                pe.wait_ge(consts.sem, 2)
                tokens(0)
                pe.wait_ge(w_att.sem, 16 * 8)
                pe.wait_ge(consts_v.sem, 2)
                step(None, None, 0, None)
                step(None, 0, 1, None)
                pe.wait_ge(w_moe.sem, 16 * 4)
                pe.wait_ge(w_l1.sem, 16 * 23)
                step(0, 1, 2, None)
                with pe.Fori(0, B - 3) as b:
                    step(b + 1, b + 2, b + 3, b)
                step(B - 2, B - 1, None, B - 3)
                step(B - 1, None, None, B - 2)
                pe.drain().then_inc(l0_done.sem, 1)
                step(None, None, None, B - 1)

            @block.scalar
            def _(act):
                def attend(b, slot):
                    n = 2 * slot[0] + slot[1] + 1
                    for g in range(*SLOTS.get((n // 2, n % 2), (0, 0))):
                        if g == 0:
                            need(act, hbias_ok, b, 1)
                        if g >= NTH:
                            need(act, est_ok, b, g - NTH + 1)
                        else:
                            need(act, est_ok, b, 0)
                        nc.scalar.activation(th[:, g % NTH, :], hk[:], ACT.Tanh, bias=hq[:, g:g + 1]).then_inc(tanh_ok.sem, 1)
                    if slot == (5, 0):
                        need(act, nmax_ok, b, 1)
                        need(act, misc_free, b, 0)
                        for c in range(NC):
                            last = nc.scalar.activation(pr[:, c, :], sc[:, c, :], ACT.Exp, bias=nmax[:, c:c + 1], accum_out=rsum[:, c:c + 1])
                        last.then_inc(exp_ok.sem, 1)

                def route(b):
                    need(act, lg_ok, b, 1)
                    nc.scalar.activation(ex[:], lg[:], ACT.Exp).then_inc(ex_ok.sem, 1)

                def gelu(b, e, half):
                    need(act, y_full, b, e - 1)
                    for f in (2 * half, 2 * half + 1):
                        need(act, hid_full, b, FC * e + f + 1)
                        nc.scalar.activation(hid[:, e % 2, f, 0:S], h_ps[f % 2][:, 0:S], ACT.Gelu, bias=b1[:, e * FC + f:e * FC + f + 1])\
                            .then_inc(hid_ok.sem, 1)

                def step(moe, att):
                    for e in range(E0):
                        for k in range(2):
                            if moe is not None:
                                gelu(moe, e, k)
                                if (e, k) == (0, 1):
                                    route(moe)
                            if att is not None:
                                attend(att, (e, k))

                act.sem_inc(hid_ok.sem, hid_ok.start)
                act.wait_ge(consts_v.sem, 2)
                step(None, 0)
                act.wait_ge(w_moe.sem, 16 * 4)
                step(0, 1)
                with act.Fori(1, B - 1) as b:
                    step(b, b + 1)
                step(B - 1, None)

            @block.vector
            def _(dve):
                dve.sem_inc(y_free.sem, y_free.start)
                nc.vector.memset(h_all[64:P, :].rearrange("p (b c d) -> p b c d", b=B, c=NC)[:, :, NC - 1, :], 0.0).then_inc(consts_v.sem, 1)
                nc.vector.memset(ones[:], 1.0)
                nc.vector.memset(qT[:, S:SP], 0.0)
                nc.vector.memset(qTs[:, S:SP], 0.0)
                nc.vector.memset(qrT[:, S:SP], 0.0)
                nc.vector.memset(v_st[:], 1.0)
                dve.sem_inc(r_free.sem, r_free.start)
                nc.vector.memset(hid[:, :, :, S:], 0.0).then_inc(consts_v.sem, 1)
                dve.wait_ge(w_tok.sem, 16 * 5)
                nc.vector.tensor_tensor(base[:, 0, :], base[:, 0, :], base_add[:, 0, :], ALU.add)
                nc.vector.tensor_tensor(base[0:S_IMG - P, 1, :], base[0:S_IMG - P, 1, :], base_add[0:S_IMG - P, 1, :], ALU.add)\
                    .then_inc(consts_v.sem, 1)
                dve.wait_ge(consts_v.sem, 3)
                dve.wait_ge(txt_in.sem, 32)
                dve.wait_ge(consts.sem, 2)

                def attend(b, slot, link):
                    for c, at in ((0, (2, 1)), (1, (4, 0)), (2, (5, 0))):
                        if slot == at:
                            need(dve, est_ok, b, min(16 * (c + 1), NG))
                            need(dve, exp_ok, b, 0)
                            nc.vector.tensor_scalar(sc[:, c, :], sc_ps[c % 2][:, 0:S], b2a[:], None, ALU.add, ALU.max,
                                                    accum_out=smax[:, c:c + 1]).then_inc(sc_free.sem, 1)
                    if slot == (5, 0):
                        need(dve, sc_free, b, NC)
                        nc.vector.tensor_scalar(nmax[:], smax[:], -1.0, None, ALU.mult).then_inc(nmax_ok.sem, 1)
                    if slot == (6, 0):
                        for kc in range(NC):
                            need(dve, misc_full, b, kc + 1)
                            nc.vector.tensor_copy(pT[0:ROWS[kc], kc, :], misc[kc % 2][0:ROWS[kc], 0:SP]).then_inc(misc_free.sem, 1)
                    if slot == (6, 1):
                        need(dve, exp_ok, b, 1)
                        link(nc.vector.reciprocal(rinv[:], rsum[:]))
                        need(dve, misc_full, b, 4)
                        for c in range(NC):
                            last = nc.vector.scalar_tensor_tensor(h1(b, c), misc[1][:, c * D:(c + 1) * D], rinv[:, c:c + 1], h1(b, c), ALU.mult, ALU.add)
                        last.then_inc(misc_free.sem, 1)
                        need(dve, misc_free, b, 4)
                        token_stats([h1(b, c) for c in range(NC)], st, mv, link)
                        nc.vector.tensor_scalar(ve[:], mv[:, :, 1], EPS, None, ALU.add).then_inc(var_ok.sem, 1)
                    if slot == (7, 0):
                        need(dve, rstd_ok, b, 1)
                        for c in range(NC):
                            last = nc.vector.tensor_scalar(xn[:, c * D:(c + 1) * D], h1(b, c), mv[:, c, 0:1], rs[:, c:c + 1],
                                                           ALU.subtract, ALU.mult)
                        last.then_inc(xn_ok.sem, 1)
                    if slot == (7, 1):
                        need(dve, hid_full, b, 0)
                        need(dve, misc_full, b, 5)
                        nc.vector.tensor_copy(xTm[:], misc[0][:, 0:SP]).then_inc(misc_free.sem, 1)
                        need(dve, misc_free, b, 5)
                        dve.sem_inc(in_ok.sem, 1)

                def front(b, slot, link):
                    if slot == (5, 0):
                        need(dve, f_full, b, 1)
                        m = sc_ps[1]
                        nc.vector.tensor_tensor(h1(b, 0), m[:, 0:D], base[:, 0, :], ALU.add)
                        rows = S_IMG - P
                        nc.vector.tensor_tensor(h_all[0:rows, bass.ds(b * SP + P, P)], m[0:rows, D:2 * D], base[0:rows, 1, :], ALU.add)\
                            .then_inc(f_free.sem, 1)
                        need(dve, f_free, b, 1)
                        token_stats([h1(b, c) for c in range(NC)], st_f, mv_f, link)
                        nc.vector.tensor_scalar(ve_f[:], mv_f[:, :, 1], EPS, None, ALU.add).then_inc(fvar_ok0.sem, 1)
                    if slot == (5, 1):
                        need(dve, frstd_ok, b, 1)
                        for c in range(NC):
                            last = nc.vector.tensor_scalar(xf[:, c * D:(c + 1) * D], h1(b, c), mv_f[:, c, 0:1], rs_f[:, c:c + 1],
                                                           ALU.subtract, ALU.mult)
                        last.then_inc(xf_ok.sem, 1)
                    if slot == (6, 0):
                        need(dve, f_full, b, 2)
                        nc.vector.tensor_copy(xfT[:], sc_ps[0][:, 0:SP]).then_inc(f_free.sem, 1)
                    if slot == (6, 1):
                        if isinstance(b, int) and b == 0:
                            dve.wait_ge(w_att.sem, 16 * 8)
                        need(dve, f_full, b, 3)
                        nc.vector.tensor_copy(qT[:, 0:S], sc_ps[1][:, 0:S])
                        nc.vector.tensor_scalar(qTs[:, 0:S], sc_ps[1][:, 0:S], SCALE, None, ALU.mult).then_inc(f_free.sem, 1)
                        need(dve, f_full, b, 4)
                        nc.vector.tensor_copy(kT[:], sc_ps[0][:, 0:S]).then_inc(f_free.sem, 1)
                    if slot == (7, 0):
                        need(dve, f_full, b, 5)
                        nc.vector.tensor_copy(v_sb[:].rearrange("p c d -> p (c d)"), sc_ps[1][:, 0:SP]).then_inc(f_free.sem, 1)
                    if slot == (7, 1):
                        need(dve, f_full, b, 6)
                        need(dve, tanh_ok, b, 0)
                        nc.vector.tensor_copy(hk[:], sc_ps[0][:, 0:S])
                        nc.vector.tensor_scalar(hq[:], sc_ps[0][:, S:S + NG], hb1[:], None, ALU.add).then_inc(f_free.sem, 1)
                        need(dve, f_free, b, 6)
                        dve.sem_inc(hbias_ok.sem, 1)

                def bc(x, n):
                    return x.unsqueeze(2).broadcast_to([P, NC, n])

                def logits(b, link):
                    need(dve, m_full, b, 1)
                    m3 = misc[1][:, 0:NC * E0].rearrange("p (c e) -> p c e", c=NC)
                    rb3 = rb[:].unsqueeze(1).broadcast_to([P, NC, E0])
                    nc.vector.tensor_tensor(lg[:], m3, rb3, ALU.add).then_inc(m_free.sem, 1)
                    need(dve, m_free, b, 1)
                    link(nc.vector.tensor_reduce(lmax[:], lg[:], AX.X, ALU.max))
                    nc.vector.tensor_tensor(lg[:], lg[:], bc(lmax[:], E0), ALU.subtract).then_inc(lg_ok.sem, 1)

                def route(b, link):
                    need(dve, ex_ok, b, 1)
                    link(nc.vector.tensor_reduce(esum[:], ex[:], AX.X, ALU.add))
                    link(nc.vector.reciprocal(einv[:], esum[:]))
                    link(nc.vector.tensor_tensor(prob[:], ex[:], bc(einv[:], E0), ALU.mult))
                    dve.sem_inc(waited.sem, 1)
                    for c in range(NC):
                        last = nc.vector.max(top[:, c, :], prob[:, c, :])
                    link(last)
                    dve.sem_inc(waited.sem, 1)
                    for c in range(NC):
                        last = nc.vector.max_index(tidx[:, c, :], top[:, c, :], prob[:, c, :])
                    link(last)
                    nc.vector.tensor_copy(tidf[:], tidx[:, :, 0:2])
                    link(nc.vector.scalar_tensor_tensor(wsum[:], top[:, :, 0], 1.0, top[:, :, 1], ALU.mult, ALU.add))
                    link(nc.vector.tensor_scalar(wsum[:], wsum[:], 1e-9, None, ALU.add))
                    link(nc.vector.reciprocal(winv[:], wsum[:]))
                    link(nc.vector.tensor_tensor(wt[:], top[:, :, 0:2], bc(winv[:], 2), ALU.mult))
                    io = iota[:, 0:E0].unsqueeze(1).broadcast_to([P, NC, E0])
                    for k in range(2):
                        last = nc.vector.tensor_tensor(eq[:, k], io, bc(tidf[:, :, k], E0), ALU.is_equal)
                    link(last)
                    for k in range(2):
                        last = nc.vector.tensor_tensor(cp[:, k], eq[:, k], bc(wt[:, :, k], E0), ALU.mult)
                    link(last)
                    need(dve, y_free, b, 0)
                    nc.vector.tensor_tensor(combm[:, :, 0:E0], cp[:, 0], cp[:, 1], ALU.add).then_inc(comb_ok.sem, 1)

                def biases(b, k):
                    need(dve, m_full, b, 2 + k)
                    if k == 0:
                        nc.vector.tensor_copy(combT[:], misc[0][0:E0, 0:SP]).then_inc(m_free.sem, 1)
                    if k == 1:
                        need(dve, y_free, b, 2)
                        nc.vector.tensor_tensor(h_all[:, bass.ds(b * SP, SP)], h_all[:, bass.ds(b * SP, SP)], misc[1][:, 0:SP], ALU.add)\
                            .then_inc(m_free.sem, 1)
                        need(dve, m_free, b, 3)

                def add_expert(b, e):
                    if e == 0:
                        need(dve, comb_ok, b, 1)
                    need(dve, y_full, b, e + 1)
                    need(dve, y_free, b, e)
                    for c in range(NC):
                        last = nc.vector.scalar_tensor_tensor(h1(b, c), y_ps[:, c * D:(c + 1) * D], combm[:, c, e:e + 1], h1(b, c),
                                                              ALU.mult, ALU.add)
                    last.then_inc(y_free.sem, 1)

                def retain(b, slot, rlink):
                    if slot == (0, 0):
                        need(dve, y_free, b, E0, waited)
                        token_stats([h1(b, c) for c in range(NC)], st_r, mv_r, rlink)
                        nc.vector.tensor_scalar(ve_r[:], mv_r[:, :, 1], EPS, None, ALU.add).then_inc(rvar_ok.sem, 1)
                    if slot == (1, 0):
                        need(dve, rrstd_ok, b, 1)
                        need(dve, parts_free, b, 0)
                        for c in range(NC):
                            last = nc.vector.tensor_scalar(src_st[:, c * D:(c + 1) * D], h1(b, c), mv_r[:, c, 0:1], rs_r[:, c:c + 1],
                                                           ALU.subtract, ALU.mult)
                        last.then_inc(src_ok.sem, 1)
                    if slot == (2, 0):
                        need(dve, r_full, b, 1)
                        nc.vector.tensor_copy(srcT[:], r_ps[:, 0:SP]).then_inc(r_free.sem, 1)
                    for c in range(NC):
                        if slot == (c + 3, 0):
                            need(dve, r_full, b, c + 2)
                            if c == 0:
                                need(dve, parts_free, b, 0)
                            nc.vector.tensor_tensor(k_st[:, c, :], r_ps[:, 0:D], bkvg[:, 0:D], ALU.add)
                            nc.vector.tensor_tensor(v_st[:, c, 0:D], r_ps[:, D:2 * D], bkvg[:, D:2 * D], ALU.add)
                            nc.vector.tensor_tensor(g_st[:, c, :], r_ps[:, 2 * D:3 * D], bkvg[:, 2 * D:], ALU.add).then_inc(r_free.sem, 1)
                            if c == NC - 1:
                                need(dve, r_free, b, 4)
                                dve.sem_inc(kvg_ok.sem, 1)
                    if slot == (6, 0):
                        need(dve, r_full, b, 5)
                        nc.vector.tensor_scalar(qrT[:, 0:S], r_ps[:, 0:S], bq1[:], None, ALU.add)
                        rlink(nc.vector.tensor_copy(ksum[:], r_ps[:, S + D:S + D + 1]))
                        nc.vector.tensor_tensor(kv_st[:, 0:D], r_ps[:, S:S + D], bd[:], ALU.mult)
                        nc.vector.tensor_scalar(kv_st[:, D:], bd8[:], ksum[:], None, ALU.mult).then_inc(r_free.sem, 1)
                    if slot == (7, 0):
                        need(dve, r_full, b, 6)
                        need(dve, parts_free, b, 0)
                        nc.vector.tensor_copy(o_st[:], r_ps[:, 0:NC * OW]).then_inc(r_free.sem, 1)
                        need(dve, r_free, b, 6)
                        dve.sem_inc(o_ok.sem, 1)

                def step(moe, att, fro, ret):
                    link, flink, mlink, rlink = Chain(dve, a_chain, att), Chain(dve, f_chain, fro), Chain(dve, m_chain, moe), Chain(dve, r_chain, ret)
                    for e in range(E0):
                        for k in range(2):
                            if k == 1 and moe is not None and e:
                                add_expert(moe, e - 1)
                            if moe is not None and (e, k) == (0, 0):
                                logits(moe, mlink)
                            if ret is not None:
                                retain(ret, (e, k), rlink)
                            if moe is not None:
                                if (e, k) == (0, 1):
                                    route(moe, mlink)
                                if (e, k) in ((2, 0), (2, 1)):
                                    biases(moe, k)
                            if att is not None:
                                attend(att, (e, k), link)
                            if fro is not None:
                                front(fro, (e, k), flink)
                    if moe is not None:
                        add_expert(moe, E0 - 1)
                        mlink.end(m_chain.per)
                    if att is not None:
                        link.end(a_chain.per)
                    if fro is not None:
                        flink.end(f_chain.per)
                    if ret is not None:
                        rlink.end(r_chain.per)

                step(None, None, 0, None)
                step(None, 0, 1, None)
                step(0, 1, 2, None)
                with dve.Fori(0, B - 3) as b:
                    step(b + 1, b + 2, b + 3, b)
                step(B - 2, B - 1, None, B - 3)
                step(B - 1, None, None, B - 2)
                step(None, None, None, B - 1)
                dve.wait_ge(y_free.sem, y_free.at(B, 0))
                dve.wait_ge(w_moe.sem, 16 * 4)

        if stop == "l0":
            fin = signal("fin")
            with nc.Block() as block:
                @block.sync
                def _(sp):
                    for b in range(B):
                        for c in range(NC):
                            sp.dma_start(out[b, c * P:c * P + ROWS[c], :], h_all[0:ROWS[c], b * SP + c * P:b * SP + (c + 1) * P]).then_inc(fin.sem, 16)
                    sp.wait_ge(fin.sem, 16 * B * NC)
            return

        with ExitStack() as l1:
            def sb1(name, shape, dt=FP32):
                return l1.enter_context(nc.sbuf_tensor(name, shape, dt))

            wgu = sb1("wgu", [P, E1 + 1, 2 * F1])
            wgu_hi, wgu_lo = sb1("wgu_hi", [P, E1 + 1, 2 * F1], FP32R), sb1("wgu_lo", [P, E1 + 1, 2 * F1], FP32R)
            x_hi, x_lo = sb1("x_hi", [P, SP], FP32R), sb1("x_lo", [P, SP], FP32R)
            wdn = sb1("wdn", [P, E1 + 1, D])
            lnb_w = sb1("lnb_w", [P, FC, P])
            o_in = sb1("o_in", [P, NC * OW]); g_in = sb1("g_in", [P, SP]); src_in = sb1("src_in", [P, SP])
            qk_sum = sb1("qk_sum", [P, NC, NH]); qk_abs = sb1("qk_abs", [P, NC, NH]); den = sb1("den", [P, NC, NH]); rden = sb1("rden", [P, NC, NH])
            og = sb1("og", [P, NC, NH, HD]); sq = sb1("sq", [P, NC, NH, HD])
            gsum = sb1("gsum", [P, NC, NH]); gmean = sb1("gmean", [P, NC, NH]); gss = sb1("gss", [P, NC, NH])
            gve = sb1("gve", [P, NC, NH]); grs = sb1("grs", [P, NC, NH])
            sg = sb1("sg", [P, SP]); oT = sb1("oT", [P, SP])
            x_pre = sb1("x_pre", [P, NC, D]); x1 = sb1("x1", [P, NC, D]); x1c = sb1("x1c", [P, NC, D]); x1T = sb1("x1T", [P, S])
            ff = sb1("ff", [P, FC, SP]); ffsq = sb1("ffsq", [P, FC, SP])
            fmean = sb1("fmean", [P, NC]); fms = sb1("fms", [P, NC]); fm2 = sb1("fm2", [P, NC]); fvar = sb1("fvar", [P, NC])
            fve = sb1("fve", [P, NC]); frs = sb1("frs", [P, NC]); fnm = sb1("fnm", [P, NC])
            x2 = sb1("x2", [P, NC, D]); x3 = sb1("x3", [P, NC, D])
            aff = sb1("aff", [P, NC, E1]); rscore = sb1("rscore", [P, NC, E1])
            top3 = sb1("top3", [P, NC, 8]); idx3 = sb1("idx3", [P, NC, 8], U32); idf3 = sb1("idf3", [P, NC, 3])
            eq3 = sb1("eq3", [P, 3, NC, E1]); sel = sb1("sel", [P, NC, E1])
            asum = sb1("asum", [P, NC]); ainv = sb1("ainv", [P, NC])
            ast = sb1("ast", [P, NC, 6]); amv = sb1("amv", [P, NC, 2]); ave = sb1("ave", [P, NC]); ars = sb1("ars", [P, NC])
            anm = sb1("anm", [P, NC]); cnm = sb1("cnm", [P, NC])
            gate = sb1("gate", [P, 2, S]); hid1 = sb1("hid1", [P, 3, SP])

            head_full, head_free = signal("head_full", NC), signal("head_free", NC)
            whi_ok, wlo_ok = signal("whi_ok"), signal("wlo_ok")
            w_moe1, o_here, g_here, src_here = signal("w_moe1"), signal("o_here", 16), signal("g_here", 16), signal("src_here", 16)
            o_used, g_used, src_used = signal("o_used"), signal("g_used"), signal("src_used")
            og_ctr, sq_ok, gve_ok, grs_ok, silu_ok, og_ok = (signal(n) for n in ("og_ctr", "sq_ok", "gve_ok", "grs_ok", "silu_ok", "og_ok"))
            oT_full, oT_ok, wo_full, wo_read = (signal(n) for n in ("oT_full", "oT_ok", "wo_full", "wo_read"))
            avar_ok, arstd_ok, xpre_ok, x1g, x1_ok = (signal(n) for n in ("avar_ok", "arstd_ok", "xpre_ok", "x1g", "x1_ok"))
            x1T_full, x1T_ok, fc1_full = signal("x1T_full"), signal("x1T_ok"), signal("fc1_full", FC)
            ff_ok, ffsq_ok = signal("ff_ok", FC), signal("ffsq_ok")
            fc2_full, fc2_read = signal("fc2_full"), signal("fc2_read")
            cvar_ok, crstd_ok = signal("cvar_ok", 3), signal("crstd_ok", 3)
            x2_ok, x3g, x3_ok, xn4_ok = signal("x2_ok"), signal("x3g"), signal("x3_ok"), signal("xn4_ok")
            anm_ok, cnm_ok = signal("anm_ok"), signal("cnm_ok")
            hx_ok, x1c_ok = signal("hx_ok"), signal("x1c_ok")
            xT_full, xT_ok, rt_full, rt_read = (signal(n) for n in ("xT_full", "xT_ok", "rt_full", "rt_read"))
            lin_ok, aff_ok = signal("lin_ok"), signal("aff_ok")
            a_link, b_link, h_link, g_link = signal("a_link", 3), signal("b_link", 10), signal("h_link", 12), signal("g_link", 7)
            gu_full, gate_ok = signal("gu_full", E1 + 1, 0), signal("gate_ok", E1 + 1, 2)
            hid1_ok = signal("hid1_ok", E1 + 1, 2)
            z_full, z_free = signal("z_full", E1 + 1, 2), signal("z_free", E1 + 1, 2)
            out_ok = signal("out_ok", 16)
            gu_ps, z_ps = banks[2:6], banks[6:8]
            NE = E1 + 1

            def back(e):
                return max(e - 1, 0)

            block = l1.enter_context(nc.Block())

            @block.sync
            def _(sp):
                def load(b):
                    need(sp, o_used, b, 0)
                    sp.dma_start(o_in[:], row(o_d, b)).then_inc(o_here.sem, 16)
                    need(sp, g_used, b, 0)
                    sp.dma_start(g_in[:], row(g_d, b)).then_inc(g_here.sem, 16)
                    need(sp, src_used, b, 0)
                    sp.dma_start(src_in[:], row(src_d, b)).then_inc(src_here.sem, 16)

                def store(b):
                    need(sp, z_free, b, NE)
                    for c in range(NC):
                        dst = out[bass.ds(b, 1), c * P:c * P + ROWS[c], :].rearrange("a s d -> (a s) d")
                        sp.dma_start(dst, h_all[0:ROWS[c], bass.ds(b * SP + c * P, P)]).then_inc(out_ok.sem, 16)

                load(0)
                sp.dma_start(wgu[:], t["wgu"]).then_inc(w_moe1.sem, 16)
                sp.dma_start(wdn[:], t["wdn"]).then_inc(w_moe1.sem, 16)
                load(1)
                load(2)
                with sp.Fori(0, B - 3) as b:
                    load(b + 3)
                    store(b)
                store(B - 3)
                store(B - 2)
                store(B - 1)
                sp.wait_ge(out_ok.sem, 16 * NC * B)

            @block.gpsimd
            def _(pool):
                def root(x, y, sig_in, sig_out, b, k):
                    need(pool, sig_in, b, k)
                    nc.gpsimd.tensor_tensor(y[:], x[:], neghalf[:, 0:NC], ALU.pow).then_inc(sig_out.sem, 1)

                def gain(b, x, y, g_, b_, sig_in, sig_mid, sig_out):
                    need(pool, sig_in, b, 1)
                    nc.gpsimd.tensor_tensor(y[:], x[:], g_[:].unsqueeze(1).broadcast_to([P, NC, D]), ALU.mult).then_inc(sig_mid.sem, 1)
                    need(pool, sig_mid, b, 1)
                    nc.gpsimd.tensor_tensor(y[:], y[:], b_[:].unsqueeze(1).broadcast_to([P, NC, D]), ALU.add).then_inc(sig_out.sem, 1)

                def step(two, one, zero):
                    if two is not None:
                        root(cve, crs, cvar_ok, crstd_ok, two, 1)
                        root(cve, crs, cvar_ok, crstd_ok, two, 2)
                        gain(two, x2, x3, n1g, n1b, x2_ok, x3g, x3_ok)
                        need(pool, x3_ok, two, 1)
                        hb = h_all[:, bass.ds(two * SP, SP)]
                        nc.gpsimd.tensor_tensor(hb, hb, x3[:].rearrange("p c d -> p (c d)"), ALU.add).then_inc(hx_ok.sem, 1)
                    if one is not None:
                        root(ave, ars, avar_ok, arstd_ok, one, 1)
                    if two is not None:
                        root(cve, crs, cvar_ok, crstd_ok, two, 3)
                    if one is not None:
                        gain(one, x_pre, x1, n0g, n0b, xpre_ok, x1g, x1_ok)
                        need(pool, x1_ok, one, 1)
                        nc.gpsimd.tensor_tensor(x1c[:], x1[:], c2[:].unsqueeze(1).broadcast_to([P, NC, D]), ALU.add).then_inc(x1c_ok.sem, 1)
                    if zero is not None:
                        need(pool, gve_ok, zero, 1)
                        nc.gpsimd.tensor_tensor(grs[:].rearrange("p c h -> p (c h)"), gve[:].rearrange("p c h -> p (c h)"), neghalf[:], ALU.pow)\
                            .then_inc(grs_ok.sem, 1)

                step(None, None, 0)
                step(None, 0, 1)
                with pool.Fori(0, B - 2) as b:
                    step(b, b + 1, b + 2)
                step(B - 2, B - 1, None)
                step(B - 1, None, None)

            @block.tensor
            def _(pe):
                pe.sem_inc(z_full.sem, z_full.start)
                pe.wait_ge(dec_in.sem, 16)
                for h in range(NH):
                    for ic in range(NC):
                        if h >= 2:
                            need(pe, head_free, h, ic + 1 - 2 * NC)
                        bank = banks[3 * (h % 2) + ic]
                        for jc in range(ic + 1):
                            last = nc.tensor.matmul(bank[0:ROWS[ic], 0:B * HD], decay[0:ROWS[jc], h, jc, ic * P:ic * P + ROWS[ic]],
                                                    v_all[0:ROWS[jc], :].rearrange("p (b c d) -> p b c d", b=B, c=NC)[:, :, jc, h * HD:(h + 1) * HD],
                                                    start=(jc == 0), stop=(jc == ic))
                        last.then_inc(head_full.sem, 1)
                pe.wait_ge(head_free.sem, NH * NC)
                pe.wait_ge(setup_v.sem, 1)
                for f in range(FC):
                    nc.tensor.matmul(banks[6][:, 0:D], ones[:], fc2g[:, f, 0:D], start=(f == 0), stop=(f == FC - 1))
                for f in range(FC):
                    nc.tensor.matmul(banks[7][:, 0:D], lnb_w[:, f, :], fc2[:, f, :], start=(f == 0), stop=False)
                nc.tensor.matmul(banks[7][:, 0:D], ones[0:1, :], fc2b[:], start=False, stop=True).then_inc(setup_pe.sem, 1)

                def first_part(b, slot):
                    if slot == 3:
                        need(pe, og_ok, b, 1)
                        need(pe, ff_ok, b, 0)
                        for c in range(NC):
                            last = nc.tensor.transpose(banks[0][:, c * P:(c + 1) * P], og[:, c].rearrange("p h d -> p (h d)"), ident[:])
                        last.then_inc(oT_full.sem, 1)
                    if slot == 5:
                        need(pe, oT_ok, b, 1)
                        for c in range(NC):
                            nc.tensor.matmul(banks[0][:, c * D:(c + 1) * D], oT[:, c * P:(c + 1) * P], wo[:], start=True, stop=False)
                            last = nc.tensor.matmul(banks[0][:, c * D:(c + 1) * D], ones[0:1, :], bo[:], start=False, stop=True)
                        last.then_inc(wo_full.sem, 1)
                    if slot == 12:
                        need(pe, x1_ok, b, 1)
                        need(pe, wo_read, b, 1)
                        for c in range(NC):
                            last = nc.tensor.transpose(banks[0][:, c * P:(c + 1) * P], x1[:, c, :], ident[:])
                        last.then_inc(x1T_full.sem, 1)

                def feed_forward(b, k):
                    if k == 0:
                        need(pe, x1T_ok, b, 1)
                        need(pe, rt_read, b, 0)
                    for f in (2 * k, 2 * k + 1):
                        if k:
                            need(pe, ff_ok, b, f - 1)
                        nc.tensor.matmul(banks[f % 2][:, 0:S], fc1[:, f * P:(f + 1) * P], x1T[:], start=True, stop=True).then_inc(fc1_full.sem, 1)

                def second_part(b, slot):
                    if slot < NC:
                        c, m = slot, banks[1]
                        need(pe, ffsq_ok, b, 1)
                        o0 = c * (D + 2)
                        for f in range(FC):
                            nc.tensor.matmul(m[:, o0:o0 + D + 1], ff[:, f, c * P:(c + 1) * P], fc2g[:, f, :], start=(f == 0), stop=(f == FC - 1))
                        for f in range(FC):
                            last = nc.tensor.matmul(m[:, o0 + D + 1:o0 + D + 2], ffsq[:, f, c * P:(c + 1) * P], ones[:, 0:1],
                                                    start=(f == 0), stop=(f == FC - 1))
                        if c == NC - 1:
                            last.then_inc(fc2_full.sem, 1)
                    if slot == 12:
                        need(pe, xn4_ok, b, 1)
                        need(pe, fc2_read, b, 1)
                        for c in range(NC):
                            last = nc.tensor.transpose(banks[1][:, c * P:(c + 1) * P], xn[:, c * D:(c + 1) * D], ident[:])
                        last.then_inc(xT_full.sem, 1)
                    if slot == 13:
                        need(pe, xT_ok, b, 1)
                        for c in range(NC):
                            last = nc.tensor.matmul(banks[1][:, c * E1:(c + 1) * E1], xT[:, c * P:(c + 1) * P], gw[:], start=True, stop=True)
                        last.then_inc(rt_full.sem, 1)

                def up(b, e):
                    if e == 0:
                        need(pe, lin_ok, b, 1)
                    need(pe, hid1_ok, b, back(e))
                    for k in range(2):
                        for n, (w, x) in enumerate(((wgu_hi, x_hi), (wgu_hi, x_lo), (wgu_lo, x_hi))):
                            last = nc.tensor.matmul(gu_ps[2 * (e % 2) + k][:, 0:S2], w[:, e, k * F1:(k + 1) * F1], x[:, 0:S2],
                                                    start=(n == 0), stop=(n == 2))
                    last.then_inc(gu_full.sem, 1)

                def down(b, e):
                    need(pe, hid1_ok, b, e + 1)
                    need(pe, z_free, b, back(e))
                    for c in range(NC):
                        last = nc.tensor.matmul(z_ps[e % 2][:, c * D:(c + 1) * D], hid1[:, e % 3, c * P:(c + 1) * P], wdn[:, e, :], start=True, stop=True)
                    last.then_inc(z_full.sem, 1)

                def step(last, moe, two, one):
                    for e in range(NE):
                        if e == 0 and last is not None:
                            down(last, NE - 2)
                        if e == 0 and two is not None:
                            second_part(two, e)
                        if moe is not None:
                            up(moe, e)
                        if e and two is not None:
                            second_part(two, e)
                        if one is not None:
                            first_part(one, e)
                            if e in (14, 15):
                                feed_forward(one, e - 14)
                        if e == 1 and last is not None:
                            down(last, NE - 1)
                        if moe is not None and e >= 2:
                            down(moe, e - 2)

                step(None, None, None, 0)
                step(None, None, 0, 1)
                pe.wait_ge(w_moe1.sem, 32)
                pe.wait_ge(wlo_ok.sem, 1)
                step(None, 0, 1, 2)
                with pe.Fori(0, B - 3) as b:
                    step(b, b + 1, b + 2, b + 3)
                step(B - 3, B - 2, B - 1, None)
                step(B - 2, B - 1, None, None)
                down(B - 1, NE - 2)
                down(B - 1, NE - 1)

            @block.scalar
            def _(act):
                act.sem_inc(gate_ok.sem, gate_ok.start)

                def normalise(b, x, rstd, minus_mean_rstd, sig_in, sig_out):
                    need(act, sig_in, b, 1)
                    for c in range(NC):
                        last = nc.scalar.activation(x[:, c, :], x[:, c, :], ACT.Identity, bias=minus_mean_rstd[:, c:c + 1], scale=rstd[:, c:c + 1])
                    last.then_inc(sig_out.sem, 1)

                def first_part(b, slot):
                    if slot == 9:
                        normalise(b, x_pre, ars, anm, anm_ok, xpre_ok)
                    if slot == 0:
                        need(act, g_here, b, 16)
                        need(act, og_ok, b, 0)
                        nc.scalar.activation(sg[:], g_in[:], ACT.Silu).then_inc(silu_ok.sem, 1)
                    if slot == 3:
                        need(act, oT_full, b, 1)
                        nc.scalar.activation(oT[:], banks[0][:, 0:SP], ACT.Copy).then_inc(oT_ok.sem, 1)
                    if slot == 13:
                        need(act, x1T_full, b, 1)
                        nc.scalar.activation(x1T[:], banks[0][:, 0:S], ACT.Copy).then_inc(x1T_ok.sem, 1)
                    if slot == 14:
                        for f in range(FC):
                            need(act, fc1_full, b, f + 1)
                            nc.scalar.activation(ff[:, f, 0:S], banks[f % 2][:, 0:S], ACT.Gelu, bias=fc1b[:, f:f + 1]).then_inc(ff_ok.sem, 1)
                    if slot == 15:
                        need(act, ff_ok, b, FC)
                        nc.scalar.activation(ffsq[:, :, 0:S], ff[:, :, 0:S], ACT.Square).then_inc(ffsq_ok.sem, 1)

                def second_part(b, slot):
                    if slot == 7:
                        normalise(b, x2, crs, cnm, cnm_ok, x2_ok)
                    if slot == 12:
                        need(act, xT_full, b, 1)
                        need(act, lin_ok, b, 0)
                        nc.scalar.activation(xT[:], banks[1][:, 0:SP], ACT.Copy).then_inc(xT_ok.sem, 1)
                    if slot == 14:
                        need(act, rt_full, b, 1)
                        nc.scalar.activation(aff[:], banks[1][:, 0:NC * E1].rearrange("p (c e) -> p c e", c=NC), ACT.Sigmoid).then_inc(aff_ok.sem, 1)
                        need(act, aff_ok, b, 1)
                        act.sem_inc(rt_read.sem, 1)

                def silu(b, e):
                    need(act, gu_full, b, e + 1)
                    need(act, hid1_ok, b, back(e))
                    nc.scalar.activation(gate[:, e % 2, :], gu_ps[2 * (e % 2)][:, 0:S], ACT.Silu).then_inc(gate_ok.sem, 1)

                def step(moe, two, one, zero):
                    for e in range(NE):
                        if moe is not None:
                            silu(moe, e)
                        if two is not None:
                            second_part(two, e)
                        if one is not None:
                            first_part(one, e)
                        if zero is not None and e == 15:
                            need(act, og_ctr, zero, 1)
                            nc.scalar.activation(sq[:], og[:], ACT.Square).then_inc(sq_ok.sem, 1)

                step(None, None, None, 0)
                step(None, None, 0, 1)
                act.wait_ge(w_moe1.sem, 32)
                nc.scalar.activation(wgu_hi[:], wgu[:], ACT.Copy).then_inc(whi_ok.sem, 1)
                step(None, 0, 1, 2)
                with act.Fori(0, B - 3) as b:
                    step(b, b + 1, b + 2, b + 3)
                step(B - 3, B - 2, B - 1, None)
                step(B - 2, B - 1, None, None)
                step(B - 1, None, None, None)

            @block.vector
            def _(dve):
                dve.sem_inc(hid1_ok.sem, hid1_ok.start)
                dve.sem_inc(z_free.sem, z_free.start)
                dve.wait_ge(w_l1.sem, 16 * 23)
                nc.vector.memset(hid1[:, :, S:], 0.0)
                nc.vector.memset(ff[:, :, S:], 0.0)
                nc.vector.memset(ffsq[:, :, S:], 0.0)
                for f in range(FC):
                    nc.vector.tensor_scalar(fc2g[:, f, 0:D], fc2[:, f, :], lng[:, f:f + 1], None, ALU.mult)
                    nc.vector.tensor_scalar(lnb_w[:, f, :], ones[:], lnb[:, f:f + 1], None, ALU.mult)
                nc.vector.memset(fc2g[:, :, D:], 1.0).then_inc(setup_v.sem, 1)
                for h in range(NH):
                    for ic in range(NC):
                        need(dve, head_full, h, ic + 1)
                        if ic == 0:
                            need(dve, head_full, h, NC)
                        dst = v_all[0:ROWS[ic], :].rearrange("p (b c d) -> p b c d", b=B, c=NC)[:, :, ic, h * HD:(h + 1) * HD]
                        nc.vector.tensor_copy(dst, banks[3 * (h % 2) + ic][0:ROWS[ic], 0:B * HD].rearrange("p (b d) -> p b d", b=B))\
                            .then_inc(head_free.sem, 1)
                dve.wait_ge(setup_pe.sem, 1)
                nc.vector.tensor_copy(c1[:], banks[6][:, 0:D])
                nc.vector.tensor_copy(c2[:], banks[7][:, 0:D]).then_inc(setup_v.sem, 1)
                dve.wait_ge(head_free.sem, NH * NC)
                dve.wait_ge(setup_v.sem, 2)

                def bc(x, n):
                    return x.unsqueeze(2).broadcast_to([P, NC, n])

                def per_head(x):
                    return x[:].rearrange("p c h -> p (c h)").unsqueeze(2).broadcast_to([P, NC * NH, HD])

                def flat(x):
                    return x[:].rearrange("p c h d -> p (c h) d")

                def normalise(x, y, mean, rstd):
                    for c in range(NC):
                        last = nc.vector.tensor_scalar(y[c], x[c], mean[:, c, 0:1], rstd[:, c:c + 1], ALU.subtract, ALU.mult)
                    return last

                def group_norm(b, slot, link):
                    if slot == 12:
                        need(dve, o_here, b, 16)
                        o3 = o_in[:].rearrange("p (c n) -> p c n", c=NC)
                        link(nc.vector.tensor_tensor(qk_sum[:], o3[:, :, D:], dsum[:], ALU.add))
                        link(nc.vector.scalar_tensor_tensor(qk_abs[:], qk_sum[:], -1.0, qk_sum[:], ALU.mult, ALU.max))
                        link(nc.vector.tensor_scalar(den[:], qk_abs[:], 1.0, None, ALU.max))
                        nc.vector.reciprocal(rden[:], den[:])
                        need(dve, oT_full, b, 0)
                        nc.vector.tensor_tensor(og[:].rearrange("p c h d -> p c (h d)"), o3[:, :, 0:D],
                                                v_all[:, bass.ds(b * SP, SP)].rearrange("p (c d) -> p c d", c=NC), ALU.add)\
                            .then_inc(o_used.sem, 1)
                        need(dve, o_used, b, 1)
                        link(nc.vector.tensor_tensor(flat(og), flat(og), per_head(rden), ALU.mult))
                    if slot == 13:
                        link(nc.vector.tensor_reduce(gsum[:].rearrange("p c h -> p (c h)"), flat(og), AX.X, ALU.add))
                        link(nc.vector.tensor_scalar(gmean[:], gsum[:], 1.0 / HD, None, ALU.mult))
                        nc.vector.tensor_tensor(flat(og), flat(og), per_head(gmean), ALU.subtract).then_inc(og_ctr.sem, 1)
                    if slot == 16:
                        need(dve, sq_ok, b, 1)
                        link(nc.vector.tensor_reduce(gss[:].rearrange("p c h -> p (c h)"), flat(sq), AX.X, ALU.add))
                        nc.vector.tensor_scalar(gve[:], gss[:], 1.0 / HD, 1e-6, ALU.mult, ALU.add).then_inc(gve_ok.sem, 1)

                def first_part(b, slot, link):
                    xs = [x_pre[:, c, :] for c in range(NC)]
                    og_flat = og[:].rearrange("p c h d -> p (c h d)")
                    if slot == 1:
                        need(dve, grs_ok, b, 1)
                        link(nc.vector.tensor_tensor(flat(og), flat(og), per_head(grs), ALU.mult))
                        need(dve, silu_ok, b, 1)
                        nc.vector.tensor_tensor(og_flat, og_flat, sg[:], ALU.mult).then_inc(og_ok.sem, 1)
                        need(dve, og_ok, b, 1)
                        dve.sem_inc(g_used.sem, 1)
                    if slot == 7:
                        need(dve, wo_full, b, 1)
                        need(dve, src_here, b, 16)
                        nc.vector.tensor_tensor(x_pre[:].rearrange("p c d -> p (c d)"), banks[0][:, 0:SP], src_in[:], ALU.add).then_inc(wo_read.sem, 1)
                        need(dve, wo_read, b, 1, waited)
                        dve.sem_inc(src_used.sem, 1)
                        token_stats(xs, ast, amv, link)
                        nc.vector.tensor_scalar(ave[:], amv[:, :, 1], EPS, None, ALU.add).then_inc(avar_ok.sem, 1)
                    if slot == 8:
                        need(dve, arstd_ok, b, 1)
                        nc.vector.scalar_tensor_tensor(anm[:], amv[:, :, 0], -1.0, ars[:], ALU.mult, ALU.mult).then_inc(anm_ok.sem, 1)

                def second_part(b, slot, link):
                    m3 = banks[1][:, 0:NC * (D + 2)].rearrange("p (c n) -> p c n", c=NC)
                    xs = [x2[:, c, :] for c in range(NC)]
                    hs = [h1(b, c) for c in range(NC)]
                    if slot == 3:
                        need(dve, fc2_full, b, 1)
                        nc.vector.tensor_scalar(fmean[:], m3[:, :, D], 1.0 / FF, None, ALU.mult)
                        link(nc.vector.tensor_scalar(fms[:], m3[:, :, D + 1], 1.0 / FF, None, ALU.mult))
                        link(nc.vector.tensor_tensor(fm2[:], fmean[:], fmean[:], ALU.mult))
                        link(nc.vector.tensor_tensor(fvar[:], fms[:], fm2[:], ALU.subtract))
                        nc.vector.tensor_scalar(cve[:], fvar[:], 0.0, 1e-6, ALU.max, ALU.add).then_inc(cvar_ok.sem, 1)
                    if slot == 4:
                        need(dve, crstd_ok, b, 1)
                        link(nc.vector.scalar_tensor_tensor(fnm[:], fmean[:], -1.0, crs[:], ALU.mult, ALU.mult))
                        need(dve, x1c_ok, b, 1)
                        for c in range(NC):
                            last = nc.vector.scalar_tensor_tensor(x2[:, c, :], c1[:], fnm[:, c:c + 1], x1c[:, c, :], ALU.mult, ALU.add)
                        link(last)
                    if slot == 4:
                        for c in range(NC):
                            last = nc.vector.scalar_tensor_tensor(x2[:, c, :], m3[:, c, 0:D], crs[:, c:c + 1], x2[:, c, :], ALU.mult, ALU.add)
                        last.then_inc(fc2_read.sem, 1)
                    if slot == 5:
                        need(dve, fc2_read, b, 1, waited)
                        token_stats(xs, cst, cmv, link)
                        nc.vector.tensor_scalar(cve[:], cmv[:, :, 1], EPS, None, ALU.add).then_inc(cvar_ok.sem, 1)
                    if slot == 6:
                        need(dve, crstd_ok, b, 2)
                        nc.vector.scalar_tensor_tensor(cnm[:], cmv[:, :, 0], -1.0, crs[:], ALU.mult, ALU.mult).then_inc(cnm_ok.sem, 1)
                    if slot == 9:
                        need(dve, hx_ok, b, 1, waited)
                        token_stats(hs, cst, cmv, link)
                        nc.vector.tensor_scalar(cve[:], cmv[:, :, 1], EPS, None, ALU.add).then_inc(cvar_ok.sem, 1)
                    if slot == 10:
                        need(dve, crstd_ok, b, 3)
                        normalise(hs, [xn[:, c * D:(c + 1) * D] for c in range(NC)], cmv, crs).then_inc(xn4_ok.sem, 1)
                def weights(b, slot, link):
                    if slot == 0:
                        need(dve, aff_ok, b, 1)
                        link(nc.vector.tensor_tensor(rscore[:], aff[:], eb[:].unsqueeze(1).broadcast_to([P, NC, E1]), ALU.add))
                        dve.sem_inc(waited.sem, 1)
                        for c in range(NC):
                            last = nc.vector.max(top3[:, c, :], rscore[:, c, :])
                        link(last)
                    if slot == 1:
                        dve.sem_inc(waited.sem, 1)
                        for c in range(NC):
                            last = nc.vector.max_index(idx3[:, c, :], top3[:, c, :], rscore[:, c, :])
                        link(last)
                        link(nc.vector.tensor_copy(idf3[:], idx3[:, :, 0:3]))
                        io = iota[:].unsqueeze(1).broadcast_to([P, NC, E1])
                        for k in range(3):
                            last = nc.vector.tensor_tensor(eq3[:, k], io, bc(idf3[:, :, k], E1), ALU.is_equal)
                        link(last)
                    if slot == 2:
                        link(nc.vector.tensor_tensor(sel[:], eq3[:, 0], eq3[:, 1], ALU.add))
                        link(nc.vector.tensor_tensor(sel[:], sel[:], eq3[:, 2], ALU.add))
                        link(nc.vector.tensor_tensor(sel[:], sel[:], aff[:], ALU.mult))
                        link(nc.vector.tensor_reduce(asum[:], sel[:], AX.X, ALU.add))
                        link(nc.vector.tensor_scalar(asum[:], asum[:], 1e-9, None, ALU.add))
                        link(nc.vector.reciprocal(ainv[:], asum[:]))
                        link(nc.vector.tensor_tensor(combm[:], sel[:], bc(ainv[:], E1), ALU.mult))

                def hidden(b, e):
                    need(dve, gate_ok, b, e + 1)
                    need(dve, z_full, b, e - 2 if e > 2 else min(e - 1, 0))
                    nc.vector.tensor_tensor(hid1[:, e % 3, 0:S], gate[:, e % 2, :], gu_ps[2 * (e % 2) + 1][:, 0:S], ALU.mult)\
                        .then_inc(hid1_ok.sem, 1)

                def add_expert(b, e):
                    need(dve, z_full, b, e + 1)
                    need(dve, z_free, b, e)
                    if e == 0:
                        hb = h_all[:, bass.ds(b * SP, SP)]
                        nc.vector.tensor_tensor(hb, hb, z_ps[0][:, 0:SP], ALU.add).then_inc(z_free.sem, 1)
                        return
                    for c in range(NC):
                        last = nc.vector.scalar_tensor_tensor(h1(b, c), z_ps[e % 2][:, c * D:(c + 1) * D], combm[:, c, e - 1:e], h1(b, c),
                                                              ALU.mult, ALU.add)
                    last.then_inc(z_free.sem, 1)

                def step(last, moe, two, one, zero):
                    alink, blink, hlink, glink = (Chain(dve, a_link, one), Chain(dve, b_link, two), Chain(dve, h_link, moe),
                                                  Chain(dve, g_link, zero))
                    for e in range(NE):
                        if moe is not None:
                            hidden(moe, e)
                            if e == NE - 1 and two is not None:
                                need(dve, gu_full, moe, NE)
                        if e == NE - 1 and two is not None:
                            need(dve, xT_ok, two, 1)
                            blink(nc.vector.tensor_copy(x_hi[:], xT[:]))
                            nc.vector.tensor_tensor(x_lo[:], xT[:], x_hi[:].bitcast(FP32), ALU.subtract).then_inc(lin_ok.sem, 1)
                        if last is not None and e < 2:
                            add_expert(last, NE - 2 + e)
                        if moe is not None:
                            if e >= 2:
                                add_expert(moe, e - 2)
                            weights(moe, e, hlink)
                        if two is not None:
                            second_part(two, e, blink)
                        if one is not None:
                            first_part(one, e, alink)
                        if zero is not None:
                            group_norm(zero, e, glink)
                    if moe is not None:
                        hlink.end(h_link.per)
                    if two is not None:
                        blink.end(b_link.per)
                    if one is not None:
                        alink.end(a_link.per)
                    if zero is not None:
                        glink.end(g_link.per)

                step(None, None, None, None, 0)
                step(None, None, None, 0, 1)
                step(None, None, 0, 1, 2)
                dve.wait_ge(whi_ok.sem, 1)
                nc.vector.tensor_tensor(wgu_lo[:], wgu[:], wgu_hi[:].bitcast(FP32), ALU.subtract).then_inc(wlo_ok.sem, 1)
                step(None, 0, 1, 2, 3)
                with dve.Fori(0, B - 4) as b:
                    step(b, b + 1, b + 2, b + 3, b + 4)
                step(B - 4, B - 3, B - 2, B - 1, None)
                step(B - 3, B - 2, B - 1, None, None)
                step(B - 2, B - 1, None, None, None)
                add_expert(B - 1, NE - 2)
                add_expert(B - 1, NE - 1)


def decay_matrices():
    i = np.arange(S)
    diff = (i[:, None] - i[None, :]).astype(np.float64)
    dec = np.log(1.0 - 2.0 ** (-5.0 - np.arange(NH)))
    dm = np.where(diff[None] >= 0, np.exp(np.maximum(diff[None], 0) * dec[:, None, None]), 0.0)
    dm = (dm / np.sqrt(dm.sum(-1, keepdims=True))).astype(np.float32)
    dT = np.zeros((P, NH, NC, S), np.float32)
    sums = np.zeros((P, NC, NH), np.float32)
    for c in range(NC):
        dT[:ROWS[c], :, c, :] = dm[:, :, c * P:c * P + ROWS[c]].transpose(2, 0, 1)
        sums[:ROWS[c], c, :] = dm.sum(-1)[:, c * P:c * P + ROWS[c]].T
    return dT, sums


def kernel(**inputs):
    import concourse.bacc as _bacc
    from concourse.bass_utils import run_bass_kernel_spmd as _run

    x = {k: np.asarray(v) for k, v in inputs.items()}
    a = {}
    for k in ("txt", "L0_tok_b", "L0_tok_token", "L0_tok_pos", "L0_attn_b2", "L0_ffn_router_w", "L0_ffn_router_b", "L0_ffn_b2",
              "L1_attn_bk", "L1_attn_bv", "L1_attn_bg", "L1_attn_n0_g", "L1_attn_n0_b", "L1_attn_n1_g", "L1_attn_n1_b", "L1_ffn_expert_bias"):
        a[k] = x[k]
    px = x["x"].reshape(B, 3, N_PATCH, 14, N_PATCH, 14).transpose(0, 1, 3, 5, 2, 4).reshape(B, 588, S_IMG - 1)
    px = np.pad(px, ((0, 0), (0, KT * KR - 588), (1, 0)))
    a["patches"] = px.reshape(B, KT, KR, S_IMG).transpose(0, 2, 1, 3)
    a["tokw"] = np.pad(x["L0_tok_W"].T, ((0, KT * KR - 588), (0, 0))).reshape(KT, KR, D).transpose(1, 0, 2)
    a["wqkv0"] = np.stack([x["L0_attn_Wq"].T, x["L0_attn_Wk"].T, x["L0_attn_Wv"].T], 1)
    w1q = np.zeros((D, QG, P), np.float32)
    w2a = np.zeros((P, 24 + QG + 24), np.float32)
    for r in range(QG):
        w1q[:, r, r * AH:(r + 1) * AH] = x["L0_attn_W1"][:, :D].T
        w2a[r * AH:(r + 1) * AH, 24 + r] = x["L0_attn_W2"][0]
    a["w1q"], a["w2a"] = w1q, w2a
    a["w1k"] = np.tile(x["L0_attn_W1"][:, D:].T, (1, QG))
    a["b1a"] = np.tile(x["L0_attn_b1"].reshape(AH, 1), (QG, 1))
    a["w1e"] = x["L0_ffn_W1"].transpose(1, 0, 2)
    a["b1e"] = x["L0_ffn_b1"].reshape(E0 * FC, P).T
    a["w2e"] = x["L0_ffn_W2"].reshape(E0, FC, P, D).transpose(2, 0, 1, 3)
    a["wkvg"] = np.concatenate([x["L1_attn_wk"].T, x["L1_attn_wv"].T, x["L1_attn_wg"].T], 1)
    a["wq1"] = x["L1_attn_wq"].T
    a["bq1"] = x["L1_attn_bq"].reshape(D, 1)
    same = np.arange(D)[:, None] // HD == np.arange(D)[None, :] // HD
    a["bd"] = np.where(same, np.float32(HD ** -0.5), np.float32(0))
    a["bd8"] = a["bd"][:, ::HD]
    a["decay"], a["dsum"] = decay_matrices()
    a["wo"] = x["L1_attn_wo"].T
    a["bo"] = x["L1_attn_bo"].reshape(1, D)
    a["fc1"] = x["L1_attn_fc1_w"].T
    a["fc1b"] = x["L1_attn_fc1_b"].reshape(FC, P).T
    a["fc2"] = x["L1_attn_fc2_w"].T.reshape(FC, P, D).transpose(1, 0, 2)
    a["fc2b"] = x["L1_attn_fc2_b"].reshape(1, D)
    a["lng"] = x["L1_attn_ln_ffn_g"].reshape(FC, P).T
    a["lnb"] = x["L1_attn_ln_ffn_b"].reshape(FC, P).T
    a["gw"] = x["L1_ffn_gate_w"].T
    a["wgu"] = np.concatenate([x["L1_ffn_shared_gate_up"][None], x["L1_ffn_expert_gate_up"]]).transpose(2, 0, 1)
    a["wdn"] = np.concatenate([x["L1_ffn_shared_down"][None], x["L1_ffn_expert_down"]]).transpose(2, 0, 1)

    nc = _bacc.Bacc("TRN2", target_bir_lowering=False, num_devices=1)
    arrays, t = {}, {}
    for k, v in a.items():
        v = np.ascontiguousarray(v)
        arrays[f"in_{k}"] = v
        t[k] = nc.dram_tensor(f"in_{k}", v.shape, FP32, kind="ExternalInput").ap()
    out = nc.dram_tensor("out_0", (B, S, D), FP32, kind="ExternalOutput").ap()
    program(nc, t, out, STOP)
    r = _run(nc, [arrays], core_ids=[0])
    return r.results[0]["out_0"]


STOP = None
```

```python
import math
from contextlib import ExitStack

import numpy as np
import concourse.bass as bass
from concourse import mybir

FP32 = mybir.dt.float32
FP32R = mybir.dt.float32r
U32 = mybir.dt.uint32
ALU = mybir.AluOpType
ACT = mybir.ActivationFunctionType
AX = mybir.AxisListType

B = 16
D = 128
N_PATCH, S_IMG, S_TXT = 14, 197, 128
S = S_IMG + S_TXT
P = 128
NC = (S + P - 1) // P
SP = NC * P
LAST = S - (NC - 1) * P
S2 = S + S % 2
ROWS = [P] * (NC - 1) + [LAST]
KT, KR = 5, 118
E0, F0 = 8, 512
FC = F0 // P
E1, F1 = 16, 128
NH, HD = 8, 16
AH = 16
QG = P // AH
NG = (S + QG - 1) // QG
FF = 512
EPS = 1e-5
SCALE = 1.0 / math.sqrt(D)
NTH = 10
SLOT_ENDS = (0, 4, 5, 10, 15, 20, 25, 30, 35, NG)
SLOTS = {(n // 2, n % 2): (SLOT_ENDS[n - 1], SLOT_ENDS[n]) for n in range(1, len(SLOT_ENDS))}


BY_ACT = (3, 5, 7, 9)


class Signal:

    def __init__(self, sem, per, start=0):
        self.sem, self.per, self.start = sem, per, start

    def at(self, b, k):
        return b * self.per + k + self.start


def need(eng, sig, b, k, alone=None):
    v = sig.at(b, k)
    if not (isinstance(v, int) and v <= 0):
        eng.wait_ge(sig.sem, v)
        if alone is not None:
            eng.sem_inc(alone.sem, 1)


class Chain:

    def __init__(self, eng, sig, b):
        self.eng, self.sig, self.b, self.n = eng, sig, b, 0

    def __call__(self, ins):
        self.n += 1
        ins.then_inc(self.sig.sem, 1)
        self.eng.wait_ge(self.sig.sem, self.sig.at(self.b, self.n))

    def end(self, per):
        assert self.n == per, (self.n, per)
        return per


def program(nc, t, out):
    ctx = ExitStack()
    with ctx:
        def sb(name, shape, dt=FP32):
            return ctx.enter_context(nc.sbuf_tensor(name, shape, dt))

        def signal(name, per=1, start=0):
            return Signal(ctx.enter_context(nc.semaphore(name)), per, start)

        h_all = sb("h_all", [P, B * SP])
        OW = D + NH
        v_all = sb("v_all", [P, B * SP])
        src_d = nc.dram_tensor("src_d", (B, P, SP), FP32, kind="Internal").ap()
        g_d = nc.dram_tensor("g_d", (B, P, SP), FP32, kind="Internal").ap()
        o_d = nc.dram_tensor("o_d", (B, P, NC * OW), FP32, kind="Internal").ap()
        src_saved, g_saved, o_saved = signal("src_saved", 16), signal("g_saved", 16), signal("o_saved", 16)
        ident = sb("ident", [P, P])
        ones = sb("ones", [P, P])
        neghalf = sb("neghalf", [P, 24])
        iota = sb("iota", [P, 16])
        w_moe0 = sb("w_moe0", [P, 2 * E0 * F0])
        w2 = w_moe0[:, 0:E0 * F0].rearrange("p (e c d) -> p e c d", e=E0, c=FC)
        w1_in = w_moe0[:, E0 * F0:].rearrange("p (e f) -> p e f", e=E0)
        hid = w_moe0[:, E0 * F0:E0 * F0 + 2 * FC * SP].rearrange("p (k f n) -> p k f n", k=2, f=FC)
        DEC = [sum(S - k * P for k in range(c)) for c in range(NC + 1)]
        decay = w_moe0[:, 0:NH * DEC[NC]].rearrange("p (h i) -> p h i", h=NH)

        xn = sb("xn", [P, SP])
        st = sb("st", [P, NC, 6]); mv = sb("mv", [P, NC, 2]); ve = sb("ve", [P, NC]); rs = sb("rs", [P, NC])
        combm = sb("combm", [P, NC, E1])

        banks = [ctx.enter_context(nc.psum_tensor(f"bank{i}", [P, 512], FP32)) for i in range(8)]
        misc = banks[0:2]

        w_tok, w_att, w_moe, w_l1, txt_in, dec_in = (signal(n) for n in ("w_tok", "w_att", "w_moe", "w_l1", "txt_in", "dec_in"))
        base_in, consts, ident_step = (signal(n) for n in ("base_in", "consts", "ident_step"))
        consts_v, setup_v, setup_pe = signal("consts_v"), signal("setup_v"), signal("setup_pe")
        waited = signal("waited")
        patch_in, patch_used = signal("patch_in", 16), signal("patch_used")

        def h1(b, c):
            return h_all[:, bass.ds(b * SP + c * P, P)]

        def row(x, b):
            return x[bass.ds(b, 1)].rearrange("a p n -> (a p) n")

        def token_stats(x, st, mv, link):
            nc.vector.sem_inc(waited.sem, 1)
            for c in range(NC):
                last = nc.vector.bn_stats(st[:, c, :], x[c])
            link(last)
            nc.vector.sem_inc(waited.sem, 1)
            for c in range(NC):
                last = nc.vector.bn_aggr(mv[:, c, :], st[:, c, :])
            link(last)

        with ExitStack() as l0:
            def sb0(name, shape, dt=FP32):
                return l0.enter_context(nc.sbuf_tensor(name, shape, dt))

            b1 = sb0("b1", [P, E0 * FC])
            b2 = sb0("b2", [E0, D])
            rw = sb0("rw", [P, E0])
            rb = sb0("rb", [P, E0])
            tokw = sb0("tokw", [KR, KT, D])
            base = sb0("base", [P, 2, D])
            base_add = sb0("base_add", [P, 2, D])
            wqkv = sb0("wqkv", [P, 3, D])
            w1q = sb0("w1q", [P, QG, P])
            w1k = sb0("w1k", [P, P])
            hb1 = sb0("hb1", [P, 1])
            w2s = sb0("w2s", [P, 24 + QG + 24])
            b2a = sb0("b2a", [P, 1])
            wkvg = sb0("wkvg", [P, 3 * D])
            bkvg = sb0("bkvg", [P, 3 * D])
            wq1 = sb0("wq1", [P, D])
            bq1 = sb0("bq1", [P, 1])
            bd = sb0("bd", [P, D])
            bd8 = sb0("bd8", [P, NH])
            xTm = sb0("xTm", [P, SP])
            combT = sb0("combT", [E0, SP])
            w1_hi, w1_lo = sb0("w1_hi", [P, E0, F0], FP32R), sb0("w1_lo", [P, E0, F0], FP32R)
            xm_hi, xm_lo = sb0("xm_hi", [P, SP], FP32R), sb0("xm_lo", [P, SP], FP32R)
            src_st = sb0("src_st", [P, SP]); srcT = sb0("srcT", [P, SP])
            k_st = sb0("k_st", [P, NC, D]); v_st = sb0("v_st", [P, NC, D + 1])
            g_st = sb0("g_st", [P, NC, D]); qrT = sb0("qrT", [P, SP])
            kv_st = sb0("kv_st", [P, OW]); ksum = sb0("ksum", [P, 1])
            patch = sb0("patch", [KR, KT, S_IMG])
            xf = sb0("xf", [P, SP]); xfT = sb0("xfT", [P, SP])
            st_f = sb0("st_f", [P, NC, 6]); mv_f = sb0("mv_f", [P, NC, 2]); ve_f = sb0("ve_f", [P, NC]); rs_f = sb0("rs_f", [P, NC])
            qT = sb0("qT", [P, SP]); qTs = sb0("qTs", [P, SP]); kT = sb0("kT", [P, S])
            v_sb = sb0("v_sb", [P, NC, D])
            hk = sb0("hk", [P, S]); hq = sb0("hq", [P, NG])
            th = sb0("th", [P, NTH, S])
            sc = sb0("sc", [P, NC, S]); smax = sb0("smax", [P, NC]); nmax = sb0("nmax", [P, NC])
            rsum = sb0("rsum", [P, NC]); rinv = sb0("rinv", [P, NC])
            pT = sb0("pT", [P, NC, SP])
            lg = sb0("lg", [P, NC, E0]); lmax = sb0("lmax", [P, NC]); ex = sb0("ex", [P, NC, E0])
            esum = sb0("esum", [P, NC]); einv = sb0("einv", [P, NC]); prob = sb0("prob", [P, NC, E0])
            top = sb0("top", [P, NC, 8]); tidx = sb0("tidx", [P, NC, 8], U32); tidf = sb0("tidf", [P, NC, 2])
            wsum = sb0("wsum", [P, NC]); winv = sb0("winv", [P, NC]); wt = sb0("wt", [P, NC, 2])
            eq = sb0("eq", [P, 2, NC, E0]); cp = sb0("cp", [P, 2, NC, E0])
            sc_ps, h_ps, y_ps, r_ps = banks[2:4], banks[4:6], banks[6], banks[7]

            misc_full, misc_free = signal("misc_full", 5), signal("misc_free", 5)
            m_full, m_free = signal("m_full", 3), signal("m_free", 3)
            f_full, f_free = signal("f_full", 6), signal("f_free", 6)
            fvar_ok, frstd_ok, xf_ok = signal("fvar_ok"), signal("frstd_ok"), signal("xf_ok")
            var_ok, rstd_ok, xn_ok = signal("var_ok"), signal("rstd_ok"), signal("xn_ok")
            hbias_ok, tanh_ok, est_ok = signal("hbias_ok"), signal("tanh_ok", NG), signal("est_ok", NG)
            sc_free = signal("sc_free", NC)
            nmax_ok, exp_ok = signal("nmax_ok"), signal("exp_ok")
            lg_ok, ex_ok, comb_ok, in_ok = signal("lg_ok"), signal("ex_ok"), signal("comb_ok"), signal("in_ok")
            hid_full, hid_ok = signal("hid_full", E0 * FC), signal("hid_ok", E0 * FC, 2)
            y_full, y_free = signal("y_full", E0, 2), signal("y_free", E0, 1)
            a_chain, f_chain, m_chain = signal("a_chain", 3), signal("f_chain", 2), signal("m_chain", 12)
            l0_done = signal("l0_done")
            r_chain, rvar_ok, rrstd_ok = signal("r_chain", 3), signal("rvar_ok"), signal("rrstd_ok")
            src_ok, v_saved, o_ok = signal("src_ok"), signal("v_saved"), signal("o_ok")
            parts_free = signal("parts_free", 1, 1)
            o_st = sb0("o_st", [P, NC * OW])
            w1hi_ok, w1split, w1lo_ok = signal("w1hi_ok"), signal("w1split"), signal("w1lo_ok")
            r_full, r_free = signal("r_full", 6), signal("r_free", 6, 1)
            kvg_ok = signal("kvg_ok")
            st_r = sb0("st_r", [P, NC, 6]); mv_r = sb0("mv_r", [P, NC, 2]); ve_r = sb0("ve_r", [P, NC]); rs_r = sb0("rs_r", [P, NC])

            block = l0.enter_context(nc.Block())

            @block.sync
            def _(sp):
                sp.dma_start(tokw[:], t["tokw"]).then_inc(w_tok.sem, 16)
                sp.dma_start(patch[:], t["patches"][0]).then_inc(patch_in.sem, 16)
                sp.dma_start(base[:, 0, :], t["L0_tok_pos"][0:P, :]).then_inc(w_tok.sem, 16)
                sp.dma_start(base[0:S_IMG - P, 1, :], t["L0_tok_pos"][P:S_IMG, :]).then_inc(w_tok.sem, 16)
                sp.dma_start(base_add[:, 0, :], t["L0_tok_b"].partition_broadcast(P)).then_inc(base_in.sem, 16)
                sp.dma_start(base_add[:, 1, :], t["L0_tok_b"].partition_broadcast(P)).then_inc(w_tok.sem, 16)
                sp.wait_ge(base_in.sem, 16)
                sp.dma_start(base_add[0:1, 0, :], t["L0_tok_token"]).then_inc(w_tok.sem, 16)
                sp.wait_ge(consts_v.sem, 1)
                txt, hv = t["txt"], h_all[:, :].rearrange("p (b c d) -> p b c d", b=B, c=NC)
                sp.dma_start(hv[S_IMG - P:P, :, 1, :], txt[:, 0:2 * P - S_IMG, :].rearrange("b s d -> s b d")).then_inc(txt_in.sem, 16)
                sp.dma_start(hv[0:LAST, :, 2, :], txt[:, 2 * P - S_IMG:, :].rearrange("b s d -> s b d")).then_inc(txt_in.sem, 16)
                sp.dma_start(wqkv[:], t["wqkv0"]).then_inc(w_att.sem, 16)
                for dst, src in ((w1q[:], t["w1q"]), (w1k[:], t["w1k"]), (hb1[:], t["b1a"]), (w2s[:], t["w2a"])):
                    sp.dma_start(dst, src).then_inc(w_att.sem, 16)
                sp.dma_start(b2a[:], t["L0_attn_b2"].partition_broadcast(P)).then_inc(w_att.sem, 16)
                sp.dma_start(rw[:], t["L0_ffn_router_w"]).then_inc(w_att.sem, 16)
                sp.dma_start(rb[:], t["L0_ffn_router_b"].partition_broadcast(P)).then_inc(w_att.sem, 16)
                sp.dma_start(w1_in, t["w1e"]).then_inc(w_moe.sem, 16)
                sp.dma_start(b1[:], t["b1e"]).then_inc(w_moe.sem, 16)
                sp.dma_start(w2, t["w2e"]).then_inc(w_moe.sem, 16)
                sp.dma_start(b2[:], t["L0_ffn_b2"]).then_inc(w_moe.sem, 16)
                for dst, src in ((wkvg[:], t["wkvg"]), (wq1[:], t["wq1"]), (bq1[:], t["bq1"]), (bd[:], t["bd"]), (bd8[:], t["bd8"]),
                                 (bkvg[:, 0:D], t["L1_attn_bk"].partition_broadcast(P)),
                                 (bkvg[:, D:2 * D], t["L1_attn_bv"].partition_broadcast(P)),
                                 (bkvg[:, 2 * D:], t["L1_attn_bg"].partition_broadcast(P))):
                    sp.dma_start(dst, src).then_inc(w_l1.sem, 16)
                with sp.Fori(1, B) as b:
                    sp.wait_ge(patch_used.sem, b)
                    sp.dma_start(patch[:], t["patches"][bass.ds(b, 1)].rearrange("b k c s -> k (b c) s")).then_inc(patch_in.sem, 16)
                sp.wait_ge(w_l1.sem, 16 * 8)
                sp.wait_ge(l0_done.sem, 1)
                sp.dma_start(decay, t["decay"]).then_inc(dec_in.sem, 16)

            @block.gpsimd
            def _(pool):
                nc.gpsimd.memset(neghalf[:], -0.5).then_inc(consts.sem, 1)
                nc.gpsimd.memset(ident[:], 0.0).then_inc(ident_step.sem, 1)
                nc.gpsimd.iota(iota[:], pattern=[[1, 16]], base=0, channel_multiplier=0, allow_small_or_imprecise_dtypes=True)
                pool.wait_ge(ident_step.sem, 1)
                nc.gpsimd.affine_select(out=ident[:], in_=ident[:], compare_op=ALU.not_equal, fill=1.0, base=0,
                                        pattern=[[-1, P]], channel_multiplier=1).then_inc(consts.sem, 1)

                def step(att, front, ret):
                    if ret is not None:
                        need(pool, rvar_ok, ret, 1)
                        nc.gpsimd.tensor_tensor(rs_r[:], ve_r[:], neghalf[:, 0:NC], ALU.pow).then_inc(rrstd_ok.sem, 1)
                        need(pool, src_ok, ret, 1, waited)
                        pool.dma_start(row(src_d, ret), src_st[:]).then_inc(src_saved.sem, 16)
                    if front is not None:
                        need(pool, fvar_ok, front, 1)
                        nc.gpsimd.tensor_tensor(rs_f[:], ve_f[:], neghalf[:, 0:NC], ALU.pow).then_inc(frstd_ok.sem, 1)
                    if ret is not None:
                        need(pool, kvg_ok, ret, 1, waited)
                        pool.dma_start(row(g_d, ret), g_st[:].rearrange("p c d -> p (c d)")).then_inc(g_saved.sem, 16)
                    if att is not None:
                        need(pool, var_ok, att, 1)
                        nc.gpsimd.tensor_tensor(rs[:], ve[:], neghalf[:, 0:NC], ALU.pow).then_inc(rstd_ok.sem, 1)
                    if ret is not None:
                        nc.gpsimd.tensor_copy(v_all[:, bass.ds(ret * SP, SP)].rearrange("p (c d) -> p c d", c=NC), v_st[:, :, 0:D])\
                            .then_inc(v_saved.sem, 1)
                        need(pool, o_ok, ret, 1, waited)
                        pool.dma_start(row(o_d, ret), o_st[:]).then_inc(o_saved.sem, 16)
                        for sig in (src_saved, g_saved, o_saved):
                            need(pool, sig, ret, 16)
                        need(pool, v_saved, ret, 1, parts_free)

                pool.sem_inc(parts_free.sem, parts_free.start)
                step(None, 0, None)
                step(0, 1, None)
                step(1, 2, None)
                with pool.Fori(0, B - 3) as b:
                    step(b + 2, b + 3, b)
                step(B - 1, None, B - 3)
                step(None, None, B - 2)
                step(None, None, B - 1)
                for sig in (src_saved, g_saved, o_saved):
                    pool.wait_ge(sig.sem, sig.at(B, 0))

            @block.tensor
            def _(pe):
                def claim(b, n):
                    if n == 0:
                        need(pe, misc_free, b, 0)
                        need(pe, m_free, b, 0)
                    else:
                        need(pe, misc_free, b, n - 1)
                    return misc[n % 2]

                def claim_f(b, n):
                    need(pe, f_free, b, n - 1 if n else 0)
                    if n < 2 and not (isinstance(b, int) and b == 0):
                        need(pe, sc_free, b, n - 1)
                    return sc_ps[1 - n % 2]

                def tokens(b):
                    need(pe, patch_in, b, 16)
                    m = claim_f(b, 0)
                    for c, rows in ((0, P), (1, S_IMG - P)):
                        for k in range(KT):
                            last = nc.tensor.matmul(m[0:rows, c * D:(c + 1) * D], patch[:, k, c * P:c * P + rows], tokw[:, k, :],
                                                    start=(k == 0), stop=(k == KT - 1))
                            if c == 1 and k == KT - 1:
                                last.then_inc(f_full.sem, 1)
                    pe.drain().then_inc(patch_used.sem, 1)

                def front(b, slot):
                    if slot == (5, 0) and not (isinstance(b, int) and b == 0):
                        tokens(b)
                    if slot == (6, 0):
                        need(pe, xf_ok, b, 1)
                        m = claim_f(b, 1)
                        for c in range(NC):
                            last = nc.tensor.transpose(m[:, c * P:(c + 1) * P], xf[:, c * D:(c + 1) * D], ident[:])
                        last.then_inc(f_full.sem, 1)
                    if slot == (6, 1):
                        need(pe, f_free, b, 2)
                        for n in (2, 3):
                            m = claim_f(b, n)
                            nc.tensor.matmul(m[:, 0:S], wqkv[:, n - 2, :], xfT[:, 0:S], start=True, stop=True).then_inc(f_full.sem, 1)
                    if slot == (7, 0):
                        m = claim_f(b, 4)
                        for c in range(NC):
                            last = nc.tensor.matmul(m[:, c * D:(c + 1) * D], xfT[:, c * P:(c + 1) * P], wqkv[:, 2, :], start=True, stop=True)
                        last.then_inc(f_full.sem, 1)
                    if slot == (7, 1):
                        need(pe, f_free, b, 4)
                        m = claim_f(b, 5)
                        nc.tensor.matmul(m[:, 0:S], w1k[:], kT[:], start=True, stop=True)
                        for r in range(QG):
                            last = nc.tensor.matmul(m[:, S:S + NG], w1q[:, r, :], qT[:, r:r + QG * (NG - 1) + 1:QG],
                                                    start=(r == 0), stop=(r == QG - 1))
                        last.then_inc(f_full.sem, 1)

                def score_groups(b, g0, g1):
                    for g in range(g0, g1):
                        c, gl = g // 16, g % 16
                        if gl == 0:
                            if c < 2:
                                need(pe, f_free, b, 6)
                            else:
                                need(pe, sc_free, b, c - 1)
                            nc.tensor.matmul(sc_ps[c % 2][:, 0:S], qTs[:, c * P:(c + 1) * P], kT[:], start=True, stop=True)
                        need(pe, tanh_ok, b, g + 1)
                        j, off = gl // 4, 24 - QG * (gl % 4)
                        last = nc.tensor.matmul(sc_ps[c % 2][32 * j:32 * j + 32, 0:S], w2s[:, off:off + 32], th[:, g % NTH, :],
                                                start=False, stop=True, skip_group_check=True)
                        last.then_inc(est_ok.sem, 1)

                def attend(b, slot):
                    if slot in SLOTS:
                        score_groups(b, *SLOTS[slot])
                    if slot == (6, 0):
                        need(pe, exp_ok, b, 1)
                        for kc in range(NC):
                            m = claim(b, kc)
                            for qc in range(NC):
                                last = nc.tensor.transpose(m[0:ROWS[kc], qc * P:(qc + 1) * P], sc[:, qc, kc * P:kc * P + ROWS[kc]], ident[:])
                            last.then_inc(misc_full.sem, 1)
                    if slot == (6, 1):
                        need(pe, misc_free, b, 3)
                        m = claim(b, 3)
                        for qc in range(NC):
                            for kc in range(NC):
                                last = nc.tensor.matmul(m[:, qc * D:(qc + 1) * D], pT[0:ROWS[kc], kc, qc * P:(qc + 1) * P],
                                                        v_sb[0:ROWS[kc], kc, :], start=(kc == 0), stop=(kc == NC - 1))
                        last.then_inc(misc_full.sem, 1)
                    if slot == (7, 1):
                        need(pe, xn_ok, b, 1)
                        m = claim(b, 4)
                        for c in range(NC):
                            last = nc.tensor.transpose(m[:, c * P:(c + 1) * P], xn[:, c * D:(c + 1) * D], ident[:])
                        last.then_inc(misc_full.sem, 1)

                def router(b):
                    need(pe, in_ok, b, 1)
                    for c in range(NC):
                        last = nc.tensor.matmul(misc[1][:, c * E0:(c + 1) * E0], xTm[:, c * P:(c + 1) * P], rw[:], start=True, stop=True)
                    last.then_inc(m_full.sem, 1)

                def up(b, e, half):
                    if e == 0:
                        need(pe, in_ok, b, 1)
                    for f in (2 * half, 2 * half + 1):
                        need(pe, hid_ok, b, FC * e + f - 1)
                        for n, (w, x) in enumerate(((w1_hi, xm_hi), (w1_hi, xm_lo), (w1_lo, xm_hi))):
                            last = nc.tensor.matmul(h_ps[f % 2][:, 0:S2], w[:, e, f * P:(f + 1) * P], x[:, 0:S2], start=(n == 0), stop=(n == 2))
                        last.then_inc(hid_full.sem, 1)

                def down(b, e):
                    need(pe, hid_ok, b, FC * (e + 1))
                    need(pe, y_free, b, e)
                    for c in range(NC):
                        for f in range(FC):
                            last = nc.tensor.matmul(y_ps[:, c * D:(c + 1) * D], hid[:, e % 2, f, c * P:(c + 1) * P], w2[:, e, f, :],
                                                    start=(f == 0), stop=(f == FC - 1))
                    last.then_inc(y_full.sem, 1)

                def biases(b, k):
                    if k == 0:
                        need(pe, comb_ok, b, 1)
                        for c in range(NC):
                            last = nc.tensor.transpose(misc[0][0:E0, c * P:(c + 1) * P], combm[:, c, 0:E0], ident[:])
                        last.then_inc(m_full.sem, 1)
                    if k == 1:
                        need(pe, m_free, b, 2)
                        for c in range(NC):
                            last = nc.tensor.matmul(misc[1][:, c * D:(c + 1) * D], combT[:, c * P:(c + 1) * P], b2[:], start=True, stop=True)
                        last.then_inc(m_full.sem, 1)

                def retain(b, slot):
                    if slot == (1, 1):
                        need(pe, src_ok, b, 1)
                        need(pe, r_free, b, 0)
                        for c in range(NC):
                            last = nc.tensor.transpose(r_ps[:, c * P:(c + 1) * P], src_st[:, c * D:(c + 1) * D], ident[:])
                        last.then_inc(r_full.sem, 1)
                    for c in range(NC):
                        if slot == (c + 2, 1):
                            need(pe, r_free, b, c + 1)
                            nc.tensor.matmul(r_ps[:, 0:3 * D], srcT[:, c * P:(c + 1) * P], wkvg[:], start=True, stop=True).then_inc(r_full.sem, 1)
                    if slot == (5, 1):
                        need(pe, r_free, b, 4)
                        nc.tensor.matmul(r_ps[:, 0:S], wq1[:], srcT[:, 0:S], start=True, stop=True)
                        for c in range(NC):
                            last = nc.tensor.matmul(r_ps[:, S:S + D + 1], k_st[0:ROWS[c], c, :], v_st[0:ROWS[c], c, :],
                                                    start=(c == 0), stop=(c == NC - 1))
                        last.then_inc(r_full.sem, 1)
                    if slot == (6, 1):
                        need(pe, r_free, b, 5)
                        for c in range(NC):
                            last = nc.tensor.matmul(r_ps[:, c * OW:(c + 1) * OW], qrT[:, c * P:(c + 1) * P], kv_st[:], start=True, stop=True)
                        last.then_inc(r_full.sem, 1)

                def step(moe, att, fro, ret):
                    for e in range(E0):
                        for k in range(2):
                            if moe is not None:
                                up(moe, e, k)
                                if k == 1 and e:
                                    down(moe, e - 1)
                                if (e, k) == (0, 0):
                                    router(moe)
                                if (e, k) in ((2, 0), (2, 1)):
                                    biases(moe, k)
                            if att is not None:
                                attend(att, (e, k))
                            if fro is not None:
                                front(fro, (e, k))
                            if ret is not None:
                                retain(ret, (e, k))
                    if moe is not None:
                        down(moe, E0 - 1)

                pe.sem_inc(y_full.sem, y_full.start)
                pe.wait_ge(w_tok.sem, 16 * 5)
                pe.wait_ge(consts.sem, 2)
                tokens(0)
                pe.wait_ge(w_att.sem, 16 * 8)
                pe.wait_ge(consts_v.sem, 2)
                step(None, None, 0, None)
                step(None, 0, 1, None)
                pe.wait_ge(w_moe.sem, 16 * 4)
                pe.wait_ge(w1lo_ok.sem, 1)
                pe.wait_ge(w_l1.sem, 16 * 8)
                step(0, 1, 2, None)
                with pe.Fori(0, B - 3) as b:
                    step(b + 1, b + 2, b + 3, b)
                step(B - 2, B - 1, None, B - 3)
                step(B - 1, None, None, B - 2)
                pe.drain().then_inc(l0_done.sem, 1)
                step(None, None, None, B - 1)

            @block.scalar
            def _(act):
                def attend(b, slot):
                    n = 2 * slot[0] + slot[1] + 1
                    for g in range(*SLOTS.get((n // 2, n % 2), (0, 0))):
                        if g == 0:
                            need(act, hbias_ok, b, 1)
                        if g >= NTH:
                            need(act, est_ok, b, g - NTH + 1)
                        else:
                            need(act, est_ok, b, 0)
                        nc.scalar.activation(th[:, g % NTH, :], hk[:], ACT.Tanh, bias=hq[:, g:g + 1]).then_inc(tanh_ok.sem, 1)
                    if slot == (5, 0):
                        need(act, nmax_ok, b, 1)
                        need(act, misc_free, b, 0)
                        for c in range(NC):
                            last = nc.scalar.activation(sc[:, c, :], sc[:, c, :], ACT.Exp, bias=nmax[:, c:c + 1],
                                                        accum_out=rsum[:, c:c + 1])
                        last.then_inc(exp_ok.sem, 1)

                def route(b):
                    need(act, lg_ok, b, 1)
                    nc.scalar.activation(ex[:], lg[:], ACT.Exp).then_inc(ex_ok.sem, 1)

                def gelu(b, e, half):
                    need(act, y_full, b, e - 1)
                    for f in (2 * half, 2 * half + 1):
                        need(act, hid_full, b, FC * e + f + 1)
                        nc.scalar.activation(hid[:, e % 2, f, 0:S], h_ps[f % 2][:, 0:S], ACT.Gelu, bias=b1[:, e * FC + f:e * FC + f + 1])\
                            .then_inc(hid_ok.sem, 1)

                def step(moe, att):
                    for e in range(E0):
                        for k in range(2):
                            if moe is not None:
                                gelu(moe, e, k)
                                if (e, k) == (0, 1):
                                    route(moe)
                            if att is not None:
                                attend(att, (e, k))

                act.sem_inc(hid_ok.sem, hid_ok.start)
                act.wait_ge(consts_v.sem, 2)
                step(None, 0)
                act.wait_ge(w_moe.sem, 16 * 4)
                nc.scalar.activation(w1_hi[:], w1_in, ACT.Copy).then_inc(w1hi_ok.sem, 1)
                act.wait_ge(w1lo_ok.sem, 1)
                step(0, 1)
                with act.Fori(1, B - 1) as b:
                    step(b, b + 1)
                step(B - 1, None)

            @block.vector
            def _(dve):
                dve.sem_inc(y_free.sem, y_free.start)
                nc.vector.memset(h_all[64:P, :].rearrange("p (b c d) -> p b c d", b=B, c=NC)[:, :, NC - 1, :], 0.0).then_inc(consts_v.sem, 1)
                nc.vector.memset(ones[:], 1.0)
                nc.vector.memset(qT[:, S:SP], 0.0)
                nc.vector.memset(qTs[:, S:SP], 0.0)
                nc.vector.memset(qrT[:, S:SP], 0.0)
                dve.sem_inc(r_free.sem, r_free.start)
                nc.vector.memset(v_st[:], 1.0).then_inc(consts_v.sem, 1)
                dve.wait_ge(w_tok.sem, 16 * 5)
                nc.vector.tensor_tensor(base[:, 0, :], base[:, 0, :], base_add[:, 0, :], ALU.add)
                nc.vector.tensor_tensor(base[0:S_IMG - P, 1, :], base[0:S_IMG - P, 1, :], base_add[0:S_IMG - P, 1, :], ALU.add)\
                    .then_inc(consts_v.sem, 1)
                dve.wait_ge(consts_v.sem, 3)
                dve.wait_ge(txt_in.sem, 32)
                dve.wait_ge(consts.sem, 2)

                def attend(b, slot, link):
                    for c, at in ((0, (2, 1)), (1, (4, 0)), (2, (5, 0))):
                        if slot == at:
                            need(dve, est_ok, b, min(16 * (c + 1), NG))
                            need(dve, misc_full, b, 0)
                            nc.vector.tensor_scalar(sc[:, c, :], sc_ps[c % 2][:, 0:S], b2a[:], None, ALU.add, ALU.max,
                                                    accum_out=smax[:, c:c + 1]).then_inc(sc_free.sem, 1)
                    if slot == (5, 0):
                        need(dve, sc_free, b, NC)
                        nc.vector.tensor_scalar(nmax[:], smax[:], -1.0, None, ALU.mult).then_inc(nmax_ok.sem, 1)
                    if slot == (6, 0):
                        for kc in range(NC):
                            need(dve, misc_full, b, kc + 1)
                            nc.vector.tensor_copy(pT[0:ROWS[kc], kc, :], misc[kc % 2][0:ROWS[kc], 0:SP]).then_inc(misc_free.sem, 1)
                    if slot == (6, 1):
                        need(dve, exp_ok, b, 1)
                        link(nc.vector.reciprocal(rinv[:], rsum[:]))
                        need(dve, misc_full, b, 4)
                        for c in range(NC):
                            last = nc.vector.scalar_tensor_tensor(h1(b, c), misc[1][:, c * D:(c + 1) * D], rinv[:, c:c + 1], h1(b, c), ALU.mult, ALU.add)
                        last.then_inc(misc_free.sem, 1)
                        need(dve, misc_free, b, 4)
                        token_stats([h1(b, c) for c in range(NC)], st, mv, link)
                        nc.vector.tensor_scalar(ve[:], mv[:, :, 1], EPS, None, ALU.add).then_inc(var_ok.sem, 1)
                    if slot == (7, 0):
                        need(dve, rstd_ok, b, 1)
                        for c in range(NC):
                            last = nc.vector.tensor_scalar(xn[:, c * D:(c + 1) * D], h1(b, c), mv[:, c, 0:1], rs[:, c:c + 1],
                                                           ALU.subtract, ALU.mult)
                        last.then_inc(xn_ok.sem, 1)
                    if slot == (7, 1):
                        need(dve, hid_full, b, 0)
                        need(dve, misc_full, b, 5)
                        nc.vector.tensor_copy(xm_hi[:], misc[0][:, 0:SP])
                        nc.vector.tensor_copy(xTm[:], misc[0][:, 0:SP]).then_inc(misc_free.sem, 1)
                        need(dve, misc_free, b, 5)
                        nc.vector.tensor_tensor(xm_lo[:], xTm[:], xm_hi[:].bitcast(FP32), ALU.subtract).then_inc(in_ok.sem, 1)

                def front(b, slot, link):
                    if slot == (5, 0):
                        need(dve, f_full, b, 1)
                        m = sc_ps[1]
                        nc.vector.tensor_tensor(h1(b, 0), m[:, 0:D], base[:, 0, :], ALU.add)
                        rows = S_IMG - P
                        nc.vector.tensor_tensor(h_all[0:rows, bass.ds(b * SP + P, P)], m[0:rows, D:2 * D], base[0:rows, 1, :], ALU.add)\
                            .then_inc(f_free.sem, 1)
                        need(dve, f_free, b, 1)
                        token_stats([h1(b, c) for c in range(NC)], st_f, mv_f, link)
                        nc.vector.tensor_scalar(ve_f[:], mv_f[:, :, 1], EPS, None, ALU.add).then_inc(fvar_ok.sem, 1)
                    if slot == (5, 1):
                        need(dve, frstd_ok, b, 1)
                        for c in range(NC):
                            last = nc.vector.tensor_scalar(xf[:, c * D:(c + 1) * D], h1(b, c), mv_f[:, c, 0:1], rs_f[:, c:c + 1],
                                                           ALU.subtract, ALU.mult)
                        last.then_inc(xf_ok.sem, 1)
                    if slot == (6, 0):
                        need(dve, f_full, b, 2)
                        nc.vector.tensor_copy(xfT[:], sc_ps[0][:, 0:SP]).then_inc(f_free.sem, 1)
                    if slot == (6, 1):
                        if isinstance(b, int) and b == 0:
                            dve.wait_ge(w_att.sem, 16 * 8)
                        need(dve, f_full, b, 3)
                        nc.vector.tensor_copy(qT[:, 0:S], sc_ps[1][:, 0:S])
                        nc.vector.tensor_scalar(qTs[:, 0:S], sc_ps[1][:, 0:S], SCALE, None, ALU.mult).then_inc(f_free.sem, 1)
                        need(dve, f_full, b, 4)
                        nc.vector.tensor_copy(kT[:], sc_ps[0][:, 0:S]).then_inc(f_free.sem, 1)
                    if slot == (7, 0):
                        need(dve, f_full, b, 5)
                        nc.vector.tensor_copy(v_sb[:].rearrange("p c d -> p (c d)"), sc_ps[1][:, 0:SP]).then_inc(f_free.sem, 1)
                    if slot == (7, 1):
                        need(dve, f_full, b, 6)
                        need(dve, tanh_ok, b, 0)
                        nc.vector.tensor_copy(hk[:], sc_ps[0][:, 0:S])
                        nc.vector.tensor_scalar(hq[:], sc_ps[0][:, S:S + NG], hb1[:], None, ALU.add).then_inc(f_free.sem, 1)
                        need(dve, f_free, b, 6)
                        dve.sem_inc(hbias_ok.sem, 1)

                def bc(x, n):
                    return x.unsqueeze(2).broadcast_to([P, NC, n])

                def logits(b, link):
                    need(dve, m_full, b, 1)
                    m3 = misc[1][:, 0:NC * E0].rearrange("p (c e) -> p c e", c=NC)
                    rb3 = rb[:].unsqueeze(1).broadcast_to([P, NC, E0])
                    nc.vector.tensor_tensor(lg[:], m3, rb3, ALU.add).then_inc(m_free.sem, 1)
                    need(dve, m_free, b, 1)
                    link(nc.vector.tensor_reduce(lmax[:], lg[:], AX.X, ALU.max))
                    nc.vector.tensor_tensor(lg[:], lg[:], bc(lmax[:], E0), ALU.subtract).then_inc(lg_ok.sem, 1)

                def route(b, link):
                    need(dve, ex_ok, b, 1)
                    link(nc.vector.tensor_reduce(esum[:], ex[:], AX.X, ALU.add))
                    link(nc.vector.reciprocal(einv[:], esum[:]))
                    link(nc.vector.tensor_tensor(prob[:], ex[:], bc(einv[:], E0), ALU.mult))
                    dve.sem_inc(waited.sem, 1)
                    for c in range(NC):
                        last = nc.vector.max(top[:, c, :], prob[:, c, :])
                    link(last)
                    dve.sem_inc(waited.sem, 1)
                    for c in range(NC):
                        last = nc.vector.max_index(tidx[:, c, :], top[:, c, :], prob[:, c, :])
                    link(last)
                    nc.vector.tensor_copy(tidf[:], tidx[:, :, 0:2])
                    link(nc.vector.scalar_tensor_tensor(wsum[:], top[:, :, 0], 1.0, top[:, :, 1], ALU.mult, ALU.add))
                    link(nc.vector.tensor_scalar(wsum[:], wsum[:], 1e-9, None, ALU.add))
                    link(nc.vector.reciprocal(winv[:], wsum[:]))
                    link(nc.vector.tensor_tensor(wt[:], top[:, :, 0:2], bc(winv[:], 2), ALU.mult))
                    io = iota[:, 0:E0].unsqueeze(1).broadcast_to([P, NC, E0])
                    for k in range(2):
                        last = nc.vector.tensor_tensor(eq[:, k], io, bc(tidf[:, :, k], E0), ALU.is_equal)
                    link(last)
                    for k in range(2):
                        last = nc.vector.tensor_tensor(cp[:, k], eq[:, k], bc(wt[:, :, k], E0), ALU.mult)
                    link(last)
                    need(dve, y_free, b, 0)
                    nc.vector.tensor_tensor(combm[:, :, 0:E0], cp[:, 0], cp[:, 1], ALU.add).then_inc(comb_ok.sem, 1)

                def biases(b, k):
                    need(dve, m_full, b, 2 + k)
                    if k == 0:
                        nc.vector.tensor_copy(combT[:], misc[0][0:E0, 0:SP]).then_inc(m_free.sem, 1)
                    if k == 1:
                        need(dve, y_free, b, 2)
                        nc.vector.tensor_tensor(h_all[:, bass.ds(b * SP, SP)], h_all[:, bass.ds(b * SP, SP)], misc[1][:, 0:SP], ALU.add)\
                            .then_inc(m_free.sem, 1)
                        need(dve, m_free, b, 3)

                def add_expert(b, e):
                    if e == 0:
                        need(dve, comb_ok, b, 1)
                    need(dve, y_full, b, e + 1)
                    need(dve, y_free, b, e)
                    for c in range(NC):
                        last = nc.vector.scalar_tensor_tensor(h1(b, c), y_ps[:, c * D:(c + 1) * D], combm[:, c, e:e + 1], h1(b, c),
                                                              ALU.mult, ALU.add)
                    last.then_inc(y_free.sem, 1)

                def retain(b, slot, rlink):
                    if slot == (0, 0):
                        need(dve, y_free, b, E0, waited)
                        token_stats([h1(b, c) for c in range(NC)], st_r, mv_r, rlink)
                        nc.vector.tensor_scalar(ve_r[:], mv_r[:, :, 1], EPS, None, ALU.add).then_inc(rvar_ok.sem, 1)
                    if slot == (1, 0):
                        need(dve, rrstd_ok, b, 1)
                        need(dve, parts_free, b, 0)
                        for c in range(NC):
                            last = nc.vector.tensor_scalar(src_st[:, c * D:(c + 1) * D], h1(b, c), mv_r[:, c, 0:1], rs_r[:, c:c + 1],
                                                           ALU.subtract, ALU.mult)
                        last.then_inc(src_ok.sem, 1)
                    if slot == (2, 0):
                        need(dve, r_full, b, 1)
                        nc.vector.tensor_copy(srcT[:], r_ps[:, 0:SP]).then_inc(r_free.sem, 1)
                    for c in range(NC):
                        if slot == (c + 3, 0):
                            need(dve, r_full, b, c + 2)
                            if c == 0:
                                need(dve, parts_free, b, 0)
                            nc.vector.tensor_tensor(k_st[:, c, :], r_ps[:, 0:D], bkvg[:, 0:D], ALU.add)
                            nc.vector.tensor_tensor(v_st[:, c, 0:D], r_ps[:, D:2 * D], bkvg[:, D:2 * D], ALU.add)
                            nc.vector.tensor_tensor(g_st[:, c, :], r_ps[:, 2 * D:3 * D], bkvg[:, 2 * D:], ALU.add).then_inc(r_free.sem, 1)
                            if c == NC - 1:
                                need(dve, r_free, b, 4)
                                dve.sem_inc(kvg_ok.sem, 1)
                    if slot == (6, 0):
                        need(dve, r_full, b, 5)
                        nc.vector.tensor_scalar(qrT[:, 0:S], r_ps[:, 0:S], bq1[:], None, ALU.add)
                        rlink(nc.vector.tensor_copy(ksum[:], r_ps[:, S + D:S + D + 1]))
                        nc.vector.tensor_tensor(kv_st[:, 0:D], r_ps[:, S:S + D], bd[:], ALU.mult)
                        nc.vector.tensor_scalar(kv_st[:, D:], bd8[:], ksum[:], None, ALU.mult).then_inc(r_free.sem, 1)
                    if slot == (7, 0):
                        need(dve, r_full, b, 6)
                        need(dve, parts_free, b, 0)
                        nc.vector.tensor_copy(o_st[:], r_ps[:, 0:NC * OW]).then_inc(r_free.sem, 1)
                        need(dve, r_free, b, 6)
                        dve.sem_inc(o_ok.sem, 1)

                def step(moe, att, fro, ret):
                    link, flink, mlink, rlink = Chain(dve, a_chain, att), Chain(dve, f_chain, fro), Chain(dve, m_chain, moe), Chain(dve, r_chain, ret)
                    for e in range(E0):
                        for k in range(2):
                            if k == 1 and moe is not None and e:
                                add_expert(moe, e - 1)
                            if moe is not None and (e, k) == (0, 0):
                                logits(moe, mlink)
                            if ret is not None:
                                retain(ret, (e, k), rlink)
                            if moe is not None:
                                if (e, k) == (0, 1):
                                    route(moe, mlink)
                                if (e, k) in ((2, 0), (2, 1)):
                                    biases(moe, k)
                            if att is not None:
                                attend(att, (e, k), link)
                            if fro is not None:
                                front(fro, (e, k), flink)
                    if moe is not None:
                        add_expert(moe, E0 - 1)
                        mlink.end(m_chain.per)
                    if att is not None:
                        link.end(a_chain.per)
                    if fro is not None:
                        flink.end(f_chain.per)
                    if ret is not None:
                        rlink.end(r_chain.per)

                step(None, None, 0, None)
                step(None, 0, 1, None)
                dve.wait_ge(w1hi_ok.sem, 1)
                nc.vector.tensor_tensor(w1_lo[:], w1_in, w1_hi[:].bitcast(FP32), ALU.subtract).then_inc(w1split.sem, 1)
                dve.wait_ge(w1split.sem, 1)
                nc.vector.memset(hid[:, :, :, S:], 0.0).then_inc(w1lo_ok.sem, 1)
                step(0, 1, 2, None)
                with dve.Fori(0, B - 3) as b:
                    step(b + 1, b + 2, b + 3, b)
                step(B - 2, B - 1, None, B - 3)
                step(B - 1, None, None, B - 2)
                step(None, None, None, B - 1)
                dve.wait_ge(y_free.sem, y_free.at(B, 0))
                dve.wait_ge(w_moe.sem, 16 * 4)

        with ExitStack() as l1:
            def sb1(name, shape, dt=FP32):
                return l1.enter_context(nc.sbuf_tensor(name, shape, dt))

            dsum = sb1("dsum", [P, NC, NH])
            wo = sb1("wo", [P, D])
            bo = sb1("bo", [1, D])
            fc1 = sb1("fc1", [P, FF])
            fc1b = sb1("fc1b", [P, FC])
            fc2 = sb1("fc2", [P, FC, D])
            fc2g = sb1("fc2g", [P, FC, D + 1])
            fc2b = sb1("fc2b", [1, D])
            lng = sb1("lng", [P, FC])
            lnb = sb1("lnb", [P, FC])
            c1 = sb1("c1", [P, D])
            c2 = sb1("c2", [P, D])
            n0g = sb1("n0g", [P, D]); n0b = sb1("n0b", [P, D])
            n1g = sb1("n1g", [P, D]); n1b = sb1("n1b", [P, D])
            gw = sb1("gw", [P, E1])
            eb = sb1("eb", [P, E1])
            xT = sb1("xT", [P, SP])
            cst = sb1("cst", [P, NC, 6]); cmv = sb1("cmv", [P, NC, 2]); cve = sb1("cve", [P, NC]); crs = sb1("crs", [P, NC])
            wgu = sb1("wgu", [P, E1 + 1, 2 * F1])
            wgu_hi, wgu_lo = sb1("wgu_hi", [P, E1 + 1, 2 * F1], FP32R), sb1("wgu_lo", [P, E1 + 1, 2 * F1], FP32R)
            x_hi, x_lo = sb1("x_hi", [P, SP], FP32R), sb1("x_lo", [P, SP], FP32R)
            wdn = sb1("wdn", [P, E1 + 1, D])
            lnb_w = sb1("lnb_w", [P, FC, P])
            o_in = sb1("o_in", [P, NC * OW]); g_in = sb1("g_in", [P, SP]); src_in = sb1("src_in", [P, SP])
            qk_sum = sb1("qk_sum", [P, NC, NH]); qk_abs = sb1("qk_abs", [P, NC, NH]); den = sb1("den", [P, NC, NH]); rden = sb1("rden", [P, NC, NH])
            og = sb1("og", [P, NC, NH, HD]); sq = sb1("sq", [P, NC, NH, HD])
            gsum = sb1("gsum", [P, NC, NH]); gmean = sb1("gmean", [P, NC, NH]); gss = sb1("gss", [P, NC, NH])
            gve = sb1("gve", [P, NC, NH]); grs = sb1("grs", [P, NC, NH])
            sg = sb1("sg", [P, SP]); oT = sb1("oT", [P, SP])
            x_pre = sb1("x_pre", [P, NC, D]); x1 = sb1("x1", [P, NC, D]); x1c = sb1("x1c", [P, NC, D]); x1T = sb1("x1T", [P, S])
            ff = sb1("ff", [P, FC, SP]); ffsq = sb1("ffsq", [P, FC, SP])
            fmean = sb1("fmean", [P, NC]); fms = sb1("fms", [P, NC]); fm2 = sb1("fm2", [P, NC]); fvar = sb1("fvar", [P, NC])
            fnm = sb1("fnm", [P, NC])
            x2 = sb1("x2", [P, NC, D]); x3 = sb1("x3", [P, NC, D])
            aff = sb1("aff", [P, NC, E1]); rscore = sb1("rscore", [P, NC, E1])
            top3 = sb1("top3", [P, NC, 8]); idx3 = sb1("idx3", [P, NC, 8], U32); idf3 = sb1("idf3", [P, NC, 3])
            eq3 = sb1("eq3", [P, 3, NC, E1]); sel = sb1("sel", [P, NC, E1])
            asum = sb1("asum", [P, NC]); ainv = sb1("ainv", [P, NC])
            ast = sb1("ast", [P, NC, 6]); amv = sb1("amv", [P, NC, 2]); ave = sb1("ave", [P, NC]); ars = sb1("ars", [P, NC])
            anm = sb1("anm", [P, NC]); cnm = sb1("cnm", [P, NC])
            acc = sb1("acc", [P, NC, D]); zw = sb1("zw", [P, len(BY_ACT) - 1, NC, D])
            gate = sb1("gate", [P, 2, S]); hid1 = sb1("hid1", [P, 3, SP])

            head_full, head_free = signal("head_full", NC), signal("head_free", NC)
            w_small = signal("w_small")
            whi_ok, wlo_ok = signal("whi_ok"), signal("wlo_ok")
            w_moe1, o_here, g_here, src_here = signal("w_moe1"), signal("o_here", 16), signal("g_here", 16), signal("src_here", 16)
            o_used, g_used, src_used = signal("o_used"), signal("g_used"), signal("src_used")
            og_ctr, sq_ok, gve_ok, grs_ok, silu_ok, og_ok = (signal(n) for n in ("og_ctr", "sq_ok", "gve_ok", "grs_ok", "silu_ok", "og_ok"))
            oT_full, oT_ok, wo_full, wo_read = (signal(n) for n in ("oT_full", "oT_ok", "wo_full", "wo_read"))
            avar_ok, arstd_ok, xpre_ok, x1g, x1_ok = (signal(n) for n in ("avar_ok", "arstd_ok", "xpre_ok", "x1g", "x1_ok"))
            x1T_full, x1T_ok, fc1_full = signal("x1T_full"), signal("x1T_ok"), signal("fc1_full", FC)
            ff_ok, ffsq_ok = signal("ff_ok", FC), signal("ffsq_ok")
            fc2_full, fc2_read = signal("fc2_full"), signal("fc2_read")
            cvar_ok, crstd_ok = signal("cvar_ok", 3), signal("crstd_ok", 3)
            x2_ok, hb_ok, x3_ok, xn4_ok = signal("x2_ok"), signal("hb_ok"), signal("x3_ok"), signal("xn4_ok")
            anm_ok, cnm_ok = signal("anm_ok"), signal("cnm_ok")
            hx_ok, x1c_ok = signal("hx_ok"), signal("x1c_ok")
            xT_full, xT_ok, rt_full, rt_read = (signal(n) for n in ("xT_full", "xT_ok", "rt_full", "rt_read"))
            lin_ok, aff_ok, comb1_ok = signal("lin_ok"), signal("aff_ok"), signal("comb1_ok")
            a_link, b_link, h_link, g_link = signal("a_link", 3), signal("b_link", 10), signal("h_link", 12), signal("g_link", 7)
            gu_full, gate_ok = signal("gu_full", E1 + 1), signal("gate_ok", E1 + 1, 2)
            hid1_ok = signal("hid1_ok", E1 + 1, 2)
            z_full, z_free = signal("z_full", E1 + 1, 2), signal("z_free", E1 + 2 - len(BY_ACT))
            z_taken, acc_ok = signal("z_taken", len(BY_ACT)), signal("acc_ok", len(BY_ACT) - 1)
            out_ok = signal("out_ok", 16)
            gu_ps, z_ps = banks[2:6], banks[6:8]
            NE = E1 + 1

            def by_dve(e):
                return e - sum(x < e for x in BY_ACT)

            def need_z_read(eng, b, e):
                if e < 2:
                    need(eng, z_free, b, -1)
                elif e - 2 in BY_ACT:
                    need(eng, z_taken, b, BY_ACT.index(e - 2) + 1)
                else:
                    need(eng, z_free, b, by_dve(e - 1))

            def back(e):
                return max(e - 1, 0)

            block = l1.enter_context(nc.Block())

            @block.sync
            def _(sp):
                def load(b):
                    need(sp, o_used, b, 0)
                    sp.dma_start(o_in[:], row(o_d, b)).then_inc(o_here.sem, 16)
                    need(sp, g_used, b, 0)
                    sp.dma_start(g_in[:], row(g_d, b)).then_inc(g_here.sem, 16)
                    need(sp, src_used, b, 0)
                    sp.dma_start(src_in[:], row(src_d, b)).then_inc(src_here.sem, 16)

                def store(b):
                    need(sp, z_free, b, z_free.per)
                    for c in range(NC):
                        dst = out[bass.ds(b, 1), c * P:c * P + ROWS[c], :].rearrange("a s d -> (a s) d")
                        sp.dma_start(dst, h_all[0:ROWS[c], bass.ds(b * SP + c * P, P)]).then_inc(out_ok.sem, 16)

                for dst, src in ((fc2[:], t["fc2"]), (fc2b[:], t["fc2b"]), (lng[:], t["lng"]), (lnb[:], t["lnb"]), (dsum[:], t["dsum"]),
                                 (wo[:], t["wo"]), (bo[:], t["bo"]), (fc1[:], t["fc1"]), (fc1b[:], t["fc1b"]),
                                 (n0g[:], t["L1_attn_n0_g"].partition_broadcast(P)), (n0b[:], t["L1_attn_n0_b"].partition_broadcast(P)),
                                 (n1g[:], t["L1_attn_n1_g"].partition_broadcast(P)), (n1b[:], t["L1_attn_n1_b"].partition_broadcast(P)),
                                 (gw[:], t["gw"]), (eb[:], t["L1_ffn_expert_bias"].partition_broadcast(P))):
                    sp.dma_start(dst, src).then_inc(w_small.sem, 16)
                load(0)
                sp.dma_start(wgu[:], t["wgu"]).then_inc(w_moe1.sem, 16)
                sp.dma_start(wdn[:], t["wdn"]).then_inc(w_moe1.sem, 16)
                load(1)
                load(2)
                with sp.Fori(0, B - 3) as b:
                    load(b + 3)
                    store(b)
                store(B - 3)
                store(B - 2)
                store(B - 1)
                sp.wait_ge(out_ok.sem, 16 * NC * B)

            @block.gpsimd
            def _(pool):
                def root(x, y, sig_in, sig_out, b, k):
                    need(pool, sig_in, b, k)
                    nc.gpsimd.tensor_tensor(y[:], x[:], neghalf[:, 0:NC], ALU.pow).then_inc(sig_out.sem, 1)

                def gain(b, x, y, g_, b_, sig_in, sig_mid, sig_out):
                    need(pool, sig_in, b, 1)
                    nc.gpsimd.tensor_tensor(y[:], x[:], g_[:].unsqueeze(1).broadcast_to([P, NC, D]), ALU.mult).then_inc(sig_mid.sem, 1)
                    need(pool, sig_mid, b, 1)
                    nc.gpsimd.tensor_tensor(y[:], y[:], b_[:].unsqueeze(1).broadcast_to([P, NC, D]), ALU.add).then_inc(sig_out.sem, 1)

                def step(moe, two, one, zero):
                    if two is not None:
                        hb = h_all[:, bass.ds(two * SP, SP)]
                        h3 = hb.rearrange("p (c d) -> p c d", c=NC)
                        nc.gpsimd.tensor_tensor(h3, h3, n1b[:].unsqueeze(1).broadcast_to([P, NC, D]), ALU.add).then_inc(hb_ok.sem, 1)
                        root(cve, crs, cvar_ok, crstd_ok, two, 1)
                        root(cve, crs, cvar_ok, crstd_ok, two, 2)
                    if one is not None:
                        root(ave, ars, avar_ok, arstd_ok, one, 1)
                    if two is not None:
                        need(pool, hb_ok, two, 1)
                        need(pool, x2_ok, two, 1)
                        nc.gpsimd.tensor_tensor(x3[:], x2[:], n1g[:].unsqueeze(1).broadcast_to([P, NC, D]), ALU.mult).then_inc(x3_ok.sem, 1)
                        need(pool, x3_ok, two, 1, waited)
                        nc.gpsimd.tensor_tensor(hb, hb, x3[:].rearrange("p c d -> p (c d)"), ALU.add).then_inc(hx_ok.sem, 1)
                    if two is not None:
                        root(cve, crs, cvar_ok, crstd_ok, two, 3)
                    if one is not None:
                        gain(one, x_pre, x1, n0g, n0b, xpre_ok, x1g, x1_ok)
                        need(pool, x1_ok, one, 1)
                        nc.gpsimd.tensor_tensor(x1c[:], x1[:], c2[:].unsqueeze(1).broadcast_to([P, NC, D]), ALU.add).then_inc(x1c_ok.sem, 1)
                    if moe is not None:
                        for i in range(1, len(BY_ACT)):
                            need(pool, z_taken, moe, i + 1)
                            if i > 1:
                                need(pool, acc_ok, moe, i - 1)
                            nc.gpsimd.tensor_tensor(acc[:], acc[:], zw[:, i - 1], ALU.add).then_inc(acc_ok.sem, 1)
                    if zero is not None:
                        need(pool, gve_ok, zero, 1)
                        nc.gpsimd.tensor_tensor(grs[:].rearrange("p c h -> p (c h)"), gve[:].rearrange("p c h -> p (c h)"), neghalf[:], ALU.pow)\
                            .then_inc(grs_ok.sem, 1)

                step(None, None, None, 0)
                step(None, None, 0, 1)
                step(None, 0, 1, 2)
                with pool.Fori(0, B - 3) as b:
                    step(b, b + 1, b + 2, b + 3)
                step(B - 3, B - 2, B - 1, None)
                step(B - 2, B - 1, None, None)
                step(B - 1, None, None, None)

            @block.tensor
            def _(pe):
                pe.sem_inc(z_full.sem, z_full.start)
                pe.wait_ge(dec_in.sem, 16)
                for h in range(NH):
                    for ic in range(NC):
                        if h >= 2:
                            need(pe, head_free, h, ic + 1 - 2 * NC)
                        bank = banks[3 * (h % 2) + ic]
                        for jc in range(ic + 1):
                            last = nc.tensor.matmul(bank[0:ROWS[ic], 0:B * HD], decay[0:ROWS[jc], h, DEC[jc] + (ic - jc) * P:DEC[jc] + (ic - jc) * P + ROWS[ic]],
                                                    v_all[0:ROWS[jc], :].rearrange("p (b c d) -> p b c d", b=B, c=NC)[:, :, jc, h * HD:(h + 1) * HD],
                                                    start=(jc == 0), stop=(jc == ic))
                        last.then_inc(head_full.sem, 1)
                pe.wait_ge(head_free.sem, NH * NC)
                pe.wait_ge(setup_v.sem, 1)
                for f in range(FC):
                    nc.tensor.matmul(banks[6][:, 0:D], ones[:], fc2g[:, f, 0:D], start=(f == 0), stop=(f == FC - 1))
                for f in range(FC):
                    nc.tensor.matmul(banks[7][:, 0:D], lnb_w[:, f, :], fc2[:, f, :], start=(f == 0), stop=False)
                nc.tensor.matmul(banks[7][:, 0:D], ones[0:1, :], fc2b[:], start=False, stop=True).then_inc(setup_pe.sem, 1)

                def first_part(b, slot):
                    if slot == 3:
                        need(pe, og_ok, b, 1)
                        need(pe, ff_ok, b, 0)
                        for c in range(NC):
                            last = nc.tensor.transpose(banks[0][:, c * P:(c + 1) * P], og[:, c].rearrange("p h d -> p (h d)"), ident[:])
                        last.then_inc(oT_full.sem, 1)
                    if slot == 5:
                        need(pe, oT_ok, b, 1)
                        for c in range(NC):
                            nc.tensor.matmul(banks[0][:, c * D:(c + 1) * D], oT[:, c * P:(c + 1) * P], wo[:], start=True, stop=False)
                            last = nc.tensor.matmul(banks[0][:, c * D:(c + 1) * D], ones[0:1, :], bo[:], start=False, stop=True)
                        last.then_inc(wo_full.sem, 1)
                    if slot == 13:
                        need(pe, x1_ok, b, 1)
                        need(pe, wo_read, b, 1)
                        for c in range(NC):
                            last = nc.tensor.transpose(banks[0][:, c * P:(c + 1) * P], x1[:, c, :], ident[:])
                        last.then_inc(x1T_full.sem, 1)

                def feed_forward(b, blocks):
                    for f in blocks:
                        if f == 0:
                            need(pe, x1T_ok, b, 1)
                        if f == 1:
                            need(pe, rt_read, b, 0)
                        if f >= 2:
                            need(pe, ff_ok, b, f - 1)
                        nc.tensor.matmul(banks[f % 2][:, 0:S], fc1[:, f * P:(f + 1) * P], x1T[:], start=True, stop=True).then_inc(fc1_full.sem, 1)

                def second_part(b, slot):
                    if slot < NC:
                        if slot == 0:
                            need(pe, ff_ok, b, FC)
                        c, m = slot, banks[1]
                        for f in range(FC):
                            last = nc.tensor.matmul(m[:, c * (D + 2):c * (D + 2) + D + 1], ff[:, f, c * P:(c + 1) * P], fc2g[:, f, :],
                                                    start=(f == 0), stop=(f == FC - 1))
                    if slot == NC - 1:
                        need(pe, ffsq_ok, b, 1)
                        for c in range(NC):
                            at = c * (D + 2) + D + 1
                            for f in range(FC):
                                last = nc.tensor.matmul(m[:, at:at + 1], ffsq[:, f, c * P:(c + 1) * P], ones[:, 0:1],
                                                        start=(f == 0), stop=(f == FC - 1))
                        last.then_inc(fc2_full.sem, 1)
                    if slot == 13:
                        need(pe, xn4_ok, b, 1)
                        need(pe, fc2_read, b, 1)
                        for c in range(NC):
                            last = nc.tensor.transpose(banks[1][:, c * P:(c + 1) * P], xn[:, c * D:(c + 1) * D], ident[:])
                        last.then_inc(xT_full.sem, 1)
                    if slot == 14:
                        need(pe, xT_ok, b, 1)
                        for c in range(NC):
                            last = nc.tensor.matmul(banks[1][:, c * E1:(c + 1) * E1], xT[:, c * P:(c + 1) * P], gw[:], start=True, stop=True)
                        last.then_inc(rt_full.sem, 1)

                def up(b, e):
                    if e == 0:
                        need(pe, lin_ok, b, 1)
                    need(pe, hid1_ok, b, back(e))
                    for k in range(2):
                        for n, (w, x) in enumerate(((wgu_hi, x_hi), (wgu_hi, x_lo), (wgu_lo, x_hi))):
                            last = nc.tensor.matmul(gu_ps[2 * (e % 2) + k][:, 0:S2], w[:, e, k * F1:(k + 1) * F1], x[:, 0:S2],
                                                    start=(n == 0), stop=(n == 2))
                    last.then_inc(gu_full.sem, 1)

                def down(b, e):
                    need(pe, hid1_ok, b, e + 1)
                    need_z_read(pe, b, e)
                    for c in range(NC):
                        last = nc.tensor.matmul(z_ps[e % 2][:, c * D:(c + 1) * D], hid1[:, e % 3, c * P:(c + 1) * P], wdn[:, e, :], start=True, stop=True)
                    last.then_inc(z_full.sem, 1)

                def step(last, moe, two, one):
                    for e in range(NE):
                        if e == 0 and last is not None:
                            down(last, NE - 2)
                        if e == 0 and two is not None:
                            second_part(two, e)
                        if moe is not None:
                            up(moe, e)
                        if e and two is not None:
                            second_part(two, e)
                        if one is not None:
                            first_part(one, e)
                            if e == 14:
                                feed_forward(one, (0,))
                            if e == 15:
                                feed_forward(one, (2, 3))
                        if e == 1 and last is not None:
                            down(last, NE - 1)
                        if moe is not None and e >= 2:
                            down(moe, e - 2)
                        if one is not None and e == 14:
                            feed_forward(one, (1,))

                step(None, None, None, 0)
                step(None, None, 0, 1)
                pe.wait_ge(w_moe1.sem, 32)
                pe.wait_ge(wlo_ok.sem, 1)
                step(None, 0, 1, 2)
                with pe.Fori(0, B - 3) as b:
                    step(b, b + 1, b + 2, b + 3)
                step(B - 3, B - 2, B - 1, None)
                step(B - 2, B - 1, None, None)
                down(B - 1, NE - 2)
                down(B - 1, NE - 1)

            @block.scalar
            def _(act):
                act.sem_inc(gate_ok.sem, gate_ok.start)

                def normalise(b, x, rstd, minus_mean_rstd, sig_in, sig_out):
                    need(act, sig_in, b, 1)
                    for c in range(NC):
                        last = nc.scalar.activation(x[:, c, :], x[:, c, :], ACT.Identity, bias=minus_mean_rstd[:, c:c + 1], scale=rstd[:, c:c + 1])
                    last.then_inc(sig_out.sem, 1)

                def first_part(b, slot):
                    if slot == 10:
                        normalise(b, x_pre, ars, anm, anm_ok, xpre_ok)
                    if slot == 0:
                        need(act, g_here, b, 16)
                        need(act, og_ok, b, 0)
                        nc.scalar.activation(sg[:], g_in[:], ACT.Silu).then_inc(silu_ok.sem, 1)
                    if slot == 3:
                        need(act, oT_full, b, 1)
                        nc.scalar.activation(oT[:], banks[0][:, 0:SP], ACT.Copy).then_inc(oT_ok.sem, 1)
                    if slot == 13:
                        need(act, x1T_full, b, 1)
                        nc.scalar.activation(x1T[:], banks[0][:, 0:S], ACT.Copy).then_inc(x1T_ok.sem, 1)
                    if slot == 14:
                        for f in range(FC):
                            need(act, fc1_full, b, f + 1)
                            nc.scalar.activation(ff[:, f, 0:S], banks[f % 2][:, 0:S], ACT.Gelu, bias=fc1b[:, f:f + 1]).then_inc(ff_ok.sem, 1)

                def second_part(b, slot):
                    if slot == 8:
                        normalise(b, x2, crs, cnm, cnm_ok, x2_ok)
                    if slot == 13:
                        need(act, xT_full, b, 1)
                        need(act, lin_ok, b, 0)
                        nc.scalar.activation(xT[:], banks[1][:, 0:SP], ACT.Copy).then_inc(xT_ok.sem, 1)
                    if slot == 14:
                        need(act, rt_full, b, 1)
                        nc.scalar.activation(aff[:], banks[1][:, 0:NC * E1].rearrange("p (c e) -> p c e", c=NC), ACT.Sigmoid).then_inc(aff_ok.sem, 1)
                        need(act, aff_ok, b, 1)
                        act.sem_inc(rt_read.sem, 1)

                def silu(b, e):
                    need(act, gu_full, b, e + 1)
                    need(act, hid1_ok, b, back(e))
                    nc.scalar.activation(gate[:, e % 2, :], gu_ps[2 * (e % 2)][:, 0:S], ACT.Silu).then_inc(gate_ok.sem, 1)

                def weigh(b, e):
                    i = BY_ACT.index(e)
                    need(act, z_full, b, e + 1)
                    if i == 0:
                        need(act, comb1_ok, b, 1)
                        need(act, z_free, b, 0)
                    dst = acc if i == 0 else zw[:, i - 1]
                    for c in range(NC):
                        last = nc.scalar.activation(dst[:, c, :], z_ps[e % 2][:, c * D:(c + 1) * D], ACT.Identity, scale=combm[:, c, e - 1:e])
                    last.then_inc(z_taken.sem, 1)

                def step(moe, two, one, zero):
                    for e in range(NE):
                        if moe is not None:
                            silu(moe, e)
                        if two is not None:
                            second_part(two, e)
                        if one is not None:
                            first_part(one, e)
                        if moe is not None and e - 2 in BY_ACT:
                            weigh(moe, e - 2)
                        if zero is not None and e == 16:
                            need(act, og_ctr, zero, 1)
                            nc.scalar.activation(sq[:], og[:], ACT.Square).then_inc(sq_ok.sem, 1)
                        if one is not None and e == 16:
                            need(act, ff_ok, one, FC)
                            nc.scalar.activation(ffsq[:, :, 0:S], ff[:, :, 0:S], ACT.Square).then_inc(ffsq_ok.sem, 1)

                step(None, None, None, 0)
                step(None, None, 0, 1)
                act.wait_ge(w_moe1.sem, 32)
                nc.scalar.activation(wgu_hi[:], wgu[:], ACT.Copy).then_inc(whi_ok.sem, 1)
                step(None, 0, 1, 2)
                with act.Fori(0, B - 3) as b:
                    step(b, b + 1, b + 2, b + 3)
                step(B - 3, B - 2, B - 1, None)
                step(B - 2, B - 1, None, None)
                step(B - 1, None, None, None)

            @block.vector
            def _(dve):
                dve.sem_inc(hid1_ok.sem, hid1_ok.start)
                nc.vector.memset(hid1[:, :, S:], 0.0)
                nc.vector.memset(ff[:, :, S:], 0.0)
                nc.vector.memset(ffsq[:, :, S:], 0.0)
                for h in range(NH):
                    for ic in range(NC):
                        need(dve, head_full, h, ic + 1)
                        if ic == 0:
                            need(dve, head_full, h, NC)
                        dst = v_all[0:ROWS[ic], :].rearrange("p (b c d) -> p b c d", b=B, c=NC)[:, :, ic, h * HD:(h + 1) * HD]
                        nc.vector.tensor_copy(dst, banks[3 * (h % 2) + ic][0:ROWS[ic], 0:B * HD].rearrange("p (b d) -> p b d", b=B))\
                            .then_inc(head_free.sem, 1)
                dve.wait_ge(w_small.sem, 16 * 15)
                for f in range(FC):
                    nc.vector.tensor_scalar(fc2g[:, f, 0:D], fc2[:, f, :], lng[:, f:f + 1], None, ALU.mult)
                    nc.vector.tensor_scalar(lnb_w[:, f, :], ones[:], lnb[:, f:f + 1], None, ALU.mult)
                nc.vector.memset(fc2g[:, :, D:], 1.0).then_inc(setup_v.sem, 1)
                dve.wait_ge(setup_pe.sem, 1)
                nc.vector.tensor_copy(c1[:], banks[6][:, 0:D])
                nc.vector.tensor_copy(c2[:], banks[7][:, 0:D]).then_inc(setup_v.sem, 1)
                dve.wait_ge(head_free.sem, NH * NC)
                dve.wait_ge(setup_v.sem, 2)

                def bc(x, n):
                    return x.unsqueeze(2).broadcast_to([P, NC, n])

                def per_head(x):
                    return x[:].rearrange("p c h -> p (c h)").unsqueeze(2).broadcast_to([P, NC * NH, HD])

                def flat(x):
                    return x[:].rearrange("p c h d -> p (c h) d")

                def normalise(x, y, mean, rstd):
                    for c in range(NC):
                        last = nc.vector.tensor_scalar(y[c], x[c], mean[:, c, 0:1], rstd[:, c:c + 1], ALU.subtract, ALU.mult)
                    return last

                def group_norm(b, slot, link):
                    if slot == 12:
                        need(dve, o_here, b, 16)
                        o3 = o_in[:].rearrange("p (c n) -> p c n", c=NC)
                        link(nc.vector.tensor_tensor(qk_sum[:], o3[:, :, D:], dsum[:], ALU.add))
                        link(nc.vector.scalar_tensor_tensor(qk_abs[:], qk_sum[:], -1.0, qk_sum[:], ALU.mult, ALU.max))
                        link(nc.vector.tensor_scalar(den[:], qk_abs[:], 1.0, None, ALU.max))
                        nc.vector.reciprocal(rden[:], den[:])
                        need(dve, oT_full, b, 0)
                        nc.vector.tensor_tensor(og[:].rearrange("p c h d -> p c (h d)"), o3[:, :, 0:D],
                                                v_all[:, bass.ds(b * SP, SP)].rearrange("p (c d) -> p c d", c=NC), ALU.add)\
                            .then_inc(o_used.sem, 1)
                        need(dve, o_used, b, 1)
                        link(nc.vector.tensor_tensor(flat(og), flat(og), per_head(rden), ALU.mult))
                    if slot == 13:
                        link(nc.vector.tensor_reduce(gsum[:].rearrange("p c h -> p (c h)"), flat(og), AX.X, ALU.add))
                        link(nc.vector.tensor_scalar(gmean[:], gsum[:], 1.0 / HD, None, ALU.mult))
                        nc.vector.tensor_tensor(flat(og), flat(og), per_head(gmean), ALU.subtract).then_inc(og_ctr.sem, 1)
                    if slot == 16:
                        need(dve, sq_ok, b, 1)
                        link(nc.vector.tensor_reduce(gss[:].rearrange("p c h -> p (c h)"), flat(sq), AX.X, ALU.add))
                        nc.vector.tensor_scalar(gve[:], gss[:], 1.0 / HD, 1e-6, ALU.mult, ALU.add).then_inc(gve_ok.sem, 1)

                def first_part(b, slot, link):
                    xs = [x_pre[:, c, :] for c in range(NC)]
                    og_flat = og[:].rearrange("p c h d -> p (c h d)")
                    if slot == 1:
                        need(dve, grs_ok, b, 1)
                        link(nc.vector.tensor_tensor(flat(og), flat(og), per_head(grs), ALU.mult))
                        need(dve, silu_ok, b, 1)
                        nc.vector.tensor_tensor(og_flat, og_flat, sg[:], ALU.mult).then_inc(og_ok.sem, 1)
                        need(dve, og_ok, b, 1)
                        dve.sem_inc(g_used.sem, 1)
                    if slot == 6:
                        need(dve, wo_full, b, 1)
                        need(dve, src_here, b, 16)
                        nc.vector.tensor_tensor(x_pre[:].rearrange("p c d -> p (c d)"), banks[0][:, 0:SP], src_in[:], ALU.add).then_inc(wo_read.sem, 1)
                        need(dve, wo_read, b, 1, waited)
                        dve.sem_inc(src_used.sem, 1)
                    if slot == 8:
                        token_stats(xs, ast, amv, link)
                        nc.vector.tensor_scalar(ave[:], amv[:, :, 1], EPS, None, ALU.add).then_inc(avar_ok.sem, 1)
                    if slot == 9:
                        need(dve, arstd_ok, b, 1)
                        nc.vector.scalar_tensor_tensor(anm[:], amv[:, :, 0], -1.0, ars[:], ALU.mult, ALU.mult).then_inc(anm_ok.sem, 1)

                def second_part(b, slot, link):
                    m3 = banks[1][:, 0:NC * (D + 2)].rearrange("p (c n) -> p c n", c=NC)
                    xs = [x2[:, c, :] for c in range(NC)]
                    hs = [h1(b, c) for c in range(NC)]
                    if slot == 3:
                        need(dve, fc2_full, b, 1)
                        nc.vector.tensor_scalar(fmean[:], m3[:, :, D], 1.0 / FF, None, ALU.mult)
                        link(nc.vector.tensor_scalar(fms[:], m3[:, :, D + 1], 1.0 / FF, None, ALU.mult))
                        link(nc.vector.tensor_tensor(fm2[:], fmean[:], fmean[:], ALU.mult))
                        link(nc.vector.tensor_tensor(fvar[:], fms[:], fm2[:], ALU.subtract))
                        nc.vector.tensor_scalar(cve[:], fvar[:], 0.0, 1e-6, ALU.max, ALU.add).then_inc(cvar_ok.sem, 1)
                    if slot == 4:
                        need(dve, crstd_ok, b, 1)
                        link(nc.vector.scalar_tensor_tensor(fnm[:], fmean[:], -1.0, crs[:], ALU.mult, ALU.mult))
                        need(dve, x1c_ok, b, 1)
                        for c in range(NC):
                            last = nc.vector.scalar_tensor_tensor(x2[:, c, :], c1[:], fnm[:, c:c + 1], x1c[:, c, :], ALU.mult, ALU.add)
                        link(last)
                    if slot == 5:
                        for c in range(NC):
                            last = nc.vector.scalar_tensor_tensor(x2[:, c, :], m3[:, c, 0:D], crs[:, c:c + 1], x2[:, c, :], ALU.mult, ALU.add)
                        last.then_inc(fc2_read.sem, 1)
                    if slot == 6:
                        need(dve, fc2_read, b, 1, waited)
                        token_stats(xs, cst, cmv, link)
                        nc.vector.tensor_scalar(cve[:], cmv[:, :, 1], EPS, None, ALU.add).then_inc(cvar_ok.sem, 1)
                    if slot == 7:
                        need(dve, crstd_ok, b, 2)
                        nc.vector.scalar_tensor_tensor(cnm[:], cmv[:, :, 0], -1.0, crs[:], ALU.mult, ALU.mult).then_inc(cnm_ok.sem, 1)
                    if slot == 10:
                        need(dve, hx_ok, b, 1, waited)
                        token_stats(hs, cst, cmv, link)
                        nc.vector.tensor_scalar(cve[:], cmv[:, :, 1], EPS, None, ALU.add).then_inc(cvar_ok.sem, 1)
                    if slot == 11:
                        need(dve, crstd_ok, b, 3)
                        normalise(hs, [xn[:, c * D:(c + 1) * D] for c in range(NC)], cmv, crs).then_inc(xn4_ok.sem, 1)
                def weights(b, slot, link):
                    if slot == 0:
                        need(dve, aff_ok, b, 1)
                        link(nc.vector.tensor_tensor(rscore[:], aff[:], eb[:].unsqueeze(1).broadcast_to([P, NC, E1]), ALU.add))
                        dve.sem_inc(waited.sem, 1)
                        for c in range(NC):
                            last = nc.vector.max(top3[:, c, :], rscore[:, c, :])
                        link(last)
                    if slot == 1:
                        dve.sem_inc(waited.sem, 1)
                        for c in range(NC):
                            last = nc.vector.max_index(idx3[:, c, :], top3[:, c, :], rscore[:, c, :])
                        link(last)
                        link(nc.vector.tensor_copy(idf3[:], idx3[:, :, 0:3]))
                        io = iota[:].unsqueeze(1).broadcast_to([P, NC, E1])
                        for k in range(3):
                            last = nc.vector.tensor_tensor(eq3[:, k], io, bc(idf3[:, :, k], E1), ALU.is_equal)
                        link(last)
                    if slot == 2:
                        link(nc.vector.tensor_tensor(sel[:], eq3[:, 0], eq3[:, 1], ALU.add))
                        link(nc.vector.tensor_tensor(sel[:], sel[:], eq3[:, 2], ALU.add))
                        link(nc.vector.tensor_tensor(sel[:], sel[:], aff[:], ALU.mult))
                        link(nc.vector.tensor_reduce(asum[:], sel[:], AX.X, ALU.add))
                        link(nc.vector.tensor_scalar(asum[:], asum[:], 1e-9, None, ALU.add))
                        link(nc.vector.reciprocal(ainv[:], asum[:]))
                        link(nc.vector.tensor_tensor(combm[:], sel[:], bc(ainv[:], E1), ALU.mult))
                        dve.sem_inc(comb1_ok.sem, 1)

                def hidden(b, e):
                    need(dve, gate_ok, b, e + 1)
                    need(dve, z_full, b, e - 2 if e > 2 else min(e - 1, 0))
                    nc.vector.tensor_tensor(hid1[:, e % 3, 0:S], gate[:, e % 2, :], gu_ps[2 * (e % 2) + 1][:, 0:S], ALU.mult)\
                        .then_inc(hid1_ok.sem, 1)

                def add_expert(b, e):
                    if e in BY_ACT:
                        return
                    need(dve, z_full, b, e + 1)
                    if e == 0:
                        hb = h_all[:, bass.ds(b * SP, SP)]
                        nc.vector.tensor_tensor(hb, hb, z_ps[0][:, 0:SP], ALU.add).then_inc(z_free.sem, 1)
                        return
                    need(dve, z_free, b, by_dve(e))
                    for c in range(NC):
                        last = nc.vector.scalar_tensor_tensor(h1(b, c), z_ps[e % 2][:, c * D:(c + 1) * D], combm[:, c, e - 1:e], h1(b, c),
                                                              ALU.mult, ALU.add)
                    last.then_inc(z_free.sem, 1)

                def add_sum(b):
                    need(dve, z_free, b, by_dve(NE))
                    need(dve, acc_ok, b, acc_ok.per)
                    hb = h_all[:, bass.ds(b * SP, SP)]
                    nc.vector.tensor_tensor(hb, hb, acc[:].rearrange("p c d -> p (c d)"), ALU.add).then_inc(z_free.sem, 1)

                def step(last, moe, two, one, zero):
                    alink, blink, hlink, glink = (Chain(dve, a_link, one), Chain(dve, b_link, two), Chain(dve, h_link, moe),
                                                  Chain(dve, g_link, zero))
                    for e in range(NE):
                        if moe is not None:
                            hidden(moe, e)
                            if e == NE - 1 and two is not None:
                                need(dve, gu_full, moe, NE)
                        if e == NE - 1 and two is not None:
                            need(dve, xT_ok, two, 1)
                            blink(nc.vector.tensor_copy(x_hi[:], xT[:]))
                            nc.vector.tensor_tensor(x_lo[:], xT[:], x_hi[:].bitcast(FP32), ALU.subtract).then_inc(lin_ok.sem, 1)
                        if last is not None and e < 2:
                            add_expert(last, NE - 2 + e)
                        if last is not None and e == 2:
                            add_sum(last)
                        if moe is not None:
                            if e >= 2:
                                add_expert(moe, e - 2)
                            weights(moe, e, hlink)
                        if two is not None:
                            second_part(two, e, blink)
                        if one is not None:
                            first_part(one, e, alink)
                        if zero is not None:
                            group_norm(zero, e, glink)
                    if moe is not None:
                        hlink.end(h_link.per)
                    if two is not None:
                        blink.end(b_link.per)
                    if one is not None:
                        alink.end(a_link.per)
                    if zero is not None:
                        glink.end(g_link.per)

                step(None, None, None, None, 0)
                step(None, None, None, 0, 1)
                step(None, None, 0, 1, 2)
                dve.wait_ge(whi_ok.sem, 1)
                nc.vector.tensor_tensor(wgu_lo[:], wgu[:], wgu_hi[:].bitcast(FP32), ALU.subtract).then_inc(wlo_ok.sem, 1)
                step(None, 0, 1, 2, 3)
                with dve.Fori(0, B - 4) as b:
                    step(b, b + 1, b + 2, b + 3, b + 4)
                step(B - 4, B - 3, B - 2, B - 1, None)
                step(B - 3, B - 2, B - 1, None, None)
                step(B - 2, B - 1, None, None, None)
                add_expert(B - 1, NE - 2)
                add_expert(B - 1, NE - 1)
                add_sum(B - 1)


def decay_matrices():
    i = np.arange(S)
    diff = (i[:, None] - i[None, :]).astype(np.float64)
    dec = np.log(1.0 - 2.0 ** (-5.0 - np.arange(NH)))
    dm = np.where(diff[None] >= 0, np.exp(np.maximum(diff[None], 0) * dec[:, None, None]), 0.0)
    dm = (dm / np.sqrt(dm.sum(-1, keepdims=True))).astype(np.float32)
    dT = []
    sums = np.zeros((P, NC, NH), np.float32)
    for c in range(NC):
        part = np.zeros((P, NH, S - c * P), np.float32)
        part[:ROWS[c]] = dm[:, c * P:, c * P:c * P + ROWS[c]].transpose(2, 0, 1)
        dT.append(part)
        sums[:ROWS[c], c, :] = dm.sum(-1)[:, c * P:c * P + ROWS[c]].T
    return np.concatenate(dT, 2), sums


def kernel(**inputs):
    import concourse.bacc as _bacc
    from concourse.bass_utils import run_bass_kernel_spmd as _run

    x = {k: np.asarray(v) for k, v in inputs.items()}
    a = {}
    for k in ("txt", "L0_tok_b", "L0_tok_token", "L0_tok_pos", "L0_attn_b2", "L0_ffn_router_w", "L0_ffn_router_b", "L0_ffn_b2",
              "L1_attn_bk", "L1_attn_bv", "L1_attn_bg", "L1_attn_n0_g", "L1_attn_n0_b", "L1_attn_n1_g", "L1_attn_n1_b", "L1_ffn_expert_bias"):
        a[k] = x[k]
    px = x["x"].reshape(B, 3, N_PATCH, 14, N_PATCH, 14).transpose(0, 1, 3, 5, 2, 4).reshape(B, 588, S_IMG - 1)
    px = np.pad(px, ((0, 0), (0, KT * KR - 588), (1, 0)))
    a["patches"] = px.reshape(B, KT, KR, S_IMG).transpose(0, 2, 1, 3)
    a["tokw"] = np.pad(x["L0_tok_W"].T, ((0, KT * KR - 588), (0, 0))).reshape(KT, KR, D).transpose(1, 0, 2)
    a["wqkv0"] = np.stack([x["L0_attn_Wq"].T, x["L0_attn_Wk"].T, x["L0_attn_Wv"].T], 1)
    w1q = np.zeros((D, QG, P), np.float32)
    w2a = np.zeros((P, 24 + QG + 24), np.float32)
    for r in range(QG):
        w1q[:, r, r * AH:(r + 1) * AH] = x["L0_attn_W1"][:, :D].T
        w2a[r * AH:(r + 1) * AH, 24 + r] = x["L0_attn_W2"][0]
    a["w1q"], a["w2a"] = w1q, w2a
    a["w1k"] = np.tile(x["L0_attn_W1"][:, D:].T, (1, QG))
    a["b1a"] = np.tile(x["L0_attn_b1"].reshape(AH, 1), (QG, 1))
    a["w1e"] = x["L0_ffn_W1"].transpose(1, 0, 2)
    a["b1e"] = x["L0_ffn_b1"].reshape(E0 * FC, P).T
    a["w2e"] = x["L0_ffn_W2"].reshape(E0, FC, P, D).transpose(2, 0, 1, 3)
    a["wkvg"] = np.concatenate([x["L1_attn_wk"].T, x["L1_attn_wv"].T, x["L1_attn_wg"].T], 1)
    a["wq1"] = x["L1_attn_wq"].T
    a["bq1"] = x["L1_attn_bq"].reshape(D, 1)
    same = np.arange(D)[:, None] // HD == np.arange(D)[None, :] // HD
    a["bd"] = np.where(same, np.float32(HD ** -0.5), np.float32(0))
    a["bd8"] = a["bd"][:, ::HD]
    a["decay"], a["dsum"] = decay_matrices()
    a["wo"] = x["L1_attn_wo"].T
    a["bo"] = x["L1_attn_bo"].reshape(1, D)
    a["fc1"] = x["L1_attn_fc1_w"].T
    a["fc1b"] = x["L1_attn_fc1_b"].reshape(FC, P).T
    a["fc2"] = x["L1_attn_fc2_w"].T.reshape(FC, P, D).transpose(1, 0, 2)
    a["fc2b"] = x["L1_attn_fc2_b"].reshape(1, D)
    a["lng"] = x["L1_attn_ln_ffn_g"].reshape(FC, P).T
    a["lnb"] = x["L1_attn_ln_ffn_b"].reshape(FC, P).T
    a["gw"] = x["L1_ffn_gate_w"].T
    a["wgu"] = np.concatenate([x["L1_ffn_shared_gate_up"][None], x["L1_ffn_expert_gate_up"]]).transpose(2, 0, 1)
    a["wdn"] = np.concatenate([x["L1_ffn_shared_down"][None], x["L1_ffn_expert_down"]]).transpose(2, 0, 1)

    nc = _bacc.Bacc("TRN2", target_bir_lowering=False, num_devices=1)
    arrays, t = {}, {}
    for k, v in a.items():
        v = np.ascontiguousarray(v)
        arrays[f"in_{k}"] = v
        t[k] = nc.dram_tensor(f"in_{k}", v.shape, FP32, kind="ExternalInput").ap()
    out = nc.dram_tensor("out_0", (B, S, D), FP32, kind="ExternalOutput").ap()
    program(nc, t, out)
    r = _run(nc, [arrays], core_ids=[0])
    return r.results[0]["out_0"]
```
